# Optimizing a Trainium2 kernel written in Bass

```python
import numpy as np
import jax
import jax.numpy as jnp

def _softmax(x, axis=-1):
    return jax.nn.softmax(x, axis=axis)

def _gelu(x):
    return jax.nn.gelu(x, approximate=True)

def _silu(x):
    return jax.nn.silu(x)

def _sigmoid(x):
    return jax.nn.sigmoid(x)

def _layernorm(x, axis=-1, eps=1e-05):
    m = jnp.mean(x, axis=axis, keepdims=True)
    v = jnp.var(x, axis=axis, keepdims=True)
    return (x - m) / jnp.sqrt(v + eps)

def _scatter_add(tgt, idx, src, axis=0):
    return tgt.at[idx].add(src)

def _segment_sum(src, seg, n):
    return jax.ops.segment_sum(src, seg, n)
kernel_name = 'mk_adaln_d2_jaxref_r8_bf2a01'

def setup_inputs(seed: int=0):
    np.random.seed(seed)
    _w = jnp.asarray

    def _L0_attn_setup():
        import jax, jax.numpy as jnp
        import numpy as np
        DIM = 128
        DT_RANK = 64
        D_STATE = 16
        B, L = (4, 64)

        def _layer_norm(x, gamma, beta, eps=1e-06):
            mu = jnp.mean(x, axis=-1, keepdims=True)
            var = jnp.mean(jnp.square(x - mu), axis=-1, keepdims=True)
            return (x - mu) * jax.lax.rsqrt(var + eps) * gamma + beta

        def _ssm(u, W_x, b_x, W_dt, b_dt, A_log, Dp):
            r = W_dt.shape[0]
            n = A_log.shape[1]
            A = -jnp.exp(A_log)
            dbc = u @ W_x + b_x
            delta = jax.nn.softplus(dbc[..., :r] @ W_dt + b_dt)
            Bmat = dbc[..., r:r + n]
            Cmat = dbc[..., r + n:]
            dA = jnp.exp(jnp.einsum('bld,dn->bldn', delta, A))
            dBu = jnp.einsum('bld,bln,bld->bldn', delta, Bmat, u)

            def step(h, xs):
                dA_t, dBu_t, C_t = xs
                h = dA_t * h + dBu_t
                y = jnp.einsum('bdn,bn->bd', h, C_t)
                return (h, y)
            h0 = jnp.zeros((u.shape[0], u.shape[2], n), u.dtype)
            _, ys = jax.lax.scan(step, h0, (jnp.swapaxes(dA, 0, 1), jnp.swapaxes(dBu, 0, 1), jnp.swapaxes(Cmat, 0, 1)))
            y = jnp.swapaxes(ys, 0, 1)
            return y + u * Dp
        key = jax.random.key(seed)
        ks = jax.random.split(key, 16)
        s = 0.02
        d, r, n = (DIM, DT_RANK, D_STATE)
        inp = {'inputs': jax.random.normal(ks[0], (B, L, d), jnp.float32), 'gamma': jnp.ones((d,), jnp.float32), 'beta': jnp.zeros((d,), jnp.float32), 'W_proj': jax.random.normal(ks[1], (d, d), jnp.float32) * s, 'b_proj': jnp.zeros((d,), jnp.float32), 'W_fc': jax.random.normal(ks[2], (d, d), jnp.float32) * s, 'b_fc': jnp.zeros((d,), jnp.float32), 'W_bc': jax.random.normal(ks[3], (d, d), jnp.float32) * s, 'b_bc': jnp.zeros((d,), jnp.float32), 'W_x1': jax.random.normal(ks[4], (d, r + 2 * n), jnp.float32) * s, 'b_x1': jnp.zeros((r + 2 * n,), jnp.float32), 'W_dt1': jax.random.normal(ks[5], (r, d), jnp.float32) * s, 'b_dt1': jnp.full((d,), -4.0, jnp.float32), 'A_log1': jnp.log(jnp.broadcast_to(jnp.arange(1, n + 1, dtype=jnp.float32), (d, n))), 'D1': jnp.ones((d,), jnp.float32), 'W_x2': jax.random.normal(ks[6], (d, r + 2 * n), jnp.float32) * s, 'b_x2': jnp.zeros((r + 2 * n,), jnp.float32), 'W_dt2': jax.random.normal(ks[7], (r, d), jnp.float32) * s, 'b_dt2': jnp.full((d,), -4.0, jnp.float32), 'A_log2': jnp.log(jnp.broadcast_to(jnp.arange(1, n + 1, dtype=jnp.float32), (d, n))), 'D2': jnp.ones((d,), jnp.float32)}
        return inp
    _L0_attn_in = _L0_attn_setup()

    def _L0_ffn_setup():
        import jax, jax.numpy as jnp
        import numpy as np
        B, N, D, E, MULT = (4, 256, 128, 8, 4)
        F = D * MULT

        def _top2_gate(xn, Wg):
            logits = jnp.einsum('bnd,ed->bne', xn, Wg)
            probs = jax.nn.softmax(logits, axis=-1)
            top1 = jnp.argmax(probs, axis=-1)
            t1v = jnp.take_along_axis(probs, top1[..., None], axis=-1)[..., 0]
            masked = jnp.where(jax.nn.one_hot(top1, probs.shape[-1], dtype=bool), -jnp.inf, probs)
            top2 = jnp.argmax(masked, axis=-1)
            t2v = jnp.take_along_axis(masked, top2[..., None], axis=-1)[..., 0]
            denom = t1v + t2v + 1e-09
            combine = jnp.stack([t1v / denom, t2v / denom], axis=-1)
            idx = jnp.stack([top1, top2], axis=-1)
            return (combine, idx)
        key = jax.random.key(seed)
        ks = jax.random.split(key, 8)
        s_in = 1.0 / np.sqrt(D)
        s_hid = 1.0 / np.sqrt(F)
        return {'x': jax.random.normal(ks[0], (B, N, D), dtype=jnp.float32), 'gamma': jnp.ones((D,), dtype=jnp.float32), 'beta': jnp.zeros((D,), dtype=jnp.float32), 'Wg': jax.random.normal(ks[1], (E, D), dtype=jnp.float32) * s_in, 'W1': jax.random.normal(ks[2], (E, D, F), dtype=jnp.float32) * s_in, 'b1': jax.random.normal(ks[3], (E, F), dtype=jnp.float32) * 0.01, 'W2': jax.random.normal(ks[4], (E, F, D), dtype=jnp.float32) * s_hid, 'b2': jax.random.normal(ks[5], (E, D), dtype=jnp.float32) * 0.01}
    _L0_ffn_in = _L0_ffn_setup()
    _L0_c = _w((lambda *s: np.random.randn(*s).astype(np.float32) * 0.05)(32, 128))
    _L0_wmod = _w((lambda *s: np.random.randn(*s).astype(np.float32) * 0.05)(128, 6 * 128) * 128 ** (-0.5))

    def _L1_attn_setup():
        import jax, jax.numpy as jnp
        import numpy as np
        HEADS = 16
        LOCAL_HEADS = 4
        DIM = 128
        DH = DIM // HEADS
        WINDOW = 128
        BLINDSPOT = 64

        def _look_around(x, buckets):
            pad_cfg = ((0, 0), (1, 0)) + ((0, 0),) * (x.ndim - 2)
            pv = -1.0 if jnp.issubdtype(x.dtype, jnp.floating) else -1
            p = jnp.pad(x, pad_cfg, constant_values=pv)
            return jnp.concatenate([p[:, :buckets], p[:, 1:buckets + 1]], axis=2)

        def _local_attn(q, k, v):
            b, lh, t, e = q.shape
            bm = b * lh
            buckets = t // WINDOW
            bq = q.reshape(bm, buckets, WINDOW, e)
            bk = k.reshape(bm, buckets, WINDOW, e)
            bv = v.reshape(bm, buckets, WINDOW, e)
            bk2 = _look_around(bk, buckets)
            bv2 = _look_around(bv, buckets)
            ticker = jnp.arange(t, dtype=jnp.int32).reshape(1, buckets, WINDOW)
            bq_k = _look_around(ticker, buckets)
            dots = jnp.einsum('buie,buje->buij', bq, bk2) * e ** (-0.5)
            mask_value = -jnp.finfo(dots.dtype).max
            causal_mask = ticker[:, :, :, None] < bq_k[:, :, None, :]
            pad_mask = bq_k[:, :, None, :] == -1
            dots = jnp.where(causal_mask | pad_mask, mask_value, dots)
            attn = jax.nn.softmax(dots, axis=-1)
            out = jnp.einsum('buij,buje->buie', attn, bv2)
            return out.reshape(b, lh, t, e)

        def _causal_linear_attn(q, k, v):
            b, h, n, e = q.shape
            u = n // BLINDSPOT
            q = jax.nn.softmax(q, axis=-1)
            k = jax.nn.elu(k) + 1.0
            bq = q.reshape(b, h, u, BLINDSPOT, e)
            bk = k.reshape(b, h, u, BLINDSPOT, e)
            bv = v.reshape(b, h, u, BLINDSPOT, e)
            bk_cumsum = jnp.cumsum(bk.sum(axis=-2), axis=-2)
            ctx = jnp.einsum('bhund,bhune->bhude', bk, bv)
            ctx = jnp.cumsum(ctx, axis=2)
            ctx = ctx / (bk_cumsum[..., None] + 1e-06)
            ctx = jnp.pad(ctx, ((0, 0), (0, 0), (1, 0), (0, 0), (0, 0)))[:, :, :u]
            attn = jnp.einsum('bhund,bhude->bhune', bq, ctx)
            return attn.reshape(b, h, n, e)
        key = jax.random.key(seed)
        ks = jax.random.split(key, 6)
        s = 1.0 / np.sqrt(DIM)
        x = jax.random.normal(ks[0], (4, 1024, DIM), dtype=jnp.float32)
        Wq = jax.random.normal(ks[1], (DIM, DIM), dtype=jnp.float32) * s
        Wk = jax.random.normal(ks[2], (DIM, DIM), dtype=jnp.float32) * s
        Wv = jax.random.normal(ks[3], (DIM, DIM), dtype=jnp.float32) * s
        Wo = jax.random.normal(ks[4], (DIM, DIM), dtype=jnp.float32) * s
        bo = jax.random.normal(ks[5], (DIM,), dtype=jnp.float32) * 0.01
        return {'x': x, 'Wq': Wq, 'Wk': Wk, 'Wv': Wv, 'Wo': Wo, 'bo': bo}
    _L1_attn_in = _L1_attn_setup()

    def _L1_ffn_setup():
        import jax, jax.numpy as jnp
        import numpy as np
        B, S, D = (8, 256, 128)
        E, K = (8, 2)
        H = 4 * D
        key = jax.random.key(seed)
        ks = jax.random.split(key, 7)
        s_d = 1.0 / np.sqrt(D)
        s_h = 1.0 / np.sqrt(H)
        return {'x': jax.random.normal(ks[0], (B, S, D), dtype=jnp.float32), 'gate_w': jax.random.uniform(ks[1], (D, E), jnp.float32, -s_d, s_d), 'gate_b': jax.random.uniform(ks[2], (E,), jnp.float32, -s_d, s_d), 'w1': jax.random.uniform(ks[3], (E, D, H), jnp.float32, -s_d, s_d), 'b1': jax.random.uniform(ks[4], (E, H), jnp.float32, -s_d, s_d), 'w2': jax.random.uniform(ks[5], (E, H, D), jnp.float32, -s_h, s_h), 'b2': jax.random.uniform(ks[6], (E, D), jnp.float32, -s_h, s_h)}
    _L1_ffn_in = _L1_ffn_setup()
    _L1_c = _w((lambda *s: np.random.randn(*s).astype(np.float32) * 0.05)(32, 128))
    _L1_wmod = _w((lambda *s: np.random.randn(*s).astype(np.float32) * 0.05)(128, 6 * 128) * 128 ** (-0.5))
    _d = {'L0_attn_inputs': _L0_attn_in['inputs'], 'L0_attn_gamma': _L0_attn_in['gamma'], 'L0_attn_beta': _L0_attn_in['beta'], 'L0_attn_W_proj': _L0_attn_in['W_proj'], 'L0_attn_b_proj': _L0_attn_in['b_proj'], 'L0_attn_W_fc': _L0_attn_in['W_fc'], 'L0_attn_b_fc': _L0_attn_in['b_fc'], 'L0_attn_W_bc': _L0_attn_in['W_bc'], 'L0_attn_b_bc': _L0_attn_in['b_bc'], 'L0_attn_W_x1': _L0_attn_in['W_x1'], 'L0_attn_b_x1': _L0_attn_in['b_x1'], 'L0_attn_W_dt1': _L0_attn_in['W_dt1'], 'L0_attn_b_dt1': _L0_attn_in['b_dt1'], 'L0_attn_A_log1': _L0_attn_in['A_log1'], 'L0_attn_D1': _L0_attn_in['D1'], 'L0_attn_W_x2': _L0_attn_in['W_x2'], 'L0_attn_b_x2': _L0_attn_in['b_x2'], 'L0_attn_W_dt2': _L0_attn_in['W_dt2'], 'L0_attn_b_dt2': _L0_attn_in['b_dt2'], 'L0_attn_A_log2': _L0_attn_in['A_log2'], 'L0_attn_D2': _L0_attn_in['D2'], 'L0_ffn_gamma': _L0_ffn_in['gamma'], 'L0_ffn_beta': _L0_ffn_in['beta'], 'L0_ffn_Wg': _L0_ffn_in['Wg'], 'L0_ffn_W1': _L0_ffn_in['W1'], 'L0_ffn_b1': _L0_ffn_in['b1'], 'L0_ffn_W2': _L0_ffn_in['W2'], 'L0_ffn_b2': _L0_ffn_in['b2'], 'L0_c': _L0_c, 'L0_wmod': _L0_wmod, 'L1_attn_Wq': _L1_attn_in['Wq'], 'L1_attn_Wk': _L1_attn_in['Wk'], 'L1_attn_Wv': _L1_attn_in['Wv'], 'L1_attn_Wo': _L1_attn_in['Wo'], 'L1_attn_bo': _L1_attn_in['bo'], 'L1_ffn_gate_w': _L1_ffn_in['gate_w'], 'L1_ffn_gate_b': _L1_ffn_in['gate_b'], 'L1_ffn_w1': _L1_ffn_in['w1'], 'L1_ffn_b1': _L1_ffn_in['b1'], 'L1_ffn_w2': _L1_ffn_in['w2'], 'L1_ffn_b2': _L1_ffn_in['b2'], 'L1_c': _L1_c, 'L1_wmod': _L1_wmod}
    _x0 = _d['L0_attn_inputs']
    _d['L0_attn_inputs'] = jax.random.normal(jax.random.fold_in(jax.random.key(seed), 1), (32, 256, 128), dtype=_x0.dtype)
    del _x0
    return _d

def reference(L0_attn_inputs, L0_attn_gamma, L0_attn_beta, L0_attn_W_proj, L0_attn_b_proj, L0_attn_W_fc, L0_attn_b_fc, L0_attn_W_bc, L0_attn_b_bc, L0_attn_W_x1, L0_attn_b_x1, L0_attn_W_dt1, L0_attn_b_dt1, L0_attn_A_log1, L0_attn_D1, L0_attn_W_x2, L0_attn_b_x2, L0_attn_W_dt2, L0_attn_b_dt2, L0_attn_A_log2, L0_attn_D2, L0_ffn_gamma, L0_ffn_beta, L0_ffn_Wg, L0_ffn_W1, L0_ffn_b1, L0_ffn_W2, L0_ffn_b2, L0_c, L0_wmod, L1_attn_Wq, L1_attn_Wk, L1_attn_Wv, L1_attn_Wo, L1_attn_bo, L1_ffn_gate_w, L1_ffn_gate_b, L1_ffn_w1, L1_ffn_b1, L1_ffn_w2, L1_ffn_b2, L1_c, L1_wmod):

    def _L0_attn_ref(inputs, gamma, beta, W_proj, b_proj, W_fc, b_fc, W_bc, b_bc, W_x1, b_x1, W_dt1, b_dt1, A_log1, D1, W_x2, b_x2, W_dt2, b_dt2, A_log2, D2):
        import jax, jax.numpy as jnp
        import numpy as np
        DIM = 128
        DT_RANK = 64
        D_STATE = 16
        B, L = (4, 64)

        def _layer_norm(x, gamma, beta, eps=1e-06):
            mu = jnp.mean(x, axis=-1, keepdims=True)
            var = jnp.mean(jnp.square(x - mu), axis=-1, keepdims=True)
            return (x - mu) * jax.lax.rsqrt(var + eps) * gamma + beta

        def _ssm(u, W_x, b_x, W_dt, b_dt, A_log, Dp):
            r = W_dt.shape[0]
            n = A_log.shape[1]
            A = -jnp.exp(A_log)
            dbc = u @ W_x + b_x
            delta = jax.nn.softplus(dbc[..., :r] @ W_dt + b_dt)
            Bmat = dbc[..., r:r + n]
            Cmat = dbc[..., r + n:]
            dA = jnp.exp(jnp.einsum('bld,dn->bldn', delta, A))
            dBu = jnp.einsum('bld,bln,bld->bldn', delta, Bmat, u)

            def step(h, xs):
                dA_t, dBu_t, C_t = xs
                h = dA_t * h + dBu_t
                y = jnp.einsum('bdn,bn->bd', h, C_t)
                return (h, y)
            h0 = jnp.zeros((u.shape[0], u.shape[2], n), u.dtype)
            _, ys = jax.lax.scan(step, h0, (jnp.swapaxes(dA, 0, 1), jnp.swapaxes(dBu, 0, 1), jnp.swapaxes(Cmat, 0, 1)))
            y = jnp.swapaxes(ys, 0, 1)
            return y + u * Dp
        skip = inputs
        x = _layer_norm(inputs, gamma, beta)
        proj = x @ W_proj + b_proj
        z = jax.nn.silu(proj)
        u1 = jax.nn.softplus(proj @ W_fc + b_fc)
        y1 = _ssm(u1, W_x1, b_x1, W_dt1, b_dt1, A_log1, D1)
        u2 = jax.nn.softplus(proj @ W_bc + b_bc)
        y2 = _ssm(u2, W_x2, b_x2, W_dt2, b_dt2, A_log2, D2)
        return y1 * z + y2 * z + skip

    def _L0_ffn_ref(x, gamma, beta, Wg, W1, b1, W2, b2):
        import jax, jax.numpy as jnp
        import numpy as np
        B, N, D, E, MULT = (4, 256, 128, 8, 4)
        F = D * MULT

        def _top2_gate(xn, Wg):
            logits = jnp.einsum('bnd,ed->bne', xn, Wg)
            probs = jax.nn.softmax(logits, axis=-1)
            top1 = jnp.argmax(probs, axis=-1)
            t1v = jnp.take_along_axis(probs, top1[..., None], axis=-1)[..., 0]
            masked = jnp.where(jax.nn.one_hot(top1, probs.shape[-1], dtype=bool), -jnp.inf, probs)
            top2 = jnp.argmax(masked, axis=-1)
            t2v = jnp.take_along_axis(masked, top2[..., None], axis=-1)[..., 0]
            denom = t1v + t2v + 1e-09
            combine = jnp.stack([t1v / denom, t2v / denom], axis=-1)
            idx = jnp.stack([top1, top2], axis=-1)
            return (combine, idx)
        residual = x
        mu = jnp.mean(x, axis=-1, keepdims=True)
        var = jnp.mean(jnp.square(x - mu), axis=-1, keepdims=True)
        xn = (x - mu) / jnp.sqrt(var + 1e-05) * gamma + beta
        combine, idx = _top2_gate(xn, Wg)
        n_expert = Wg.shape[0]
        onehot = jax.nn.one_hot(idx, n_expert, dtype=x.dtype)
        gates = jnp.einsum('bns,bnse->ebn', combine, onehot)

        def body(acc, params):
            w1, b1e, w2, b2e, g = params
            h = jax.nn.gelu(jnp.einsum('bnd,df->bnf', xn, w1) + b1e, approximate=True)
            y = jnp.einsum('bnf,fd->bnd', h, w2) + b2e
            return (acc + g[..., None] * y, None)
        out, _ = jax.lax.scan(body, jnp.zeros_like(x), (W1, b1, W2, b2, gates))
        return residual + out

    def _L1_attn_ref(x, Wq, Wk, Wv, Wo, bo):
        import jax, jax.numpy as jnp
        import numpy as np
        HEADS = 16
        LOCAL_HEADS = 4
        DIM = 128
        DH = DIM // HEADS
        WINDOW = 128
        BLINDSPOT = 64

        def _look_around(x, buckets):
            pad_cfg = ((0, 0), (1, 0)) + ((0, 0),) * (x.ndim - 2)
            pv = -1.0 if jnp.issubdtype(x.dtype, jnp.floating) else -1
            p = jnp.pad(x, pad_cfg, constant_values=pv)
            return jnp.concatenate([p[:, :buckets], p[:, 1:buckets + 1]], axis=2)

        def _local_attn(q, k, v):
            b, lh, t, e = q.shape
            bm = b * lh
            buckets = t // WINDOW
            bq = q.reshape(bm, buckets, WINDOW, e)
            bk = k.reshape(bm, buckets, WINDOW, e)
            bv = v.reshape(bm, buckets, WINDOW, e)
            bk2 = _look_around(bk, buckets)
            bv2 = _look_around(bv, buckets)
            ticker = jnp.arange(t, dtype=jnp.int32).reshape(1, buckets, WINDOW)
            bq_k = _look_around(ticker, buckets)
            dots = jnp.einsum('buie,buje->buij', bq, bk2) * e ** (-0.5)
            mask_value = -jnp.finfo(dots.dtype).max
            causal_mask = ticker[:, :, :, None] < bq_k[:, :, None, :]
            pad_mask = bq_k[:, :, None, :] == -1
            dots = jnp.where(causal_mask | pad_mask, mask_value, dots)
            attn = jax.nn.softmax(dots, axis=-1)
            out = jnp.einsum('buij,buje->buie', attn, bv2)
            return out.reshape(b, lh, t, e)

        def _causal_linear_attn(q, k, v):
            b, h, n, e = q.shape
            u = n // BLINDSPOT
            q = jax.nn.softmax(q, axis=-1)
            k = jax.nn.elu(k) + 1.0
            bq = q.reshape(b, h, u, BLINDSPOT, e)
            bk = k.reshape(b, h, u, BLINDSPOT, e)
            bv = v.reshape(b, h, u, BLINDSPOT, e)
            bk_cumsum = jnp.cumsum(bk.sum(axis=-2), axis=-2)
            ctx = jnp.einsum('bhund,bhune->bhude', bk, bv)
            ctx = jnp.cumsum(ctx, axis=2)
            ctx = ctx / (bk_cumsum[..., None] + 1e-06)
            ctx = jnp.pad(ctx, ((0, 0), (0, 0), (1, 0), (0, 0), (0, 0)))[:, :, :u]
            attn = jnp.einsum('bhund,bhude->bhune', bq, ctx)
            return attn.reshape(b, h, n, e)
        b, t, dim = x.shape
        q = x @ Wq
        k = x @ Wk
        v = x @ Wv
        mh = lambda z: z.reshape(b, t, HEADS, DH).transpose(0, 2, 1, 3)
        q, k, v = (mh(q), mh(k), mh(v))
        lq, gq = (q[:, :LOCAL_HEADS], q[:, LOCAL_HEADS:])
        lk, gk = (k[:, :LOCAL_HEADS], k[:, LOCAL_HEADS:])
        lv, gv = (v[:, :LOCAL_HEADS], v[:, LOCAL_HEADS:])
        local_out = _local_attn(lq, lk, lv)
        global_out = _causal_linear_attn(gq, gk, gv)
        attn = jnp.concatenate([local_out, global_out], axis=1)
        attn = attn.transpose(0, 2, 1, 3).reshape(b, t, dim)
        return attn @ Wo + bo

    def _L1_ffn_ref(x, gate_w, gate_b, w1, b1, w2, b2):
        import jax, jax.numpy as jnp
        import numpy as np
        B, S, D = (8, 256, 128)
        E, K = (8, 2)
        H = 4 * D
        logits = jnp.einsum('bsd,de->bse', x, gate_w) + gate_b
        probs = jax.nn.softmax(logits, axis=-1)
        top_w, top_i = jax.lax.top_k(probs, K)
        top_w = top_w / jnp.sum(top_w, axis=-1, keepdims=True)
        out = jnp.zeros_like(x)
        for e in range(E):
            w_e = jnp.sum(jnp.where(top_i == e, top_w, 0.0), axis=-1)
            h = jax.nn.gelu(jnp.einsum('bsd,dh->bsh', x, w1[e]) + b1[e], approximate=False)
            y = jnp.einsum('bsh,hd->bsd', h, w2[e]) + b2[e]
            out = out + w_e[..., None] * y
        return out
    x = L0_attn_inputs
    mod = (_silu(L0_c) @ L0_wmod).reshape(L0_c.shape[0], 6, 1, -1)
    sa, ca, ga, sb, cb, gb = (mod[:, 0], mod[:, 1], mod[:, 2], mod[:, 3], mod[:, 4], mod[:, 5])
    ga = (2 * (ga >= 0) - 1) * jnp.maximum(jnp.abs(ga), 0.25)
    gb = (2 * (gb >= 0) - 1) * jnp.maximum(jnp.abs(gb), 0.25)
    h = _layernorm(x, axis=-1) * (1 + ca) + sa
    x = x + ga * _L0_attn_ref(h, L0_attn_gamma, L0_attn_beta, L0_attn_W_proj, L0_attn_b_proj, L0_attn_W_fc, L0_attn_b_fc, L0_attn_W_bc, L0_attn_b_bc, L0_attn_W_x1, L0_attn_b_x1, L0_attn_W_dt1, L0_attn_b_dt1, L0_attn_A_log1, L0_attn_D1, L0_attn_W_x2, L0_attn_b_x2, L0_attn_W_dt2, L0_attn_b_dt2, L0_attn_A_log2, L0_attn_D2)
    h = _layernorm(x, axis=-1) * (1 + cb) + sb
    x = x + gb * _L0_ffn_ref(h, L0_ffn_gamma, L0_ffn_beta, L0_ffn_Wg, L0_ffn_W1, L0_ffn_b1, L0_ffn_W2, L0_ffn_b2)
    mod = (_silu(L1_c) @ L1_wmod).reshape(L1_c.shape[0], 6, 1, -1)
    sa, ca, ga, sb, cb, gb = (mod[:, 0], mod[:, 1], mod[:, 2], mod[:, 3], mod[:, 4], mod[:, 5])
    ga = (2 * (ga >= 0) - 1) * jnp.maximum(jnp.abs(ga), 0.25)
    gb = (2 * (gb >= 0) - 1) * jnp.maximum(jnp.abs(gb), 0.25)
    h = _layernorm(x, axis=-1) * (1 + ca) + sa
    x = x + ga * _L1_attn_ref(h, L1_attn_Wq, L1_attn_Wk, L1_attn_Wv, L1_attn_Wo, L1_attn_bo)
    h = _layernorm(x, axis=-1) * (1 + cb) + sb
    x = x + gb * _L1_ffn_ref(h, L1_ffn_gate_w, L1_ffn_gate_b, L1_ffn_w1, L1_ffn_b1, L1_ffn_w2, L1_ffn_b2)
    return x

_drawn_inputs = setup_inputs


def setup_inputs(seed=0):
    import zlib

    import numpy as np

    out = dict(_drawn_inputs(seed))
    spreads = {'L0_attn_gamma': (1.0, 0.6),
     'L0_attn_beta': (0.0, 0.8),
     'L0_attn_b_proj': (0.0, 0.345),
     'L0_attn_b_fc': (0.0, 0.8),
     'L0_attn_b_bc': (0.0, 0.8),
     'L0_attn_b_x1': (0.0, 0.8),
     'L0_attn_b_dt1': (-4.0, 0.6),
     'L0_attn_D1': (1.0, 0.6),
     'L0_attn_b_x2': (0.0, 0.8),
     'L0_attn_b_dt2': (-4.0, 0.6),
     'L0_attn_D2': (1.0, 0.6),
     'L0_ffn_gamma': (1.0, 0.2),
     'L0_ffn_beta': (0.0, 0.438)}
    factors = {'L0_attn_W_fc': 8.0,
     'L0_attn_W_bc': 8.0,
     'L0_attn_W_x1': 8.0,
     'L0_attn_W_dt1': 8.0,
     'L0_attn_A_log1': 8.0,
     'L0_attn_W_x2': 8.0,
     'L0_attn_W_dt2': 8.0,
     'L0_attn_A_log2': 8.0,
     'L0_ffn_b1': 64.0,
     'L0_ffn_b2': 54.044,
     'L1_attn_bo': 36.471,
     'L1_ffn_gate_b': 20.742,
     'L1_ffn_b1': 33.35,
     'L1_ffn_b2': 23.425,
     'L1_attn_Wq': 2.937,
     'L1_attn_Wk': 2.799,
     'L1_ffn_w1': 3.155}
    for name, (base, spread) in spreads.items():
        noise = np.random.default_rng([zlib.crc32(name.encode()), seed]).standard_normal(out[name].shape)
        drawn = base * np.exp(spread * noise) if base else spread * noise
        out[name] = jnp.asarray(drawn.astype(out[name].dtype))
    for name, factor in factors.items():
        out[name] = (out[name] * factor).astype(out[name].dtype)
    return out
```

```python
from contextlib import ExitStack

import numpy as np

import concourse.bass as bass
from concourse import mybir

F32 = mybir.dt.float32
F32R = mybir.dt.float32r
ALU = mybir.AluOpType
ACT = mybir.ActivationFunctionType
AX = mybir.AxisListType

D = 128
NSEQ, SEQ = 32, 256
TOK = NSEQ * SEQ
R, NS = 64, 16
CH = 1024
NCH = TOK // CH
SPC = CH // SEQ
HB = 512
SA, CA, GA, SB, CB, GB = range(6)

C_ID, C_AVG, C_SEL = 0, 128, 256
C_END = 288
(V_GAM, V_BET, V_BPROJ, V_BFC, V_BBC, V_BDT1, V_BDT2, V_D1, V_D2, V_BX1, V_BX2) = range(11)
V_ALOG = 11
V_CT = V_ALOG + 2 * NS
V_END = V_CT + 2 * NSEQ
W_PROJ, W_FC, W_BC, W_X1, W_X2 = 0, 128, 256, 384, 480
W_END = 576


class Steps:

    def __init__(self, sem, names):
        self.sem, self.names, self.per, self.at = sem, list(names), len(names), 0
        self.index = {n: i + 1 for i, n in enumerate(self.names)}
        assert len(self.index) == self.per, "two steps of one name"

    def step(self, name):
        assert self.names[self.at % self.per] == name, (self.names[self.at % self.per], name)
        self.at += 1
        return 1

    def now(self, c, name):
        return (c + 1) * self.per + self.index[name]

    def before(self, c, name):
        return c * self.per + self.index[name]

    def at0(self, name):
        return self.index[name]


PE_1 = {"mean1": 6, "var1": 13, "mean2": 19, "var2": 22}
PE_2 = {"proj": 0, "fc": 2, "bc": 4, "x1": 9, "wdt1": 11, "x2": 15, "wdt2": 17}
ACT_1 = {"sq1": 9, "ln1": 15, "rs1": 15, "h0": 17, "h1": 17, "h2": 18, "h3": 18, "sq2": 22, "ln2": 24, "rs2": 24,
         "xn": 27}
ACT_2 = {"pj": 2, "vu1": 4, "au1": 4, "eu1": 5, "lu1": 5, "vu2": 6, "au2": 6, "eu2": 7, "lu2": 7, "ez": 8, "lz": 10,
         "sz": 10, "dbc1": 11, "vd1": 13, "ad1": 13, "ed1": 14, "ld1": 14, "dbc2": 17, "vd2": 19, "ad2": 19,
         "ed2": 20, "ld2": 20}
DVE_1 = {"xc": 8, "xg0": 20, "xg1": 20, "xg2": 20, "xg3": 20, "hc": 21}
DVE_2 = {"mz": 3, "tu1": 6, "tu2": 8, "u1": 9, "u2": 11, "bh1": 12, "bl1": 12, "acc": 13, "td1": 15, "d1": 17, "bh2": 18,
         "bl2": 18, "td2": 21, "d2": 24}
POOL_1 = {"xh": 16, "hn": 25}
POOL_2 = {"cu1": 7, "su1": 7, "cu2": 9, "su2": 9, "ud1": 11, "z": 11, "cd1": 15, "sd1": 15, "du1": 18,
          "cd2": 21, "sd2": 21, "du2": 25}
READER = {"mean1": "xc", "var1": "ln1", "mean2": "hc", "var2": "ln2", "proj": "pj", "fc": "vu1", "bc": "vu2",
          "x1": "dbc1", "wdt1": "vd1", "x2": "dbc2", "wdt2": "vd2"}
NK = 2 * NS
POOL_B = [k for k in range(NK) if k % 2 == 1]


class Kept:

    def __init__(self, nc, ctx):
        def sb(name, shape, dt=F32):
            return ctx.enter_context(nc.sbuf_tensor(name, shape, dt))

        self.sem = lambda name: ctx.enter_context(nc.semaphore(name))
        self.x_f = sb("x_f", [D, TOK])
        self.cst = sb("cst", [128, C_END])
        self.mod = sb("mod", [128, 2, 6, NSEQ])
        self.eps = sb("eps", [128, 2])
        self.ident, self.avg = self.cst[:, C_ID:C_ID + 128], self.cst[:, C_AVG:C_AVG + 128]


def build(nc, xT, consts, vec, wpk, wdt, wmod, fvec, w1_0, w2_0, b2_0, w1_1, w2_1, b2_1, wat, out):
    with ExitStack() as ctx:
        kept = Kept(nc, ctx)
        ssm_layer(nc, kept, xT, consts, vec, wpk, wdt, wmod)
        mixture_layer(nc, kept, 0, fvec, w1_0, w2_0, b2_0)
        attention_layer(nc, kept, wat)
        mixture_layer(nc, kept, 1, fvec, w1_1, w2_1, b2_1, out)


def ssm_layer(nc, kept, xT, consts, vec, wpk, wdt, wmod):
    with ExitStack() as ctx:
        def sb(name, shape, dt=F32):
            return ctx.enter_context(nc.sbuf_tensor(name, shape, dt))

        def ps(name, shape):
            return ctx.enter_context(nc.psum_tensor(name, shape, F32))

        sem, x_f, cst, mod, eps, ident, avg = (kept.sem, kept.x_f, kept.cst, kept.mod, kept.eps, kept.ident,
                                               kept.avg)
        vecs = sb("vecs", [128, V_END])
        w = sb("w", [128, W_END])
        wd = sb("wd", [R, 2 * D])
        sel = sb("sel", [128, 32], F32R)
        msc = sb("msc", [128, 4, 2 * NSEQ])
        negA = sb("negA", [128, 2 * NS])

        def col(v, p=128):
            return vecs[0:p, v:v + 1]

        def two(name, shape=(128, CH), dt=F32):
            return [sb(f"{name}{i}", list(shape), dt) for i in range(2)]

        z_, acc_ = two("z"), two("acc")
        delta_ = [two("delta1"), two("delta2")]
        du_ = [two("du1"), two("du2")]
        bcs_ = [two("bcs1", (128, CH), F32R), two("bcs2", (128, CH), F32R)]
        dA, dB = two("dA"), two("dB")
        hs = [sb(f"hs{i}", [128, CH]) for i in range(3)]
        hC = two("hC")
        Bc = sb("Bc", [128, CH])
        A0, A1, H = sb("A0", [128, CH]), sb("A1", [128, CH]), sb("H", [128, CH])
        XN, PJ = sb("XN", [128, CH]), sb("PJ", [128, CH])
        Pv = two("Pv")
        Pe = two("Pe")
        Pl = two("Pl")
        Pt = two("Pt")
        wm = [t[:, 0:6 * D] for t in Pv]
        U = [sb("U1", [128, CH]), sb("U2", [128, CH])]
        dbc = sb("dbc", [R + 2 * NS, CH])

        py, pB, pC, pP = ps("py", [128, CH]), ps("pB", [128, CH]), ps("pC", [128, CH]), ps("pP", [128, CH])

        ld0, ldc, ldx = sem("ld0"), sem("ldc"), sem("ldx")
        set_pe, set_act, set_dve, set_pool = sem("set_pe"), sem("set_act"), sem("set_dve"), sem("set_pool")
        pe_1, act_1, dve_1, pool_1 = (Steps(sem(n), t) for n, t in
                                      (("pe_1", PE_1), ("act_1", ACT_1), ("dve_1", DVE_1), ("pool_1", POOL_1)))
        pe_2, act_2, dve_2, pool_2 = (Steps(sem(n), t) for n, t in
                                      (("pe_2", PE_2), ("act_2", ACT_2), ("dve_2", DVE_2), ("pool_2", POOL_2)))
        pe_names = ["B0", "C0", "B1"]
        for k in range(NK):
            pe_names += ([f"B{k + 2}"] if k + 2 < NK else []) + ([f"C{k + 1}"] if k + 1 < NK else []) + [f"y{k}"]
        pe_s = Steps(sem("pe_s"), pe_names)
        act_names = ["e0"]
        for k in range(NK):
            if k + 1 < NK:
                act_names += [f"e{k + 1}"] + ([f"b{k + 1}"] if k + 1 in POOL_B else [])
        act_s = Steps(sem("act_s"), act_names)
        dve_names = ["b0"]
        for k in range(NK):
            dve_names += [f"s{k}"] + ([f"b{k + 1}"] if k + 1 < NK and k + 1 not in POOL_B else [])
            dve_names += [f"c{k - 1}"] if k else []
        dve_names += [f"c{NK - 1}"]
        dve_names += ["y0", "y1"] + [f"x{q}" for q in range(SPC)]
        dve_s = Steps(sem("dve_s"), dve_names)
        pool_s = Steps(sem("pool_s"), [f"b{k}" for k in POOL_B])

        block = ctx.enter_context(nc.Block())

        def woven(k, c, with_2, with_1, steps_2, steps_1, step_2, step_1):
            for name, at in steps_2.items():
                if with_2 and at == k:
                    step_2(name, c + 1)
            for name, at in steps_1.items():
                if with_1 and at == k:
                    step_1(name, c + 2)

        def rounds(eng, steps_2, steps_1, step_2, step_1, states, at_loop=lambda c: None):
            for name in steps_1:
                step_1(name, 0)
            for name in steps_2:
                step_2(name, 0, 0)
            for name in steps_1:
                step_1(name, 1)
            with eng.Fori(0, NCH // 2 - 1) as i:
                at_loop(i * 2)
                for p in range(2):
                    states(i * 2 + p, p, True, True)
            states(NCH - 2, 0, True, False)
            states(NCH - 1, 1, False, False)

        @block.sync
        def _(sp):
            sp.dma_start(cst[:, :], consts).then_inc(ldc, 16)
            sp.dma_start(vecs[:, :], vec).then_inc(ldc, 16)
            for l in range(2):
                sp.dma_start(wm[l], wmod[:, l, :]).then_inc(ldc, 16)
            sp.dma_start(x_f[:, 0:CH], xT[:, 0:CH]).then_inc(ld0, 16)
            sp.dma_start(w[:, :], wpk).then_inc(ldc, 16)
            sp.dma_start(wd[:, :], wdt).then_inc(ldc, 16)
            sp.dma_start(x_f[:, CH:TOK], xT[:, CH:TOK]).then_inc(ldx, 16)

        @block.tensor
        def _(pe):
            for s in (pe_1, pe_2, pe_s):
                pe.sem_inc(s.sem, s.per)
            pe.wait_ge(ldc, 96)
            pe.wait_ge(set_dve, 3)
            for l in range(2):
                for j in range(6):
                    at = (l * 6 + j) * NSEQ
                    mm = pe.matmul(pP[:, at:at + NSEQ], wm[l][:, j * D:(j + 1) * D],
                                   msc[:, 3, l * NSEQ:(l + 1) * NSEQ], start=True, stop=True)
            mm.then_inc(set_pe, 1)

            def full(dst, lhsT, rhs, name, m=128, start=True, stop=True, S=None):
                for q in range(CH // HB):
                    mm = pe.matmul(dst[0:m, q * HB:(q + 1) * HB], lhsT, rhs(q), start=start, stop=stop)
                mm.then_inc(S.sem, S.step(name))

            def half(t):
                return lambda q: t[:, q * HB:(q + 1) * HB]

            reader = [(act_1, 0, None)]

            def free_pP():
                S, c, name = reader[0]
                if name:
                    pe.wait_ge(S.sem, S.now(c, name))

            def step_1(name, c):
                free_pP()
                if name == "mean1":
                    if isinstance(c, int) and c == 0:
                        pe.wait_ge(ld0, 16)
                        pe.wait_ge(set_dve, 4)
                    else:
                        pe.wait_ge(ldx, 16)
                    full(pP, avg, lambda q: x_f[:, bass.ds(c * CH + q * HB, HB)], name, S=pe_1)
                elif name == "mean2":
                    pe.wait_ge(act_1.sem, act_1.now(c, "h3"))
                    full(pP, avg, half(H), name, S=pe_1)
                else:
                    pe.wait_ge(act_1.sem, act_1.now(c, f"sq{name[3]}"))
                    full(pP, avg, half(A1), name, S=pe_1)
                reader[0] = (dve_1 if name[0] == "m" else act_1, c, READER[name])

            def step_2(name, c, p=0):
                free_pP()
                if name == "proj":
                    pe.wait_ge(act_1.sem, act_1.now(c, "xn"))
                    full(pP, w[:, W_PROJ:W_PROJ + D], half(XN), name, S=pe_2)
                elif name in ("fc", "bc"):
                    at = {"fc": W_FC, "bc": W_BC}[name]
                    pe.wait_ge(act_2.sem, act_2.now(c, "pj"))
                    full(pP, w[:, at:at + D], half(PJ), name, S=pe_2)
                elif name[0] == "x":
                    s = int(name[1]) - 1
                    at = (W_X1, W_X2)[s]
                    pe.wait_ge(dve_2.sem, dve_2.now(c, f"u{s + 1}"))
                    full(pP, w[:, at:at + R + 2 * NS], half(U[s]), name, m=R + 2 * NS, S=pe_2)
                else:
                    s = int(name[3]) - 1
                    pe.wait_ge(act_2.sem, act_2.now(c, f"dbc{s + 1}"))
                    full(pP, wd[:, s * D:(s + 1) * D], lambda q: dbc[0:R, q * HB:(q + 1) * HB], name, S=pe_2)
                reader[0] = (act_2, c, READER[name])

            def spread(dst, k, is_c, p, name):
                row = (k % NS) + (NS if is_c else 0)
                rows = bcs_[k // NS][p]
                full(dst, sel[64:128, row:row + 1].to_broadcast([64, 128]),
                     lambda q: rows[64:128, q * HB:(q + 1) * HB], name, S=pe_s)

            def states(c, p, with_2, with_1):
                pe.wait_ge(dve_2.sem, dve_2.now(c, "bl2"))
                pe.wait_ge(dve_s.sem, dve_s.before(c, f"c{NK - 1}"))
                pe.wait_ge(act_s.sem, act_s.before(c, f"b{NK - 1}"))
                spread(pB, 0, False, p, "B0")
                spread(pC, 0, True, p, "C0")
                pe.wait_ge(dve_s.sem, dve_s.now(c, "b0"))
                spread(pB, 1, False, p, "B1")

                for k in range(NK):
                    if k + 2 < NK:
                        if k + 1 in POOL_B:
                            pe.wait_ge(act_s.sem, act_s.now(c, f"b{k + 1}"))
                        else:
                            pe.wait_ge(dve_s.sem, dve_s.now(c, f"b{k + 1}"))
                        spread(pB, k + 2, False, p, f"B{k + 2}")
                    pe.wait_ge(dve_s.sem, dve_s.now(c, f"c{k}"))
                    if k + 1 < NK:
                        spread(pC, k + 1, True, p, f"C{k + 1}")
                    if k == 0:
                        pe.wait_ge(dve_s.sem, dve_s.before(c, "y0"))
                    full(py, ident, half(hC[k % 2]), f"y{k}", start=k == 0, stop=k == NK - 1, S=pe_s)
                    woven(k, c, with_2, with_1, PE_2, PE_1, step_2, step_1)

            def at_loop(c):
                free_pP()
                reader[0] = (act_1, c + 1, READER["var2"])

            rounds(pe, PE_2, PE_1, step_2, step_1, states, at_loop)

        @block.scalar
        def _(act):
            for s in (act_1, act_2, act_s):
                act.sem_inc(s.sem, s.per)
            act.preload_act_table_set("natural_log_exp_and_others")
            act.wait_ge(set_dve, 1)
            act.activation(msc[:, 1, :], msc[:, 0, :], ACT.Exp).then_inc(set_act, 1)
            act.wait_ge(set_act, 1)
            act.activation(msc[:, 2, :], msc[:, 1, :], ACT.Ln, bias=1.0).then_inc(set_act, 1)
            act.wait_ge(set_act, 2)
            act.activation(msc[:, 1, :], msc[:, 2, :], ACT.Exp, scale=-1.0).then_inc(set_act, 1)
            act.activation(negA[:, :], vecs[:, V_ALOG:V_ALOG + 2 * NS], ACT.Exp).then_inc(set_act, 1)
            act.wait_ge(set_act, 4)
            act.mul(negA[:, :], negA[:, :], -1.0).then_inc(set_act, 1)

            act.wait_ge(set_dve, 7)
            act.wait_ge(set_pool, 4)

            def do(dst, src, f, name, S, **kw):
                act.activation(dst, src, f, **kw).then_inc(S.sem, S.step(name))

            def step_1(name, c):
                if name == "sq1":
                    act.wait_ge(dve_1.sem, dve_1.now(c, "xc"))
                    act.wait_ge(pool_1.sem, pool_1.before(c, "hn"))
                    do(A1[:, :], A0[:, :], ACT.Square, name, act_1)
                elif name == "sq2":
                    act.wait_ge(dve_1.sem, dve_1.now(c, "hc"))
                    do(A1[:, :], A0[:, :], ACT.Square, name, act_1)
                elif name in ("ln1", "ln2"):
                    act.wait_ge(pe_1.sem, pe_1.now(c, f"var{name[2]}"))
                    do(A1[:, :], pP[:, :], ACT.Ln, name, act_1, bias=eps[:, int(name[2]) - 1:int(name[2])])
                elif name in ("rs1", "rs2"):
                    act.wait_ge(act_1.sem, act_1.now(c, f"ln{name[2]}"))
                    do(A1[:, :], A1[:, :], ACT.Exp, name, act_1, scale=-0.5)
                elif name == "xn":
                    act.wait_ge(pool_1.sem, pool_1.now(c, "hn"))
                    act.wait_ge(pe_2.sem, pe_2.before(c, "proj"))
                    do(XN[:, :], A0[:, :], ACT.Identity, name, act_1, scale=col(V_GAM), bias=col(V_BET))
                else:
                    q = int(name[1])
                    act.wait_ge(pool_1.sem, pool_1.now(c, "xh"))
                    act.wait_ge(dve_1.sem, dve_1.before(c, "hc"))
                    b = c * SPC + q
                    do(H[:, q * SEQ:(q + 1) * SEQ], A0[:, q * SEQ:(q + 1) * SEQ], ACT.Identity, name, act_1,
                       scale=mod[:, 0, CA, bass.ds(b, 1)], bias=mod[:, 0, SA, bass.ds(b, 1)])

            def step_2(name, c, p):
                if name == "pj":
                    act.wait_ge(pe_2.sem, pe_2.now(c, "proj"))
                    act.wait_ge(pe_2.sem, pe_2.before(c, "bc"))
                    act.wait_ge(pool_2.sem, pool_2.before(c, "z"))
                    do(PJ[:, :], pP[:, :], ACT.Identity, name, act_2, bias=col(V_BPROJ))
                elif name in ("ez", "lz", "sz"):
                    z = z_[p][:, :]
                    if name == "ez":
                        act.wait_ge(dve_2.sem, dve_2.now(c, "mz"))
                        do(z, z, ACT.Exp, name, act_2, scale=-1.0)
                    elif name == "lz":
                        act.wait_ge(act_2.sem, act_2.now(c, "ez"))
                        do(z, z, ACT.Ln, name, act_2, bias=1.0)
                    else:
                        act.wait_ge(act_2.sem, act_2.now(c, "lz"))
                        do(z, z, ACT.Exp, name, act_2, scale=-1.0)
                elif name.startswith("dbc"):
                    s = int(name[3]) - 1
                    act.wait_ge(pe_2.sem, pe_2.now(c, f"x{s + 1}"))
                    act.wait_ge(dve_2.sem, dve_2.before(c, "bl2") if s == 0 else dve_2.now(c, "bl1"))
                    do(dbc[:, :], pP[0:R + 2 * NS, :], ACT.Identity, name, act_2, bias=col(V_BX1 + s, R + 2 * NS))
                else:
                    kind, which, s = name[0], name[1], int(name[2]) - 1
                    v, e, l = Pv[s], Pe[s], Pl[s]
                    if kind == "v":
                        b = {"u": V_BFC, "d": V_BDT1}[which] + s
                        act.wait_ge(pe_2.sem, pe_2.now(c, {"u": ("fc", "bc")[s], "d": f"wdt{s + 1}"}[which]))
                        if which == "u":
                            act.wait_ge(dve_2.sem, dve_2.before(c, f"d{s + 1}"))
                        else:
                            act.wait_ge(dve_2.sem, dve_2.now(c, f"u{s + 1}"))
                        do(v[:, :], pP[:, :], ACT.Identity, name, act_2, bias=col(b))
                    elif kind == "a":
                        act.wait_ge(act_2.sem, act_2.now(c, f"v{which}{s + 1}"))
                        do(e[:, :], v[:, :], ACT.Abs, name, act_2)
                    elif kind == "e":
                        act.wait_ge(act_2.sem, act_2.now(c, f"a{which}{s + 1}"))
                        do(e[:, :], e[:, :], ACT.Exp, name, act_2, scale=-1.0)
                    else:
                        act.wait_ge(act_2.sem, act_2.now(c, f"e{which}{s + 1}"))
                        do(l[:, :], e[:, :], ACT.Ln, name, act_2, bias=1.0)

            def later(t):
                return t.rearrange("p (s t) -> p s t", t=SEQ)[:, :, 1:SEQ]

            def states(c, p, with_2, with_1):
                def decay(k):
                    if k >= 2:
                        act.wait_ge(dve_s.sem, dve_s.now(c, f"s{k - 2}"))
                    else:
                        act.wait_ge(dve_s.sem, dve_s.before(c, f"s{NK - 2 + k}"))
                        act.wait_ge(dve_2.sem, dve_2.now(c, "d2"))
                    do(later(dA[k % 2][:, :]), later(delta_[k // NS][p][:, :]), ACT.Exp, f"e{k}", act_s,
                       scale=negA[:, k:k + 1])

                decay(0)
                for k in range(NK):
                    if k + 1 < NK:
                        decay(k + 1)
                        if k + 1 in POOL_B:
                            act.wait_ge(pe_s.sem, pe_s.now(c, f"B{k + 1}"))
                            last = POOL_B[POOL_B.index(k + 1) - 1]
                            act.wait_ge(pool_s.sem, pool_s.now(c, f"b{last}") if k + 1 != POOL_B[0]
                                        else pool_s.before(c, f"b{last}"))
                            do(Bc[:, :], pB[:, :], ACT.Copy, f"b{k + 1}", act_s)
                    woven(k, c, with_2, with_1, ACT_2, ACT_1, lambda n, cc: step_2(n, cc, 1 - p), step_1)

            rounds(act, ACT_2, ACT_1, step_2, step_1, states)

        @block.vector
        def _(dve):
            for s in (dve_1, dve_2, dve_s):
                dve.sem_inc(s.sem, s.per)
            dve.wait_ge(ldc, 96)
            dve.tensor_scalar(msc[:, 0, :], vecs[:, V_CT:V_END], -1.0, 44.0, ALU.mult, ALU.min).then_inc(set_dve, 1)
            dve.tensor_copy(sel[64:128, :], cst[64:128, C_SEL:C_SEL + 32]).then_inc(set_dve, 1)
            dve.wait_ge(set_act, 3)
            dve.tensor_tensor(msc[:, 3, :], vecs[:, V_CT:V_END], msc[:, 1, :], ALU.mult).then_inc(set_dve, 1)
            dve.wait_ge(set_pe, 1)
            mflat = mod[:, :, :, :].rearrange("p l j b -> p (l j b)")
            dve.tensor_copy(mflat, pP[:, 0:12 * NSEQ]).then_inc(set_dve, 1)
            dve.wait_ge(set_dve, 4)
            for l in range(2):
                for j in (CA, CB):
                    m = mod[:, l, j, :]
                    last = dve.tensor_scalar(m, m, 1.0, None, ALU.add)
            for l in range(2):
                for n, j in enumerate((GA, GB)):
                    o = slice(n * NSEQ, (n + 1) * NSEQ)
                    dve.tensor_scalar(msc[:, l, o], mod[:, l, j, :], 0.0, 2.0, ALU.is_ge, ALU.mult)
                    last = dve.scalar_tensor_tensor(msc[:, 2 + l, o], mod[:, l, j, :], -1.0, mod[:, l, j, :],
                                                    ALU.mult, ALU.max)
            last.then_inc(set_dve, 1)
            dve.wait_ge(set_dve, 5)
            dve.tensor_scalar(msc[:, 2:4, :], msc[:, 2:4, :], 0.25, None, ALU.max).then_inc(set_dve, 1)
            dve.wait_ge(set_dve, 6)
            for l in range(2):
                for n, j in enumerate((GA, GB)):
                    o = slice(n * NSEQ, (n + 1) * NSEQ)
                    last = dve.scalar_tensor_tensor(mod[:, l, j, :], msc[:, l, o], -1.0, msc[:, 2 + l, o],
                                                    ALU.add, ALU.mult)
            last.then_inc(set_dve, 1)

            def tt(dst, a, b, op, name, S):
                dve.tensor_tensor(dst, a, b, op).then_inc(S.sem, S.step(name))

            def gated(src, q, c, name, S):
                xq = x_f[:, bass.ds(c * CH + q * SEQ, SEQ)]
                dve.scalar_tensor_tensor(xq, src[:, q * SEQ:(q + 1) * SEQ], mod[:, 0, GA, bass.ds(c * SPC + q, 1)],
                                         xq, ALU.mult, ALU.add).then_inc(S.sem, S.step(name))

            def step_1(name, c):
                if name == "xc":
                    dve.wait_ge(pe_1.sem, pe_1.now(c, "mean1"))
                    dve.wait_ge(act_1.sem, act_1.before(c, "xn"))
                    tt(A0[:, :], x_f[:, bass.ds(c * CH, CH)], pP[:, :], ALU.subtract, name, dve_1)
                elif name == "hc":
                    dve.wait_ge(pe_1.sem, pe_1.now(c, "mean2"))
                    tt(A0[:, :], H[:, :], pP[:, :], ALU.subtract, name, dve_1)
                else:
                    if name == "xg0":
                        dve.wait_ge(act_1.sem, act_1.now(c, "h3"))
                    gated(H, int(name[2]), c, name, dve_1)

            def step_2(name, c, p):
                if name == "mz":
                    dve.wait_ge(act_2.sem, act_2.now(c, "pj"))
                    dve.tensor_scalar(z_[p][:, :], PJ[:, :], -44.0, None, ALU.max)\
                        .then_inc(dve_2.sem, dve_2.step(name))
                elif name in ("u1", "u2", "d1", "d2"):
                    s = int(name[1]) - 1
                    dst = U[s] if name[0] == "u" else delta_[s][p]
                    dve.wait_ge(pool_2.sem, pool_2.now(c, "s" + name))
                    if name[0] == "u":
                        dve.wait_ge(pool_2.sem, pool_2.before(c, f"du{s + 1}"))
                        dve.wait_ge(dve_2.sem, dve_2.before(c, "acc"))
                    dve.scalar_tensor_tensor(dst[:, :], Pv[s][:, :], 0.0, Pl[s][:, :], ALU.max, ALU.add)\
                        .then_inc(dve_2.sem, dve_2.step(name))
                elif name in ("tu1", "tu2", "td1", "td2"):
                    s = int(name[2]) - 1
                    dve.wait_ge(act_2.sem, act_2.now(c, f"e{name[1:]}"))
                    dve.wait_ge(pool_2.sem, pool_2.before(c, f"sd{s + 1}") if name[1] == "u"
                                else pool_2.now(c, f"su{s + 1}"))
                    dve.tensor_scalar(Pt[s][:, :], Pe[s][:, :], 1.0, -1.0, ALU.add, ALU.add)\
                        .then_inc(dve_2.sem, dve_2.step(name))
                elif name in ("bh1", "bh2"):
                    s = int(name[2]) - 1
                    dve.wait_ge(act_2.sem, act_2.now(c, f"dbc{s + 1}"))
                    dve.tensor_copy(bcs_[s][p][64:96, :], dbc[R:R + 2 * NS, :]).then_inc(dve_2.sem, dve_2.step(name))
                elif name in ("bl1", "bl2"):
                    s = int(name[2]) - 1
                    dve.wait_ge(dve_2.sem, dve_2.now(c, f"bh{s + 1}"))
                    tt(bcs_[s][p][96:128, :], dbc[R:R + 2 * NS, :], bcs_[s][p][64:96, :].bitcast(F32),
                       ALU.subtract, name, dve_2)
                else:
                    dve.wait_ge(pool_2.sem, pool_2.now(c, "ud1"))
                    dve.scalar_tensor_tensor(acc_[p][:, :], U[1][:, :], col(V_D2), acc_[p][:, :], ALU.mult, ALU.add)\
                        .then_inc(dve_2.sem, dve_2.step(name))

            def states(c, p, with_2, with_1):
                def b_product(k):
                    dve.wait_ge(pe_s.sem, pe_s.now(c, f"B{k}"))
                    if k >= 2:
                        dve.wait_ge(dve_s.sem, dve_s.now(c, f"s{k - 2}"))
                    tt(dB[k % 2][:, :], du_[k // NS][p][:, :], pB[:, :], ALU.mult, f"b{k}", dve_s)

                def c_product(k):
                    dve.wait_ge(dve_s.sem, dve_s.now(c, f"s{k}"))
                    dve.wait_ge(pe_s.sem, pe_s.now(c, f"C{k}"))
                    if k >= 2:
                        dve.wait_ge(pe_s.sem, pe_s.now(c, f"y{k - 2}"))
                    else:
                        dve.wait_ge(pe_s.sem, pe_s.before(c, f"y{NK - 2 + k}"))
                    tt(hC[k % 2][:, :], hs[k % 3][:, :], pC[:, :], ALU.mult, f"c{k}", dve_s)

                dve.wait_ge(pool_2.sem, pool_2.now(c, "du2"))
                b_product(0)
                for k in range(NK):
                    dve.wait_ge(act_s.sem, act_s.now(c, f"e{k}"))
                    if k in POOL_B:
                        dve.wait_ge(pool_s.sem, pool_s.now(c, f"b{k}"))
                    else:
                        dve.wait_ge(dve_s.sem, dve_s.now(c, f"b{k}"))
                    if k >= 3:
                        dve.wait_ge(dve_s.sem, dve_s.now(c, f"c{k - 3}"))
                    dve.tensor_tensor_scan(hs[k % 3][:, :], dA[k % 2][:, :], dB[k % 2][:, :], 0.0, ALU.mult, ALU.add)\
                        .then_inc(dve_s.sem, dve_s.step(f"s{k}"))
                    if k + 1 < NK and k + 1 not in POOL_B:
                        b_product(k + 1)
                    if k:
                        c_product(k - 1)
                    woven(k, c, with_2, with_1, DVE_2, DVE_1, lambda n, cc: step_2(n, cc, 1 - p), step_1)
                c_product(NK - 1)
                dve.wait_ge(pe_s.sem, pe_s.now(c, f"y{NK - 1}"))
                dve.wait_ge(dve_s.sem, dve_s.now(c, f"c{NK - 1}"))
                tt(hs[0][:, :], acc_[p][:, :], py[:, :], ALU.add, "y0", dve_s)
                dve.wait_ge(dve_s.sem, dve_s.now(c, "y0"))
                tt(hs[0][:, :], hs[0][:, :], z_[p][:, :], ALU.mult, "y1", dve_s)
                dve.wait_ge(dve_s.sem, dve_s.now(c, "y1"))
                for q in range(SPC):
                    gated(hs[0], q, c, f"x{q}", dve_s)
                dve.wait_ge(dve_s.sem, dve_s.now(c, f"x{SPC - 1}"))

            rounds(dve, DVE_2, DVE_1, step_2, step_1, states)

        @block.gpsimd
        def _(pool):
            for s in (pool_1, pool_2, pool_s):
                pool.sem_inc(s.sem, s.per)
            pool.memset(eps[:, 0:1], 1e-5).then_inc(set_pool, 1)
            pool.memset(eps[:, 1:2], 1e-6).then_inc(set_pool, 1)
            for i in range(2):
                pool.memset(dA[i][:, :], 0.0).then_inc(set_pool, 1)
            pool.wait_ge(set_pool, 4)

            def tt(dst, a, b, op, name, S):
                pool.tensor_tensor(dst, a, b, op).then_inc(S.sem, S.step(name))

            def step_1(name, c):
                pool.wait_ge(act_1.sem, act_1.now(c, {"xh": "rs1", "hn": "rs2"}[name]))
                tt(A0[:, :], A0[:, :], A1[:, :], ALU.mult, name, pool_1)

            def step_2(name, c, p):
                if name == "z":
                    pool.wait_ge(act_2.sem, act_2.now(c, "sz"))
                    tt(z_[p][:, :], PJ[:, :], z_[p][:, :], ALU.mult, name, pool_2)
                elif name == "ud1":
                    pool.wait_ge(dve_2.sem, dve_2.now(c, "u1"))
                    tt(acc_[p][:, :], U[0][:, :], col(V_D1).to_broadcast([128, CH]), ALU.mult, name, pool_2)
                elif name in ("du1", "du2"):
                    s = int(name[2]) - 1
                    pool.wait_ge(dve_2.sem, dve_2.now(c, f"d{s + 1}"))
                    tt(du_[s][p][:, :], delta_[s][p][:, :], U[s][:, :], ALU.mult, name, pool_2)
                else:
                    kind, which, s = name[0], name[1], int(name[2]) - 1
                    if kind == "c":
                        pool.wait_ge(dve_2.sem, dve_2.now(c, f"t{which}{s + 1}"))
                        tt(Pt[s][:, :], Pe[s][:, :], Pt[s][:, :], ALU.subtract, name, pool_2)
                    else:
                        pool.wait_ge(pool_2.sem, pool_2.now(c, f"c{which}{s + 1}"))
                        pool.wait_ge(act_2.sem, act_2.now(c, f"l{which}{s + 1}"))
                        tt(Pl[s][:, :], Pl[s][:, :], Pt[s][:, :], ALU.add, name, pool_2)

            def states(c, p, with_2, with_1):
                for k in range(NK):
                    if k + 1 in POOL_B:
                        b = k + 1
                        pool.wait_ge(act_s.sem, act_s.now(c, f"b{b}"))
                        if b >= 2:
                            pool.wait_ge(dve_s.sem, dve_s.now(c, f"s{b - 2}"))
                        else:
                            pool.wait_ge(dve_s.sem, dve_s.before(c, f"s{NK - 2 + b}"))
                        tt(dB[b % 2][:, :], du_[b // NS][p][:, :], Bc[:, :], ALU.mult, f"b{b}", pool_s)
                    woven(k, c, with_2, with_1, POOL_2, POOL_1, lambda n, cc: step_2(n, cc, 1 - p), step_1)

            rounds(pool, POOL_2, POOL_1, step_2, step_1, states)


GSUB = 4
SUB = 512
NG = TOK // (GSUB * SUB)
NT = TOK // 128
NE, NF = 8, 4
QS = SUB // SEQ
F_WG, F_GB, F_B1 = 0, NE, 2 * NE
F_PER = 2 * NE + NE * NF
F_GAM, F_BET = 2 * F_PER, 2 * F_PER + 1
F_RANK = 2 * F_PER + 2
F_END = F_RANK + NE


def mixture_layer(nc, kept, layer, fvec, w1, w2, b2, out=None):
    two_norms = layer == 0
    L = f"m{layer}_"
    with ExitStack() as ctx:
        def sb(name, shape, dt=F32):
            return ctx.enter_context(nc.sbuf_tensor(L + name, shape, dt))

        def sem(name):
            return kept.sem(L + name)

        x_f, mod, eps, ident, avg = kept.x_f, kept.mod, kept.eps, kept.ident, kept.avg
        xn_f = sb("xn_f", [D, TOK])
        fv = sb("fv", [128, F_END])
        o = layer * F_PER
        wg, gbias = fv[:, o + F_WG:o + F_WG + NE], fv[:, o + F_GB:o + F_GB + NE]
        W1 = sb("W1", [D, NE * NF * 128])
        W2 = sb("W2", [128, NE * NF * D])
        b2b = sb("b2b", [128, NE * D])
        gate = sb("gate", [128, NT, NE])
        loaded = sem("loaded")
        loaded_w = sem("loaded_w")

        names = lambda kinds: [f"{k}{j}" for k in kinds for j in range(GSUB)]
        if two_norms:
            pe_n = Steps(sem("pe_n"), names(("mean1_", "var1_", "mean2_", "var2_", "lg_")))
            act_n = Steps(sem("act_n"), names(("sq1_", "ln1_", "rs1_", "h_", "sq2_", "ln2_", "rs2_", "xn_")))
            dve_n = Steps(sem("dve_n"), names(("xc_", "xh_", "xg_", "hc_", "hn_", "lc_")))
        else:
            pe_n = Steps(sem("pe_n"), names(("mean1_", "var1_", "lg_")))
            act_n = Steps(sem("act_n"), names(("sq1_", "ln1_", "rs1_", "h_")))
            dve_n = Steps(sem("dve_n"), names(("xc_", "xh_", "lc_")))
        pool_n = Steps(sem("pool_n"), names(("keep_",)))
        dve_g = Steps(sem("dve_g"), GATE_DVE)
        act_g = Steps(sem("act_g"), ["exp"])

        with ExitStack() as pre:
            A = [pre.enter_context(nc.sbuf_tensor(f"{L}A{j}", [128, SUB], F32)) for j in range(GSUB)]
            B = [pre.enter_context(nc.sbuf_tensor(f"{L}B{j}", [128, SUB], F32)) for j in range(GSUB)]
            H = [pre.enter_context(nc.sbuf_tensor(f"{L}H{j}", [128, SUB], F32)) for j in range(GSUB)]
            pa = [pre.enter_context(nc.psum_tensor(f"{L}pa{j}", [128, SUB], F32)) for j in range(GSUB)]
            pb = [pre.enter_context(nc.psum_tensor(f"{L}pb{j}", [128, SUB], F32)) for j in range(GSUB)]
            lg = pre.enter_context(nc.sbuf_tensor(L + "lg", [128, NT, NE], F32))
            t3 = [pre.enter_context(nc.sbuf_tensor(f"{L}t3{j}", [128, NT, NE], F32)) for j in range(3)]
            t1 = [pre.enter_context(nc.sbuf_tensor(f"{L}t1{j}", [128, NT, 1], F32)) for j in range(4)]
            block = pre.enter_context(nc.Block())

            def at(g, j, n=SUB, off=0):
                return bass.ds(g * (GSUB * SUB) + j * SUB + off, n)

            @block.sync
            def _(sp):
                sp.dma_start(fv[:, :], fvec).then_inc(loaded, 16)
                sp.dma_start(W1[:, :], w1).then_inc(loaded_w, 16)
                sp.dma_start(W2[:, :], w2).then_inc(loaded_w, 16)
                sp.dma_start(b2b[:, :], b2).then_inc(loaded_w, 16)

            @block.tensor
            def _(pe):
                pe.sem_inc(pe_n.sem, pe_n.per)
                pe.wait_ge(loaded, 16)
                with pe.Fori(0, NG) as g:
                    for j in range(GSUB):
                        pe.wait_ge(dve_n.sem, dve_n.before(g, f"lc_{j}"))
                        pe.matmul(pa[j][:, :], avg, x_f[:, at(g, j)], start=True, stop=True)\
                            .then_inc(pe_n.sem, pe_n.step(f"mean1_{j}"))
                    for j in range(GSUB):
                        pe.wait_ge(act_n.sem, act_n.now(g, f"sq1_{j}"))
                        pe.matmul(pb[j][:, :], avg, B[j][:, :], start=True, stop=True)\
                            .then_inc(pe_n.sem, pe_n.step(f"var1_{j}"))
                    if two_norms:
                        for j in range(GSUB):
                            pe.wait_ge(act_n.sem, act_n.now(g, f"h_{j}"))
                            pe.matmul(pa[j][:, :], avg, H[j][:, :], start=True, stop=True)\
                                .then_inc(pe_n.sem, pe_n.step(f"mean2_{j}"))
                        for j in range(GSUB):
                            pe.wait_ge(act_n.sem, act_n.now(g, f"sq2_{j}"))
                            pe.matmul(pb[j][:, :], avg, B[j][:, :], start=True, stop=True)\
                                .then_inc(pe_n.sem, pe_n.step(f"var2_{j}"))
                    for j in range(GSUB):
                        pe.wait_ge(act_n.sem, act_n.now(g, f"xn_{j}" if two_norms else f"h_{j}"))
                        for q in range(SUB // 128):
                            mm = pe.matmul(pa[j][:, q * NE:(q + 1) * NE], A[j][:, q * 128:(q + 1) * 128], wg,
                                           start=True, stop=True)
                        mm.then_inc(pe_n.sem, pe_n.step(f"lg_{j}"))

            @block.scalar
            def _(act):
                act.sem_inc(act_n.sem, act_n.per)
                act.preload_act_table_set("natural_log_exp_and_others")
                act.wait_ge(loaded, 16)
                with act.Fori(0, NG) as g:
                    def square(n, j, ready):
                        act.wait_ge(dve_n.sem, dve_n.now(g, f"{ready}_{j}"))
                        act.activation(B[j][:, :], A[j][:, :], ACT.Square)\
                            .then_inc(act_n.sem, act_n.step(f"sq{n}_{j}"))

                    def rstd(n):
                        for j in range(GSUB):
                            act.wait_ge(pe_n.sem, pe_n.now(g, f"var{n}_{j}"))
                            act.activation(B[j][:, :], pb[j][:, :], ACT.Ln, bias=eps[:, 0:1])\
                                .then_inc(act_n.sem, act_n.step(f"ln{n}_{j}"))
                        for j in range(GSUB):
                            act.wait_ge(act_n.sem, act_n.now(g, f"ln{n}_{j}"))
                            act.activation(B[j][:, :], B[j][:, :], ACT.Exp, scale=-0.5)\
                                .then_inc(act_n.sem, act_n.step(f"rs{n}_{j}"))

                    for j in range(GSUB):
                        square(1, j, "xc")
                    rstd(1)
                    for j in range(GSUB):
                        act.wait_ge(dve_n.sem, dve_n.now(g, f"xh_{j}"))
                        for q in range(QS):
                            s = g * (GSUB * QS) + j * QS + q
                            dst = (H if two_norms else A)[j][:, q * SEQ:(q + 1) * SEQ]
                            a = act.activation(dst, A[j][:, q * SEQ:(q + 1) * SEQ], ACT.Identity,
                                               scale=mod[:, layer, CB, bass.ds(s, 1)],
                                               bias=mod[:, layer, SB, bass.ds(s, 1)])
                        a.then_inc(act_n.sem, act_n.step(f"h_{j}"))
                    if two_norms:
                        for j in range(GSUB):
                            square(2, j, "hc")
                        rstd(2)
                        for j in range(GSUB):
                            act.wait_ge(dve_n.sem, dve_n.now(g, f"hn_{j}"))
                            act.activation(A[j][:, :], A[j][:, :], ACT.Identity, scale=fv[:, F_GAM:F_GAM + 1],
                                           bias=fv[:, F_BET:F_BET + 1])\
                                .then_inc(act_n.sem, act_n.step(f"xn_{j}"))
                act.wait_ge(dve_g.sem, dve_g.at0("shift"))
                act.activation(t3[0][:, :, :], t3[0][:, :, :], ACT.Exp).then_inc(act_g.sem, act_g.step("exp"))

            @block.gpsimd
            def _(pool):
                pool.sem_inc(pool_n.sem, pool_n.per)
                with pool.Fori(0, NG) as g:
                    for j in range(GSUB):
                        pool.wait_ge(act_n.sem, act_n.now(g, f"xn_{j}" if two_norms else f"h_{j}"))
                        pool.tensor_copy(xn_f[:, at(g, j)], A[j][:, :]).then_inc(pool_n.sem, pool_n.step(f"keep_{j}"))

            @block.vector
            def _(dve):
                dve.sem_inc(dve_n.sem, dve_n.per)
                dve.wait_ge(loaded, 16)
                with dve.Fori(0, NG) as g:
                    for j in range(GSUB):
                        dve.wait_ge(pe_n.sem, pe_n.now(g, f"mean1_{j}"))
                        dve.wait_ge(pool_n.sem, pool_n.before(g, f"keep_{j}"))
                        dve.tensor_tensor(A[j][:, :], x_f[:, at(g, j)], pa[j][:, :], ALU.subtract)\
                            .then_inc(dve_n.sem, dve_n.step(f"xc_{j}"))
                    for j in range(GSUB):
                        dve.wait_ge(act_n.sem, act_n.now(g, f"rs1_{j}"))
                        dve.tensor_tensor(A[j][:, :], A[j][:, :], B[j][:, :], ALU.mult)\
                            .then_inc(dve_n.sem, dve_n.step(f"xh_{j}"))
                    if two_norms:
                        for j in range(GSUB):
                            dve.wait_ge(act_n.sem, act_n.now(g, f"h_{j}"))
                            for q in range(QS):
                                s = g * (GSUB * QS) + j * QS + q
                                xq = x_f[:, at(g, j, SEQ, q * SEQ)]
                                v = dve.scalar_tensor_tensor(xq, H[j][:, q * SEQ:(q + 1) * SEQ],
                                                             mod[:, layer, GB, bass.ds(s, 1)], xq,
                                                             ALU.mult, ALU.add)
                            v.then_inc(dve_n.sem, dve_n.step(f"xg_{j}"))
                        for j in range(GSUB):
                            dve.wait_ge(pe_n.sem, pe_n.now(g, f"mean2_{j}"))
                            dve.tensor_tensor(A[j][:, :], H[j][:, :], pa[j][:, :], ALU.subtract)\
                                .then_inc(dve_n.sem, dve_n.step(f"hc_{j}"))
                        for j in range(GSUB):
                            dve.wait_ge(act_n.sem, act_n.now(g, f"rs2_{j}"))
                            dve.tensor_tensor(A[j][:, :], A[j][:, :], B[j][:, :], ALU.mult)\
                                .then_inc(dve_n.sem, dve_n.step(f"hn_{j}"))
                    for j in range(GSUB):
                        dve.wait_ge(pe_n.sem, pe_n.now(g, f"lg_{j}"))
                        nq = SUB // 128
                        dve.tensor_tensor(lg[:, bass.ds(g * (GSUB * nq) + j * nq, nq), :],
                                          pa[j][:, 0:nq * NE].rearrange("p (q e) -> p q e", e=NE),
                                          gbias.rearrange("p (q e) -> p q e", q=1).to_broadcast([128, nq, NE]),
                                          ALU.add).then_inc(dve_n.sem, dve_n.step(f"lc_{j}"))

                def wide(t):
                    return t[:, :, :].to_broadcast([128, NT, NE])

                def do(name, ins):
                    ins.then_inc(dve_g.sem, dve_g.step(name))
                    dve.wait_ge(dve_g.sem, dve_g.at0(name))

                dve.wait_ge(dve_n.sem, (NG + 1) * dve_n.per)
                P, Q, O = t3
                do("max0", dve.tensor_reduce(t1[0][:, :, 0], lg[:, :, :], AX.X, ALU.max))
                do("shift", dve.tensor_tensor(P[:, :, :], lg[:, :, :], wide(t1[0]), ALU.subtract))
                dve.wait_ge(act_g.sem, 1)
                do("sum", dve.tensor_reduce(t1[0][:, :, 0], P[:, :, :], AX.X, ALU.add))
                do("inv", dve.reciprocal(t1[0][:, :, :], t1[0][:, :, :]))
                do("prob", dve.tensor_tensor(P[:, :, :], P[:, :, :], wide(t1[0]), ALU.mult))
                rank = fv[:, F_RANK:F_RANK + NE].rearrange("p (q e) -> p q e", q=1).to_broadcast([128, NT, NE])
                for n, one in ((1, O), (2, lg)):
                    m = t1[n]
                    do(f"max{n}", dve.tensor_reduce(m[:, :, 0], P[:, :, :], AX.X, ALU.max))
                    do(f"is{n}", dve.tensor_tensor(Q[:, :, :], P[:, :, :], wide(m), ALU.is_equal))
                    do(f"rank{n}", dve.tensor_tensor(Q[:, :, :], Q[:, :, :], rank, ALU.mult))
                    do(f"first{n}", dve.tensor_reduce(t1[3][:, :, 0], Q[:, :, :], AX.X, ALU.max))
                    do(f"one{n}", dve.tensor_tensor(one[:, :, :], Q[:, :, :], wide(t1[3]), ALU.is_equal))
                    if n == 1:
                        do("mask", dve.scalar_tensor_tensor(P[:, :, :], O[:, :, :], -2.0, P[:, :, :],
                                                            ALU.mult, ALU.add))
                do("den", dve.tensor_tensor(t1[0][:, :, :], t1[1][:, :, :], t1[2][:, :, :], ALU.add))
                do("den1", dve.tensor_scalar(t1[0][:, :, :], t1[0][:, :, :], 1e-9 if layer == 0 else 0.0, None,
                                             ALU.add))
                do("inv2", dve.reciprocal(t1[0][:, :, :], t1[0][:, :, :]))
                do("g1", dve.tensor_tensor(t1[1][:, :, :], t1[1][:, :, :], t1[0][:, :, :], ALU.mult))
                do("g2", dve.tensor_tensor(t1[2][:, :, :], t1[2][:, :, :], t1[0][:, :, :], ALU.mult))
                do("w1", dve.tensor_tensor(O[:, :, :], O[:, :, :], wide(t1[1]), ALU.mult))
                do("w2", dve.tensor_tensor(lg[:, :, :], lg[:, :, :], wide(t1[2]), ALU.mult))
                do("gate", dve.tensor_tensor(gate[:, :, :], O[:, :, :], lg[:, :, :], ALU.add))

        experts(nc, kept, layer, L, sem, xn_f, W1, W2, b2b, fv, gate, loaded_w, out)


GATE_DVE = (["max0", "shift", "sum", "inv", "prob"] + [f"{n}1" for n in ("max", "is", "rank", "first", "one")]
            + ["mask"] + [f"{n}2" for n in ("max", "is", "rank", "first", "one")]
            + ["den", "den1", "inv2", "g1", "g2", "w1", "w2", "gate"])


def experts(nc, kept, layer, L, sem, xn_f, W1, W2, b2b, fv, gate, loaded_w, out):
    NX = TOK // SUB
    x_f, mod, ident = kept.x_f, kept.mod, kept.ident
    b1 = fv[:, layer * F_PER + F_B1:layer * F_PER + F_B1 + NE * NF]
    gelu = ACT.Gelu_apprx_tanh if layer == 0 else ACT.Gelu
    NB = SUB // 128
    with ExitStack() as ctx:
        hT = [[ctx.enter_context(nc.sbuf_tensor(f"{L}hT{i}{f}", [128, SUB], F32)) for f in range(NF)]
              for i in range(2)]
        tmp = [ctx.enter_context(nc.sbuf_tensor(f"{L}tmp{i}", [128, NB, D], F32)) for i in range(2)]
        acc = ctx.enter_context(nc.sbuf_tensor(L + "acc", [128, NB, D], F32))
        pu = [ctx.enter_context(nc.psum_tensor(f"{L}pu{f}", [128, SUB], F32)) for f in range(NF)]
        pd = [ctx.enter_context(nc.psum_tensor(f"{L}pd{i}", [128, NB, D], F32)) for i in range(2)]
        pt = ctx.enter_context(nc.psum_tensor(L + "pt", [128, SUB], F32))
        pe_names = []
        for e in range(NE):
            pe_names += [f"up{e}_{f}" for f in range(NF)] + ([f"down{e - 1}"] if e else [])
        pe_x = Steps(sem("pe_x"), pe_names + [f"down{NE - 1}", "back"])
        act_x = Steps(sem("act_x"), [f"g{e}_{f}" for e in range(NE) for f in range(NF)])
        dve_x = Steps(sem("dve_x"), [f"{k}{e}" for e in range(NE) for k in ("b", "a")] + ["x"])
        stored = sem("stored")
        block = ctx.enter_context(nc.Block())

        @block.sync
        def _(sp):
            if out is not None:
                sp.wait_ge(dve_x.sem, (NX + 1) * dve_x.per)
                sp.dma_start(out, x_f[:, :]).then_inc(stored, 16)
                sp.wait_ge(stored, 16)

        @block.tensor
        def _(pe):
            pe.sem_inc(pe_x.sem, pe_x.per)
            pe.wait_ge(loaded_w, 48)
            with pe.Fori(0, NX) as c:
                def down(e):
                    pe.wait_ge(act_x.sem, act_x.now(c, f"g{e}_{NF - 1}"))
                    pe.wait_ge(dve_x.sem, dve_x.now(c, f"b{e - 2}") if e >= 2 else dve_x.before(c, f"b{NE - 2 + e}"))
                    for q in range(NB):
                        for f in range(NF):
                            mm = pe.matmul(pd[e % 2][:, q, :], hT[e % 2][f][:, q * 128:(q + 1) * 128],
                                           W2[:, (e * NF + f) * D:(e * NF + f + 1) * D],
                                           start=f == 0, stop=f == NF - 1)
                    mm.then_inc(pe_x.sem, pe_x.step(f"down{e}"))

                for e in range(NE):
                    for f in range(NF):
                        pe.wait_ge(act_x.sem, act_x.now(c, f"g{e - 1}_{f}") if e else
                                   act_x.before(c, f"g{NE - 1}_{f}"))
                        pe.matmul(pu[f][:, :], W1[:, (e * NF + f) * 128:(e * NF + f + 1) * 128],
                                  xn_f[:, bass.ds(c * SUB, SUB)], start=True, stop=True)\
                            .then_inc(pe_x.sem, pe_x.step(f"up{e}_{f}"))
                    if e:
                        down(e - 1)
                down(NE - 1)
                pe.wait_ge(dve_x.sem, dve_x.now(c, f"a{NE - 1}"))
                for q in range(NB):
                    mm = pe.transpose(pt[:, q * 128:(q + 1) * 128], acc[:, q, :], ident)
                mm.then_inc(pe_x.sem, pe_x.step("back"))

        @block.scalar
        def _(act):
            act.sem_inc(act_x.sem, act_x.per)
            with act.Fori(0, NX) as c:
                for e in range(NE):
                    for f in range(NF):
                        act.wait_ge(pe_x.sem, pe_x.now(c, f"up{e}_{f}"))
                        act.wait_ge(pe_x.sem, pe_x.now(c, f"down{e - 2}") if e >= 2 else
                                    pe_x.before(c, f"down{NE - 2 + e}"))
                        act.activation(hT[e % 2][f][:, :], pu[f][:, :], gelu, bias=b1[:, e * NF + f:e * NF + f + 1])\
                            .then_inc(act_x.sem, act_x.step(f"g{e}_{f}"))

        @block.vector
        def _(dve):
            dve.sem_inc(dve_x.sem, dve_x.per)
            dve.wait_ge(loaded_w, 48)
            with dve.Fori(0, NX) as c:
                for e in range(NE):
                    t = tmp[e % 2]
                    dve.wait_ge(pe_x.sem, pe_x.now(c, f"down{e}"))
                    dve.wait_ge(dve_x.sem, dve_x.now(c, f"a{e - 2}") if e >= 2 else dve_x.before(c, f"a{NE - 2 + e}"))
                    bb = b2b[:, e * D:(e + 1) * D].rearrange("p (q d) -> p q d", q=1).to_broadcast([128, NB, D])
                    dve.tensor_tensor(t[:, :, :], pd[e % 2][:, :, :], bb, ALU.add)\
                        .then_inc(dve_x.sem, dve_x.step(f"b{e}"))
                    dve.wait_ge(dve_x.sem, dve_x.now(c, f"b{e}"))
                    if not e:
                        dve.wait_ge(pe_x.sem, pe_x.before(c, "back"))
                    for q in range(NB):
                        g = gate[:, bass.ds(c * NB + q, 1), e]
                        if e:
                            v = dve.scalar_tensor_tensor(acc[:, q, :], t[:, q, :], g, acc[:, q, :],
                                                         ALU.mult, ALU.add)
                        else:
                            v = dve.tensor_scalar(acc[:, q, :], t[:, q, :], g, None, ALU.mult)
                    v.then_inc(dve_x.sem, dve_x.step(f"a{e}"))
                dve.wait_ge(pe_x.sem, pe_x.now(c, "back"))
                for q in range(QS):
                    xq = x_f[:, bass.ds(c * SUB + q * SEQ, SEQ)]
                    v = dve.scalar_tensor_tensor(xq, pt[:, q * SEQ:(q + 1) * SEQ],
                                                 mod[:, layer, GB, bass.ds(c * QS + q, 1)], xq, ALU.mult, ALU.add)
                v.then_inc(dve_x.sem, dve_x.step("x"))


NLOC, DH = 4, 8
LF, GF = NLOC * DH, D - NLOC * DH
BLK = 64
HV = DH + 1
VW = NLOC * HV + GF + 1
PW = 2 * GF + D
(A_QK, A_TOK, A_WOG, A_WOL, A_CAUS, A_HEAD) = (0, D, D + PW, 2 * D + PW, 3 * D + PW, 4 * D + PW)
A_ROWS = A_HEAD + GF
A_END = A_ROWS + NLOC
SCALE = DH ** -0.5


def attention_layer(nc, kept, wat):
    L = "a_"
    with ExitStack() as ctx:
        def sb(name, shape, dt=F32):
            return ctx.enter_context(nc.sbuf_tensor(L + name, shape, dt))

        def sem(name):
            return kept.sem(L + name)

        h_f = sb("h_f", [D, TOK])
        wa = sb("wa", [128, A_END])
        loaded, fixed = sem("loaded"), sem("fixed")
        normalise(nc, kept, 1, L, sem, h_f, SA, CA, lambda sp: sp.dma_start(wa[:, :], wat).then_inc(loaded, 16))
        attend(nc, kept, L, sem, h_f, wa, loaded, fixed)


def normalise(nc, kept, layer, L, sem, h_f, shift, scale, load):
    x_f, mod, eps, avg = kept.x_f, kept.mod, kept.eps, kept.avg
    with ExitStack() as pre:
        A = [pre.enter_context(nc.sbuf_tensor(f"{L}A{j}", [128, SUB], F32)) for j in range(GSUB)]
        B = [pre.enter_context(nc.sbuf_tensor(f"{L}B{j}", [128, SUB], F32)) for j in range(GSUB)]
        pa = [pre.enter_context(nc.psum_tensor(f"{L}pa{j}", [128, SUB], F32)) for j in range(GSUB)]
        pb = [pre.enter_context(nc.psum_tensor(f"{L}pb{j}", [128, SUB], F32)) for j in range(GSUB)]
        names = lambda kinds: [f"{k}{j}" for k in kinds for j in range(GSUB)]
        pe_n = Steps(sem("pe_n"), names(("mean_", "var_")))
        act_n = Steps(sem("act_n"), names(("sq_", "ln_", "rs_", "h_")))
        dve_n = Steps(sem("dve_n"), names(("xc_", "xh_")))
        block = pre.enter_context(nc.Block())

        def at(g, j):
            return bass.ds(g * (GSUB * SUB) + j * SUB, SUB)

        @block.sync
        def _(sp):
            load(sp)

        @block.tensor
        def _(pe):
            pe.sem_inc(pe_n.sem, pe_n.per)
            with pe.Fori(0, NG) as g:
                for j in range(GSUB):
                    pe.wait_ge(dve_n.sem, dve_n.before(g, f"xc_{j}"))
                    pe.matmul(pa[j][:, :], avg, x_f[:, at(g, j)], start=True, stop=True)\
                        .then_inc(pe_n.sem, pe_n.step(f"mean_{j}"))
                for j in range(GSUB):
                    pe.wait_ge(act_n.sem, act_n.now(g, f"sq_{j}"))
                    pe.matmul(pb[j][:, :], avg, B[j][:, :], start=True, stop=True)\
                        .then_inc(pe_n.sem, pe_n.step(f"var_{j}"))

        @block.scalar
        def _(act):
            act.sem_inc(act_n.sem, act_n.per)
            act.preload_act_table_set("natural_log_exp_and_others")
            with act.Fori(0, NG) as g:
                for j in range(GSUB):
                    act.wait_ge(dve_n.sem, dve_n.now(g, f"xc_{j}"))
                    act.activation(B[j][:, :], A[j][:, :], ACT.Square).then_inc(act_n.sem, act_n.step(f"sq_{j}"))
                for j in range(GSUB):
                    act.wait_ge(pe_n.sem, pe_n.now(g, f"var_{j}"))
                    act.activation(B[j][:, :], pb[j][:, :], ACT.Ln, bias=eps[:, 0:1])\
                        .then_inc(act_n.sem, act_n.step(f"ln_{j}"))
                for j in range(GSUB):
                    act.wait_ge(act_n.sem, act_n.now(g, f"ln_{j}"))
                    act.activation(B[j][:, :], B[j][:, :], ACT.Exp, scale=-0.5)\
                        .then_inc(act_n.sem, act_n.step(f"rs_{j}"))
                for j in range(GSUB):
                    act.wait_ge(dve_n.sem, dve_n.now(g, f"xh_{j}"))
                    for q in range(QS):
                        s = g * (GSUB * QS) + j * QS + q
                        a = act.activation(h_f[:, bass.ds(g * (GSUB * SUB) + j * SUB + q * SEQ, SEQ)],
                                           A[j][:, q * SEQ:(q + 1) * SEQ], ACT.Identity,
                                           scale=mod[:, layer, scale, bass.ds(s, 1)],
                                           bias=mod[:, layer, shift, bass.ds(s, 1)])
                    a.then_inc(act_n.sem, act_n.step(f"h_{j}"))

        @block.vector
        def _(dve):
            dve.sem_inc(dve_n.sem, dve_n.per)
            with dve.Fori(0, NG) as g:
                for j in range(GSUB):
                    dve.wait_ge(pe_n.sem, pe_n.now(g, f"mean_{j}"))
                    dve.wait_ge(act_n.sem, act_n.before(g, f"h_{j}"))
                    dve.tensor_tensor(A[j][:, :], x_f[:, at(g, j)], pa[j][:, :], ALU.subtract)\
                        .then_inc(dve_n.sem, dve_n.step(f"xc_{j}"))
                for j in range(GSUB):
                    dve.wait_ge(act_n.sem, act_n.now(g, f"rs_{j}"))
                    dve.tensor_tensor(A[j][:, :], A[j][:, :], B[j][:, :], ALU.mult)\
                        .then_inc(dve_n.sem, dve_n.step(f"xh_{j}"))


def attend(nc, kept, L, sem, h_f, wa, loaded, fixed):
    x_f, mod, ident = kept.x_f, kept.mod, kept.ident
    NP = NSEQ // 2
    BF = mybir.dt.bfloat16
    wqk = wa[:, A_QK:A_QK + 2 * LF]
    wtok = wa[:, A_TOK:A_TOK + PW]
    wog, wol = wa[0:GF, A_WOG:A_WOG + D], wa[0:LF + 1, A_WOL:A_WOL + D]
    caus, same = wa[:, A_CAUS:A_CAUS + 128], wa[0:GF, A_HEAD:A_HEAD + GF]
    with ExitStack() as ctx:
        def sb(name, shape, dt=F32):
            return ctx.enter_context(nc.sbuf_tensor(L + name, shape, dt))

        def two(name, shape):
            return [sb(f"{name}{p}", shape) for p in range(2)]

        idb, mask0, mask1 = sb("idb", [128, 128], BF), sb("mask0", [128, 4, 128], BF), sb("mask1", [128, 2, 256], BF)
        hs = two("hs", [128, SEQ])
        qk = two("qk", [LF, SEQ])
        kd = two("kd", [LF, NLOC, SEQ])
        tk = two("tk", [128, 2, 2 * GF])
        va = two("va", [128, 2, VW])
        qe, qm = two("qe", [128, 2, 12, DH]), two("qm", [128, 2, 12])
        kk, km = two("kk", [128, 2, GF]), two("km", [128, 2, GF])
        mx = two("mx", [128, 2, NLOC])
        P0, P1 = two("P0", [128, NLOC, 128]), two("P1", [128, NLOC, 256])
        pt = two("pt", [128, 3, NLOC, 128])
        kr, cn = two("kr", [GF, 3, 1]), two("cn", [GF, 3, GF])
        qT, og = two("qT", [GF, SEQ]), two("og", [GF, SEQ])
        rs, ol, olT = two("rs", [128, 2, NLOC, 1]), two("ol", [128, 2, NLOC, DH]), two("olT", [LF + 1, SEQ])
        S0 = [ctx.enter_context(nc.psum_tensor(f"{L}S0{p}", [128, 512], F32)) for p in range(2)]
        S1 = [ctx.enter_context(nc.psum_tensor(f"{L}S1{p}", [128, 2, 512], F32)) for p in range(2)]
        X = [ctx.enter_context(nc.psum_tensor(f"{L}X{p}", [128, 512], F32)) for p in range(2)]
        CW = GF + 1
        both = lambda kinds: [f"{k}{p}" for k in kinds for p in range(2)]
        pe_s = Steps(sem("pe_s"), both(("proj", "S", "ctx", "qT", "PT", "og", "pv", "olT", "wo")))
        act_s = Steps(sem("act_s"), [f"{k}{p}" for p in range(2) for k in ("tk", "qk", "vl", "vg")]
                      + both(("kex", "qex", "sexp", "pt", "og")))
        dve_s = Steps(sem("dve_s"), both(("kd", "kmn")) + [f"{k}{p}" for p in range(2) for k in ("qmx", "qsh")]
                      + both(("kk", "smx", "smn", "qsm", "qrc", "qn", "kr", "krc", "cn", "qT", "pt", "rrc", "ol", "olT",
                              "x")))

        pool_s = Steps(sem("pool_s"), both(("hs",)))
        made, MADE = sem("made"), 6
        block = ctx.enter_context(nc.Block())

        @block.tensor
        def _(pe):
            pe.wait_ge(made, MADE)
            pe.sem_inc(pe_s.sem, pe_s.per)
            pe.wait_ge(loaded, 16)
            pe.wait_ge(fixed, 3)
            with pe.Fori(0, NP) as i:
                for p in range(2):
                    pe.wait_ge(pool_s.sem, pool_s.now(i, f"hs{p}"))
                    pe.wait_ge(dve_s.sem, dve_s.before(i, f"x{p}"))
                    pe.matmul(S0[p][0:2 * LF, 0:SEQ], wqk, hs[p][:, :], start=True, stop=True)
                    for t in range(2):
                        mm = pe.matmul(S1[p][:, t, 0:PW], hs[p][:, t * 128:(t + 1) * 128], wtok, start=True, stop=True)
                    mm.then_inc(pe_s.sem, pe_s.step(f"proj{p}"))
                for p in range(2):
                    pe.wait_ge(act_s.sem, act_s.now(i, f"vg{p}"))
                    pe.wait_ge(dve_s.sem, dve_s.now(i, f"kd{p}"))
                    pe.matmul(S0[p][:, :], idb[:, :], mask0[:, :, :].rearrange("p a b -> p (a b)"), start=True,
                              stop=False)
                    for b in range(2):
                        pe.matmul(S1[p][:, b, :], idb[:, :], mask1[:, :, :].rearrange("p a b -> p (a b)"),
                                  start=True, stop=False)
                    pe.matmul(S0[p][:, :], qk[p][:, 0:128], kd[p][:, :, 0:128], start=False, stop=True)
                    for b in range(2):
                        mm = pe.matmul(S1[p][:, b, :], qk[p][:, 128:256],
                                       kd[p][:, 2 * b:2 * b + 2, :].rearrange("p a b -> p (a b)"),
                                       start=False, stop=True)
                    mm.then_inc(pe_s.sem, pe_s.step(f"S{p}"))
                for p in range(2):
                    pe.wait_ge(dve_s.sem, dve_s.now(i, f"kk{p}"))
                    pe.wait_ge(act_s.sem, act_s.before(i, f"og{p}"))
                    g = slice(NLOC * HV, VW)
                    pe.matmul(X[p][0:GF, 0:CW], kk[p][0:BLK, 0, :], va[p][0:BLK, 0, g], start=True, stop=True)
                    pe.matmul(X[p][0:GF, CW:2 * CW], kk[p][:, 0, :], va[p][:, 0, g], start=True, stop=True)
                    pe.matmul(X[p][0:GF, 2 * CW:3 * CW], kk[p][:, 0, :], va[p][:, 0, g], start=True, stop=False)
                    pe.matmul(X[p][0:GF, 2 * CW:3 * CW], kk[p][0:BLK, 1, :], va[p][0:BLK, 1, g], start=False,
                              stop=True).then_inc(pe_s.sem, pe_s.step(f"ctx{p}"))
                for p in range(2):
                    pe.wait_ge(dve_s.sem, dve_s.now(i, f"cn{p}"))
                    for t in range(2):
                        mm = pe.transpose(X[p][0:GF, t * 128:(t + 1) * 128],
                                          qe[p][:, t, :, :].rearrange("p h x -> p (h x)"), ident)
                    mm.then_inc(pe_s.sem, pe_s.step(f"qT{p}"))
                for p in range(2):
                    pe.wait_ge(act_s.sem, act_s.now(i, f"sexp{p}"))
                    for h in range(NLOC):
                        o = slice(h * 128, (h + 1) * 128)
                        pe.transpose(S0[p][:, o], P0[p][:, h, :], ident)
                        pe.transpose(S1[p][:, 0, o], P1[p][:, h, 0:128], ident)
                        mm = pe.transpose(S1[p][:, 1, o], P1[p][:, h, 128:256], ident)
                    mm.then_inc(pe_s.sem, pe_s.step(f"PT{p}"))
                for p in range(2):
                    pe.wait_ge(dve_s.sem, dve_s.now(i, f"qT{p}"))
                    for b in range(1, SEQ // BLK):
                        mm = pe.matmul(X[p][0:GF, b * BLK:(b + 1) * BLK], cn[p][:, b - 1, :],
                                       qT[p][:, b * BLK:(b + 1) * BLK], start=True, stop=True)
                    mm.then_inc(pe_s.sem, pe_s.step(f"og{p}"))
                for p in range(2):
                    pe.wait_ge(act_s.sem, act_s.now(i, f"pt{p}"))
                    pe.wait_ge(dve_s.sem, dve_s.now(i, f"pt{p}"))
                    for h in range(NLOC):
                        v = slice(h * HV, (h + 1) * HV)
                        pe.matmul(S0[p][:, h * HV:(h + 1) * HV], pt[p][:, 0, h, :], va[p][:, 0, v],
                                  start=True, stop=True)
                        o = slice((NLOC + h) * HV, (NLOC + h + 1) * HV)
                        pe.matmul(S0[p][:, o], pt[p][:, 1, h, :], va[p][:, 0, v], start=True, stop=False)
                        mm = pe.matmul(S0[p][:, o], pt[p][:, 2, h, :], va[p][:, 1, v], start=False, stop=True)
                    mm.then_inc(pe_s.sem, pe_s.step(f"pv{p}"))
                for p in range(2):
                    pe.wait_ge(dve_s.sem, dve_s.now(i, f"ol{p}"))
                    for t in range(2):
                        mm = pe.transpose(S0[p][0:LF, t * 128:(t + 1) * 128],
                                          ol[p][:, t, :, :].rearrange("p h x -> p (h x)"), ident)
                    mm.then_inc(pe_s.sem, pe_s.step(f"olT{p}"))
                for p in range(2):
                    pe.wait_ge(dve_s.sem, dve_s.now(i, f"olT{p}"))
                    pe.wait_ge(act_s.sem, act_s.now(i, f"og{p}"))
                    o = S0[p][:, SEQ:2 * SEQ]
                    pe.matmul(o, wog, og[p][:, :], start=True, stop=False)
                    pe.matmul(o, wol, olT[p][:, :], start=False, stop=True).then_inc(pe_s.sem, pe_s.step(f"wo{p}"))

        @block.scalar
        def _(act):
            act.sem_inc(act_s.sem, act_s.per)
            act.preload_act_table_set("natural_log_exp_and_others")
            act.wait_ge(made, MADE)
            with act.Fori(0, NP) as i:
                for p in range(2):
                    act.wait_ge(pe_s.sem, pe_s.now(i, f"proj{p}"))
                    act.wait_ge(dve_s.sem, dve_s.before(i, f"kk{p}"))
                    act.wait_ge(pe_s.sem, pe_s.before(i, f"pv{p}"))
                    act.activation(tk[p][:, :, :], S1[p][:, :, 0:2 * GF], ACT.Copy)\
                        .then_inc(act_s.sem, act_s.step(f"tk{p}"))
                    act.wait_ge(dve_s.sem, dve_s.now(i, f"kd{p}"))
                    act.activation(qk[p][:, :], S0[p][0:LF, 0:SEQ], ACT.Copy)\
                        .then_inc(act_s.sem, act_s.step(f"qk{p}"))
                    vl = va[p][:, :, 0:NLOC * HV].rearrange("p t (h x) -> p t h x", x=HV)[:, :, :, 0:DH]
                    act.activation(vl, S1[p][:, :, 2 * GF:2 * GF + LF].rearrange("p t (h x) -> p t h x", x=DH),
                                   ACT.Copy).then_inc(act_s.sem, act_s.step(f"vl{p}"))
                    act.activation(va[p][:, :, NLOC * HV:VW - 1], S1[p][:, :, 2 * GF + LF:PW], ACT.Copy)\
                        .then_inc(act_s.sem, act_s.step(f"vg{p}"))
                for p in range(2):
                    act.wait_ge(dve_s.sem, dve_s.now(i, f"kmn{p}"))
                    act.activation(km[p][:, :, :], km[p][:, :, :], ACT.Exp).then_inc(act_s.sem, act_s.step(f"kex{p}"))
                for p in range(2):
                    act.wait_ge(dve_s.sem, dve_s.now(i, f"qsh{p}"))
                    act.activation(qe[p][:, :, :, :], qe[p][:, :, :, :], ACT.Exp)\
                        .then_inc(act_s.sem, act_s.step(f"qex{p}"))
                for p in range(2):
                    act.wait_ge(dve_s.sem, dve_s.now(i, f"smn{p}"))
                    for h in range(NLOC):
                        act.activation(P0[p][:, h, :], S0[p][:, h * 128:(h + 1) * 128], ACT.Exp, scale=SCALE,
                                       bias=mx[p][:, 0, h:h + 1])
                    for h in range(NLOC):
                        a = act.activation(P1[p][:, h, :], S1[p][:, h // 2, (h % 2) * 256:(h % 2 + 1) * 256], ACT.Exp,
                                           scale=SCALE, bias=mx[p][:, 1, h:h + 1])
                    a.then_inc(act_s.sem, act_s.step(f"sexp{p}"))
                for p in range(2):
                    act.wait_ge(pe_s.sem, pe_s.now(i, f"PT{p}"))
                    for b in range(2):
                        a = act.activation(pt[p][:, b, :, :].rearrange("p h q -> p (h q)"),
                                           S0[p][:, :] if b == 0 else S1[p][:, 0, :], ACT.Copy)
                    a.then_inc(act_s.sem, act_s.step(f"pt{p}"))
                for p in range(2):
                    act.wait_ge(pe_s.sem, pe_s.now(i, f"og{p}"))
                    act.wait_ge(pe_s.sem, pe_s.before(i, f"wo{p}"))
                    act.activation(og[p][:, BLK:SEQ], X[p][0:GF, BLK:SEQ], ACT.Copy)\
                        .then_inc(act_s.sem, act_s.step(f"og{p}"))

        @block.gpsimd
        def _(pool):
            n = 0
            for p in range(2):
                for t, v in ((va[p][:, :, :], 1.0), (og[p][:, 0:BLK], 0.0), (olT[p][LF:LF + 1, :], 1.0)):
                    pool.memset(t, v).then_inc(made, 1)
                    n += 1
                    pool.wait_ge(made, n)
            pool.sem_inc(pool_s.sem, pool_s.per)
            with pool.Fori(0, NP) as i:
                for p in range(2):
                    pool.wait_ge(pe_s.sem, pe_s.before(i, f"proj{p}"))
                    pool.tensor_copy(hs[p][:, :], h_f[:, bass.ds((i * 2 + p) * SEQ, SEQ)])\
                        .then_inc(pool_s.sem, pool_s.step(f"hs{p}"))

        @block.vector
        def _(dve):
            dve.sem_inc(dve_s.sem, dve_s.per)
            dve.wait_ge(loaded, 16)
            dve.wait_ge(made, MADE)
            dve.tensor_copy(idb[:, :], ident).then_inc(fixed, 1)
            dve.tensor_copy(mask0[:, :, :],
                            caus.rearrange("p (a b) -> p a b", a=1).to_broadcast([128, NLOC, 128]))\
                .then_inc(fixed, 1)
            dve.memset(mask1[:, :, 0:128], 0.0)
            dve.tensor_copy(mask1[:, :, 128:256],
                            caus.rearrange("p (a b) -> p a b", a=1).to_broadcast([128, 2, 128])).then_inc(fixed, 1)
            with dve.Fori(0, NP) as i:
                def tok(p, at, n):
                    return tk[p][:, :, at:at + n]

                def heads(t):
                    return t.rearrange("p t (h x) -> p t h x", x=DH)

                def wide(t, n):
                    return t.rearrange("p t (h x) -> p t h x", x=1).to_broadcast([128, 2, 12, n])

                def done(name, ins):
                    ins.then_inc(dve_s.sem, dve_s.step(name))

                def after(name):
                    dve.wait_ge(dve_s.sem, dve_s.now(i, name))

                for p in range(2):
                    dve.wait_ge(pe_s.sem, pe_s.now(i, f"proj{p}"))
                    done(f"kd{p}", dve.tensor_tensor(
                        kd[p][:, :, :],
                        S0[p][LF:2 * LF, 0:SEQ].rearrange("p (a t) -> p a t", a=1).to_broadcast([LF, NLOC, SEQ]),
                        wa[LF:2 * LF, A_ROWS:A_ROWS + NLOC].rearrange("p (a t) -> p a t", t=1)
                        .to_broadcast([LF, NLOC, SEQ]), ALU.mult))
                for p in range(2):
                    dve.wait_ge(act_s.sem, act_s.now(i, f"tk{p}"))
                    done(f"kmn{p}", dve.tensor_scalar(km[p][:, :, :], tok(p, GF, GF), 0.0, None, ALU.min))
                for p in range(2):
                    done(f"qmx{p}", dve.tensor_reduce(qm[p][:, :, :], heads(tok(p, 0, GF)), AX.X, ALU.max))
                    after(f"qmx{p}")
                    done(f"qsh{p}", dve.tensor_tensor(qe[p][:, :, :, :], heads(tok(p, 0, GF)),
                                                      wide(qm[p][:, :, :], DH), ALU.subtract))
                for p in range(2):
                    dve.wait_ge(act_s.sem, act_s.now(i, f"kex{p}"))
                    done(f"kk{p}", dve.scalar_tensor_tensor(kk[p][:, :, :], tok(p, GF, GF), 0.0, km[p][:, :, :],
                                                            ALU.max, ALU.add))
                for p in range(2):
                    dve.wait_ge(pe_s.sem, pe_s.now(i, f"S{p}"))
                    dve.tensor_reduce(mx[p][:, 0, :], S0[p][:, :].rearrange("p (h k) -> p h k", h=NLOC), AX.X,
                                      ALU.max)
                    done(f"smx{p}", dve.tensor_reduce(
                        mx[p][:, 1, :], S1[p][:, :, :].rearrange("p b (h k) -> p (b h) k", h=2), AX.X, ALU.max))
                for p in range(2):
                    after(f"smx{p}")
                    done(f"smn{p}", dve.tensor_scalar(mx[p][:, :, :], mx[p][:, :, :], -SCALE, None, ALU.mult))
                for p in range(2):
                    dve.wait_ge(act_s.sem, act_s.now(i, f"qex{p}"))
                    done(f"qsm{p}", dve.tensor_reduce(qm[p][:, :, :], qe[p][:, :, :, :], AX.X, ALU.add))
                for p in range(2):
                    after(f"qsm{p}")
                    done(f"qrc{p}", dve.reciprocal(qm[p][:, :, :], qm[p][:, :, :]))
                for p in range(2):
                    after(f"qrc{p}")
                    done(f"qn{p}", dve.tensor_tensor(qe[p][:, :, :, :], qe[p][:, :, :, :], wide(qm[p][:, :, :], DH),
                                                     ALU.mult))
                for p in range(2):
                    dve.wait_ge(pe_s.sem, pe_s.now(i, f"ctx{p}"))
                    c = X[p][0:GF, 0:3 * CW].rearrange("p (b e) -> p b e", e=CW)
                    done(f"kr{p}", dve.tensor_scalar(kr[p][:, :, :], c[:, :, GF:CW], 1e-6, None, ALU.add))
                for p in range(2):
                    after(f"kr{p}")
                    done(f"krc{p}", dve.reciprocal(kr[p][:, :, :], kr[p][:, :, :]))
                for p in range(2):
                    after(f"krc{p}")
                    for b in range(3):
                        v = dve.scalar_tensor_tensor(cn[p][:, b, :], X[p][0:GF, b * CW:b * CW + GF],
                                                     kr[p][:, b, :], same, ALU.mult, ALU.mult)
                    done(f"cn{p}", v)
                for p in range(2):
                    dve.wait_ge(pe_s.sem, pe_s.now(i, f"qT{p}"))
                    done(f"qT{p}", dve.tensor_copy(qT[p][:, :], X[p][0:GF, 0:SEQ]))
                for p in range(2):
                    dve.wait_ge(pe_s.sem, pe_s.now(i, f"PT{p}"))
                    done(f"pt{p}", dve.tensor_copy(pt[p][:, 2, :, :].rearrange("p h q -> p (h q)"), S1[p][:, 1, :]))
                for p in range(2):
                    dve.wait_ge(pe_s.sem, pe_s.now(i, f"pv{p}"))
                    o = S0[p][:, 0:2 * NLOC * HV].rearrange("p (t h x) -> p t h x", t=2, x=HV)
                    done(f"rrc{p}", dve.reciprocal(rs[p][:, :, :, :], o[:, :, :, DH:HV]))
                for p in range(2):
                    o = S0[p][:, 0:2 * NLOC * HV].rearrange("p (t h x) -> p t h x", t=2, x=HV)
                    after(f"rrc{p}")
                    done(f"ol{p}", dve.tensor_tensor(ol[p][:, :, :, :], o[:, :, :, 0:DH],
                                                     rs[p][:, :, :, :].to_broadcast([128, 2, NLOC, DH]), ALU.mult))
                for p in range(2):
                    dve.wait_ge(pe_s.sem, pe_s.now(i, f"olT{p}"))
                    done(f"olT{p}", dve.tensor_copy(olT[p][0:LF, :], S0[p][0:LF, 0:SEQ]))
                for p in range(2):
                    dve.wait_ge(pe_s.sem, pe_s.now(i, f"wo{p}"))
                    xq = x_f[:, bass.ds((i * 2 + p) * SEQ, SEQ)]
                    done(f"x{p}", dve.scalar_tensor_tensor(xq, S0[p][:, SEQ:2 * SEQ],
                                                           mod[:, 1, GA, bass.ds(i * 2 + p, 1)], xq,
                                                           ALU.mult, ALU.add))


def pack(i):
    f = {k: np.asarray(v) for k, v in i.items()}
    xT = np.ascontiguousarray(f["L0_attn_inputs"].reshape(TOK, D).T)
    eye = np.eye(128, dtype=np.float32)
    sel = np.zeros((128, 32), np.float32)
    sel[64:96], sel[96:128] = np.eye(32), np.eye(32)
    consts = np.concatenate([eye, np.full((128, 128), 1 / 128, np.float32), sel], axis=1)

    def pad(v):
        return np.concatenate([v, np.zeros(128 - len(v), np.float32)]) if len(v) < 128 else v

    a = "L0_attn_"
    cols = [f[a + n] for n in ("gamma", "beta", "b_proj", "b_fc", "b_bc", "b_dt1", "b_dt2", "D1", "D2")]
    cols += [pad(f[a + "b_x1"]), pad(f[a + "b_x2"])]
    vec = np.concatenate([np.stack(cols, 1), f[a + "A_log1"], f[a + "A_log2"], f["L0_c"].T, f["L1_c"].T], axis=1)
    wpk = np.concatenate([f[a + n] for n in ("W_proj", "W_fc", "W_bc", "W_x1", "W_x2")], axis=1)
    wdt = np.concatenate([f[a + "W_dt1"], f[a + "W_dt2"]], axis=1)
    wmod = np.stack([f["L0_wmod"], f["L1_wmod"]], 1)
    m0 = {"wg": f["L0_ffn_Wg"].T, "gb": np.zeros((128, NE), np.float32), "b1": f["L0_ffn_b1"], "w1": f["L0_ffn_W1"],
          "w2": f["L0_ffn_W2"], "b2": f["L0_ffn_b2"]}
    m1 = {"wg": f["L1_ffn_gate_w"], "gb": np.tile(f["L1_ffn_gate_b"], (128, 1)), "b1": f["L1_ffn_b1"],
          "w1": f["L1_ffn_w1"], "w2": f["L1_ffn_w2"], "b2": f["L1_ffn_b2"]}
    fcols = []
    for m in (m0, m1):
        fcols += [m["wg"], m["gb"], m["b1"].reshape(NE, NF, 128).transpose(2, 0, 1).reshape(128, NE * NF)]
    fcols += [f["L0_ffn_gamma"][:, None], f["L0_ffn_beta"][:, None],
              np.tile(np.arange(NE, 0, -1, dtype=np.float32), (128, 1))]
    packed = {"xT": xT, "consts": consts, "vec": vec, "wpk": wpk, "wdt": wdt, "wmod": wmod,
              "fvec": np.concatenate(fcols, axis=1)}
    for l, m in enumerate((m0, m1)):
        packed[f"w1_{l}"] = m["w1"].transpose(1, 0, 2).reshape(D, NE * NF * 128)
        packed[f"w2_{l}"] = m["w2"].reshape(NE, NF, 128, D).transpose(2, 0, 1, 3).reshape(128, NE * NF * D)
        packed[f"b2_{l}"] = np.tile(m["b2"].reshape(1, NE * D), (128, 1))
    wq, wk, wv, wo = (f["L1_attn_" + n] for n in ("Wq", "Wk", "Wv", "Wo"))
    wat = np.zeros((128, A_END), np.float32)
    wat[:, A_QK:A_QK + LF], wat[:, A_QK + LF:A_QK + 2 * LF] = wq[:, :LF], wk[:, :LF]
    wat[LF:2 * LF, A_ROWS:A_ROWS + NLOC] = np.kron(np.eye(NLOC), np.ones((DH, 1)))
    wat[:, A_TOK:A_TOK + PW] = np.concatenate([wq[:, LF:], wk[:, LF:], wv], axis=1)
    wat[0:GF, A_WOG:A_WOG + D] = wo[LF:]
    wat[0:LF, A_WOL:A_WOL + D] = wo[:LF]
    wat[LF, A_WOL:A_WOL + D] = f["L1_attn_bo"]
    wat[:, A_CAUS:A_CAUS + 128] = np.where(np.tril(np.ones((128, 128), bool)), 0, -3e38)
    wat[0:GF, A_HEAD:A_HEAD + GF] = np.kron(np.eye(12), np.ones((DH, DH)))
    packed["wat"] = wat
    return {k: np.ascontiguousarray(v, dtype=np.float32) for k, v in packed.items()}


_OUT = (D, TOK)


def kernel(**inputs):
    import concourse.bacc as bacc
    from concourse.bass_utils import run_bass_kernel_spmd

    nc = bacc.Bacc("TRN2", target_bir_lowering=False, num_devices=1)
    packed = pack(inputs)
    args = [nc.dram_tensor(k, v.shape, mybir.dt.from_np(v.dtype), kind="ExternalInput").ap()
            for k, v in packed.items()]
    out = nc.dram_tensor("out_0_dram", _OUT, F32, kind="ExternalOutput").ap()
    build(nc, *args, out)
    r = run_bass_kernel_spmd(nc, [packed], core_ids=[0])
    return np.ascontiguousarray(r.results[0]["out_0_dram"].T).reshape(NSEQ, SEQ, D)
```

```python
from contextlib import ExitStack

import numpy as np

import concourse.bass as bass
from concourse import mybir

F32 = mybir.dt.float32
F32R = mybir.dt.float32r
ALU = mybir.AluOpType
ACT = mybir.ActivationFunctionType
AX = mybir.AxisListType

D = 128
NSEQ, SEQ = 32, 256
TOK = NSEQ * SEQ
R, NS = 64, 16
CH = 512
NCH = TOK // CH
SPC = CH // SEQ
HB = 512
SA, CA, GA, SB, CB, GB = range(6)

C_ID, C_AVG, C_SEL = 0, 128, 256
C_END = 288
(V_GAM, V_BET, V_BPROJ, V_BFC, V_BBC, V_BDT1, V_BDT2, V_D1, V_D2, V_BX1, V_BX2) = range(11)
V_ALOG = 11
V_CT = V_ALOG + 2 * NS
V_END = V_CT + 2 * NSEQ
W_PROJ, W_FC, W_BC, W_X1, W_X2 = 0, 128, 256, 384, 480
W_END = 576


class Steps:

    def __init__(self, sem, names):
        self.sem, self.names, self.per, self.at = sem, list(names), len(names), 0
        self.index = {n: i + 1 for i, n in enumerate(self.names)}
        assert len(self.index) == self.per, "two steps of one name"

    def step(self, name):
        assert self.names[self.at % self.per] == name, (self.names[self.at % self.per], name)
        self.at += 1
        return 1

    def now(self, c, name):
        return (c + 1) * self.per + self.index[name]

    def before(self, c, name):
        return c * self.per + self.index[name]

    def at0(self, name):
        return self.index[name]


PE_1 = {"mean1": 6, "var1": 13, "mean2": 19, "var2": 22}
PE_2 = {"proj": 0, "fc": 2, "bc": 4, "x1": 9, "wdt1": 11, "x2": 15, "wdt2": 17}
ACT_1 = {"sq1": 9, "ln1": 15, "rs1": 15, "h0": 17, "h1": 17, "sq2": 22, "ln2": 24, "rs2": 24,
         "xn": 27}
ACT_2 = {"pj": 2, "vu1": 4, "au1": 4, "eu1": 5, "lu1": 5, "vu2": 6, "au2": 6, "eu2": 7, "lu2": 7, "ez": 8, "lz": 10,
         "sz": 10, "dbc1": 11, "vd1": 13, "ad1": 13, "ed1": 14, "ld1": 14, "dbc2": 17, "vd2": 19, "ad2": 19,
         "ed2": 20, "ld2": 20}
DVE_1 = {"xc": 8, "xg0": 20, "xg1": 20, "hc": 21}
DVE_2 = {"mz": 3, "tu1": 6, "tu2": 8, "u1": 9, "u2": 11, "bh1": 12, "bl1": 12, "acc": 13, "td1": 15, "d1": 17, "bh2": 18,
         "bl2": 18, "td2": 21, "d2": 24}
POOL_1 = {"xh": 16, "hn": 25}
POOL_2 = {"cu1": 7, "su1": 7, "cu2": 9, "su2": 9, "ud1": 11, "z": 11, "cd1": 15, "sd1": 15, "du1": 18,
          "cd2": 21, "sd2": 21, "du2": 25}
READER = {"mean1": "xc", "var1": "ln1", "mean2": "hc", "var2": "ln2", "proj": "pj", "fc": "vu1", "bc": "vu2",
          "x1": "dbc1", "wdt1": "vd1", "x2": "dbc2", "wdt2": "vd2"}
NK = 2 * NS
RB = 3
POOL_B = [k for k in range(NK) if k % 2 == 1]


class Kept:

    def __init__(self, nc, ctx):
        def sb(name, shape, dt=F32):
            return ctx.enter_context(nc.sbuf_tensor(name, shape, dt))

        self.sem = lambda name: ctx.enter_context(nc.semaphore(name))
        self.x_f = sb("x_f", [D, TOK])
        self.cst = sb("cst", [128, C_END])
        self.mod = sb("mod", [128, 2, 6, NSEQ])
        self.eps = sb("eps", [128, 2])
        self.ident, self.avg = self.cst[:, C_ID:C_ID + 128], self.cst[:, C_AVG:C_AVG + 128]


def build(nc, xT, consts, vec, wpk, wdt, wmod, rconst, fvec, wexp0, wexp1, wat, out):
    with ExitStack() as ctx:
        kept = Kept(nc, ctx)
        ssm_layer(nc, kept, xT, consts, vec, wpk, wdt, wmod)
        routed = nc.dram_tensor("routed", (ROWS, RW), F32, kind="Internal").ap()
        results = nc.dram_tensor("results", (2 * TOK, D), F32, kind="Internal").ap()
        mixture_layer(nc, kept, 0, rconst, fvec, wexp0, routed, results)
        attention_layer(nc, kept, wat)
        mixture_layer(nc, kept, 1, rconst, fvec, wexp1, routed, results, out)


def ssm_layer(nc, kept, xT, consts, vec, wpk, wdt, wmod):
    with ExitStack() as ctx:
        def sb(name, shape, dt=F32):
            return ctx.enter_context(nc.sbuf_tensor(name, shape, dt))

        def ps(name, shape):
            return ctx.enter_context(nc.psum_tensor(name, shape, F32))

        sem, x_f, cst, mod, eps, ident, avg = (kept.sem, kept.x_f, kept.cst, kept.mod, kept.eps, kept.ident,
                                               kept.avg)
        vecs = sb("vecs", [128, V_END])
        w = sb("w", [128, W_END])
        wd = sb("wd", [R, 2 * D])
        sel = sb("sel", [128, 32], F32R)
        msc = sb("msc", [128, 4, 2 * NSEQ])
        negA = sb("negA", [128, 2 * NS])

        def col(v, p=128):
            return vecs[0:p, v:v + 1]

        def two(name, shape=(128, CH), dt=F32):
            return [sb(f"{name}{i}", list(shape), dt) for i in range(2)]

        z_, acc_ = two("z"), two("acc")
        delta_ = [two("delta1"), two("delta2")]
        du_ = [two("du1"), two("du2")]
        bcs_ = [two("bcs1", (128, CH), F32R), two("bcs2", (128, CH), F32R)]
        def ring(name, n=RB):
            return [sb(f"{name}{i}", [128, CH]) for i in range(n)]

        dA, dB, hs, hC, Bc = ring("dA"), ring("dB"), ring("hs"), ring("hC"), ring("Bc", 2)
        A0, A1, H = sb("A0", [128, CH]), sb("A1", [128, CH]), sb("H", [128, CH])
        XN, PJ = sb("XN", [128, CH]), sb("PJ", [128, CH])
        Pv = two("Pv")
        Pe = two("Pe")
        Pl = two("Pl")
        Pt = two("Pt")
        wm = [sb(f"wm{l}", [128, 6 * D]) for l in range(2)]
        U = [sb("U1", [128, CH]), sb("U2", [128, CH])]
        dbc = sb("dbc", [R + 2 * NS, CH])

        py, pB, pC = ps("py", [128, CH]), [ps(f"pB{i}", [128, CH]) for i in range(RB)], \
            [ps(f"pC{i}", [128, CH]) for i in range(2)]
        pP_1, pP_2 = ps("pP_1", [128, CH]), ps("pP_2", [128, CH])

        ld0, ldc, ldx = sem("ld0"), sem("ldc"), sem("ldx")
        set_pe, set_act, set_dve, set_pool = sem("set_pe"), sem("set_act"), sem("set_dve"), sem("set_pool")
        pe_1, act_1, dve_1, pool_1 = (Steps(sem(n), t) for n, t in
                                      (("pe_1", PE_1), ("act_1", ACT_1), ("dve_1", DVE_1), ("pool_1", POOL_1)))
        pe_2, act_2, dve_2, pool_2 = (Steps(sem(n), t) for n, t in
                                      (("pe_2", PE_2), ("act_2", ACT_2), ("dve_2", DVE_2), ("pool_2", POOL_2)))
        pe_names = ["B0", "C0", "B1", "B2"]
        for k in range(NK):
            pe_names += ([f"B{k + 3}"] if k + 3 < NK else []) + ([f"C{k + 1}"] if k + 1 < NK else [])
            pe_names += [f"y{k - 1}"] if k else []
        pe_s = Steps(sem("pe_s"), pe_names + [f"y{NK - 1}"])
        act_names = ["e0", "e1", "b1"]
        for k in range(NK - 2):
            act_names += [f"e{k + 2}"] + ([f"b{k + 2}"] if k + 2 in POOL_B else [])
        act_s = Steps(sem("act_s"), act_names)
        dve_names = ["b0"]
        for k in range(NK):
            dve_names += [f"s{k}"] + ([f"b{k + 1}"] if k + 1 < NK and k + 1 not in POOL_B else [])
            dve_names += [f"c{k - 1}"] if k else []
        dve_names += [f"c{NK - 1}"]
        dve_names += ["y0", "y1"] + [f"x{q}" for q in range(SPC)]
        dve_s = Steps(sem("dve_s"), dve_names)
        pool_s = Steps(sem("pool_s"), [f"b{k}" for k in POOL_B])

        block = ctx.enter_context(nc.Block())

        def used(S, c, name, k, n=RB):
            if k >= n:
                return S.now(c, f"{name}{k - n}")
            return S.before(c, f"{name}{max(j for j in range(NK) if j % n == k % n)}")

        def woven(k, c, with_2, with_1, steps_2, steps_1, step_2, step_1):
            for name, at in steps_2.items():
                if with_2 and at == k:
                    step_2(name, c + 1)
            for name, at in steps_1.items():
                if with_1 and at == k:
                    step_1(name, c + 2)

        def rounds(eng, steps_2, steps_1, step_2, step_1, states, at_loop=lambda c: None):
            for name in steps_1:
                step_1(name, 0)
            for name in steps_2:
                step_2(name, 0, 0)
            for name in steps_1:
                step_1(name, 1)
            with eng.Fori(0, NCH // 2 - 1) as i:
                at_loop(i * 2)
                for p in range(2):
                    states(i * 2 + p, p, True, True)
            states(NCH - 2, 0, True, False)
            states(NCH - 1, 1, False, False)

        @block.sync
        def _(sp):
            sp.dma_start(cst[:, :], consts).then_inc(ldc, 16)
            sp.dma_start(vecs[:, :], vec).then_inc(ldc, 16)
            for l in range(2):
                sp.dma_start(wm[l][:, :], wmod[:, l, :]).then_inc(ldc, 16)
            sp.dma_start(x_f[:, 0:CH], xT[:, 0:CH]).then_inc(ld0, 16)
            sp.dma_start(w[:, :], wpk).then_inc(ldc, 16)
            sp.dma_start(wd[:, :], wdt).then_inc(ldc, 16)
            sp.dma_start(x_f[:, CH:TOK], xT[:, CH:TOK]).then_inc(ldx, 16)

        @block.tensor
        def _(pe):
            for s in (pe_1, pe_2, pe_s):
                pe.sem_inc(s.sem, s.per)
            pe.wait_ge(ldc, 96)
            pe.wait_ge(set_dve, 3)
            for l in range(2):
                for j in range(6):
                    at = (l * 6 + j) * NSEQ
                    mm = pe.matmul(pP_1[:, at:at + NSEQ], wm[l][:, j * D:(j + 1) * D],
                                   msc[:, 3, l * NSEQ:(l + 1) * NSEQ], start=True, stop=True)
            mm.then_inc(set_pe, 1)

            def full(dst, lhsT, rhs, name, m=128, start=True, stop=True, S=None):
                for q in range(CH // HB):
                    mm = pe.matmul(dst[0:m, q * HB:(q + 1) * HB], lhsT, rhs(q), start=start, stop=stop)
                mm.then_inc(S.sem, S.step(name))

            def half(t):
                return lambda q: t[:, q * HB:(q + 1) * HB]

            reader = [(act_1, 0, None), (act_2, 0, None)]

            def free_pP(n):
                S, c, name = reader[n - 1]
                if name:
                    pe.wait_ge(S.sem, S.now(c, name))

            def step_1(name, c):
                free_pP(1)
                if name == "mean1":
                    if isinstance(c, int) and c == 0:
                        pe.wait_ge(ld0, 16)
                        pe.wait_ge(set_dve, 4)
                    else:
                        pe.wait_ge(ldx, 16)
                    full(pP_1, avg, lambda q: x_f[:, bass.ds(c * CH + q * HB, HB)], name, S=pe_1)
                elif name == "mean2":
                    pe.wait_ge(act_1.sem, act_1.now(c, f"h{SPC - 1}"))
                    full(pP_1, avg, half(H), name, S=pe_1)
                else:
                    pe.wait_ge(act_1.sem, act_1.now(c, f"sq{name[3]}"))
                    full(pP_1, avg, half(A1), name, S=pe_1)
                reader[0] = (dve_1 if name[0] == "m" else act_1, c, READER[name])

            def step_2(name, c, p=0):
                free_pP(2)
                if name == "proj":
                    pe.wait_ge(act_1.sem, act_1.now(c, "xn"))
                    full(pP_2, w[:, W_PROJ:W_PROJ + D], half(XN), name, S=pe_2)
                elif name in ("fc", "bc"):
                    at = {"fc": W_FC, "bc": W_BC}[name]
                    pe.wait_ge(act_2.sem, act_2.now(c, "pj"))
                    full(pP_2, w[:, at:at + D], half(PJ), name, S=pe_2)
                elif name[0] == "x":
                    s = int(name[1]) - 1
                    at = (W_X1, W_X2)[s]
                    pe.wait_ge(dve_2.sem, dve_2.now(c, f"u{s + 1}"))
                    full(pP_2, w[:, at:at + R + 2 * NS], half(U[s]), name, m=R + 2 * NS, S=pe_2)
                else:
                    s = int(name[3]) - 1
                    pe.wait_ge(act_2.sem, act_2.now(c, f"dbc{s + 1}"))
                    full(pP_2, wd[:, s * D:(s + 1) * D], lambda q: dbc[0:R, q * HB:(q + 1) * HB], name, S=pe_2)
                reader[1] = (act_2, c, READER[name])

            def spread(dst, k, is_c, p, name):
                row = (k % NS) + (NS if is_c else 0)
                rows = bcs_[k // NS][p]
                full(dst, sel[64:128, row:row + 1].to_broadcast([64, 128]),
                     lambda q: rows[64:128, q * HB:(q + 1) * HB], name, S=pe_s)

            def spread_B(k, c, p):
                of = k - RB if k >= RB else max(j for j in range(NK) if j % RB == k % RB)
                S = act_s if of in POOL_B else dve_s
                pe.wait_ge(S.sem, used(S, c, "b", k))
                spread(pB[k % RB], k, False, p, f"B{k}")

            def spread_C(k, c, p):
                pe.wait_ge(dve_s.sem, used(dve_s, c, "c", k, 2))
                spread(pC[k % 2], k, True, p, f"C{k}")

            def add_y(k, c):
                pe.wait_ge(dve_s.sem, dve_s.now(c, f"c{k}"))
                if k == 0:
                    pe.wait_ge(dve_s.sem, dve_s.before(c, "y0"))
                full(py, ident, half(hC[k % RB]), f"y{k}", start=k == 0, stop=k == NK - 1, S=pe_s)

            def states(c, p, with_2, with_1):
                pe.wait_ge(dve_2.sem, dve_2.now(c, "bl2"))
                spread_B(0, c, p)
                spread_C(0, c, p)
                spread_B(1, c, p)
                spread_B(2, c, p)
                for k in range(NK):
                    if k + 3 < NK:
                        spread_B(k + 3, c, p)
                    if k + 1 < NK:
                        spread_C(k + 1, c, p)
                    if k:
                        add_y(k - 1, c)
                    woven(k, c, with_2, with_1, PE_2, PE_1, step_2, step_1)
                add_y(NK - 1, c)

            def at_loop(c):
                free_pP(1)
                free_pP(2)
                reader[0] = (act_1, c + 1, READER["var2"])
                reader[1] = (act_2, c, READER["wdt2"])

            rounds(pe, PE_2, PE_1, step_2, step_1, states, at_loop)

        @block.scalar
        def _(act):
            for s in (act_1, act_2, act_s):
                act.sem_inc(s.sem, s.per)
            act.preload_act_table_set("natural_log_exp_and_others")
            act.wait_ge(set_dve, 1)
            act.activation(msc[:, 1, :], msc[:, 0, :], ACT.Exp).then_inc(set_act, 1)
            act.wait_ge(set_act, 1)
            act.activation(msc[:, 2, :], msc[:, 1, :], ACT.Ln, bias=1.0).then_inc(set_act, 1)
            act.wait_ge(set_act, 2)
            act.activation(msc[:, 1, :], msc[:, 2, :], ACT.Exp, scale=-1.0).then_inc(set_act, 1)
            act.activation(negA[:, :], vecs[:, V_ALOG:V_ALOG + 2 * NS], ACT.Exp).then_inc(set_act, 1)
            act.wait_ge(set_act, 4)
            act.mul(negA[:, :], negA[:, :], -1.0).then_inc(set_act, 1)

            act.wait_ge(set_dve, 7)
            act.wait_ge(set_pool, 2 + RB)

            def do(dst, src, f, name, S, **kw):
                act.activation(dst, src, f, **kw).then_inc(S.sem, S.step(name))

            def step_1(name, c):
                if name == "sq1":
                    act.wait_ge(dve_1.sem, dve_1.now(c, "xc"))
                    act.wait_ge(pool_1.sem, pool_1.before(c, "hn"))
                    do(A1[:, :], A0[:, :], ACT.Square, name, act_1)
                elif name == "sq2":
                    act.wait_ge(dve_1.sem, dve_1.now(c, "hc"))
                    do(A1[:, :], A0[:, :], ACT.Square, name, act_1)
                elif name in ("ln1", "ln2"):
                    act.wait_ge(pe_1.sem, pe_1.now(c, f"var{name[2]}"))
                    do(A1[:, :], pP_1[:, :], ACT.Ln, name, act_1, bias=eps[:, int(name[2]) - 1:int(name[2])])
                elif name in ("rs1", "rs2"):
                    act.wait_ge(act_1.sem, act_1.now(c, f"ln{name[2]}"))
                    do(A1[:, :], A1[:, :], ACT.Exp, name, act_1, scale=-0.5)
                elif name == "xn":
                    act.wait_ge(pool_1.sem, pool_1.now(c, "hn"))
                    act.wait_ge(pe_2.sem, pe_2.before(c, "proj"))
                    do(XN[:, :], A0[:, :], ACT.Identity, name, act_1, scale=col(V_GAM), bias=col(V_BET))
                else:
                    q = int(name[1])
                    act.wait_ge(pool_1.sem, pool_1.now(c, "xh"))
                    act.wait_ge(dve_1.sem, dve_1.before(c, "hc"))
                    b = c * SPC + q
                    do(H[:, q * SEQ:(q + 1) * SEQ], A0[:, q * SEQ:(q + 1) * SEQ], ACT.Identity, name, act_1,
                       scale=mod[:, 0, CA, bass.ds(b, 1)], bias=mod[:, 0, SA, bass.ds(b, 1)])

            def step_2(name, c, p):
                if name == "pj":
                    act.wait_ge(pe_2.sem, pe_2.now(c, "proj"))
                    act.wait_ge(pe_2.sem, pe_2.before(c, "bc"))
                    act.wait_ge(pool_2.sem, pool_2.before(c, "z"))
                    do(PJ[:, :], pP_2[:, :], ACT.Identity, name, act_2, bias=col(V_BPROJ))
                elif name in ("ez", "lz", "sz"):
                    z = z_[p][:, :]
                    if name == "ez":
                        act.wait_ge(dve_2.sem, dve_2.now(c, "mz"))
                        do(z, z, ACT.Exp, name, act_2, scale=-1.0)
                    elif name == "lz":
                        act.wait_ge(act_2.sem, act_2.now(c, "ez"))
                        do(z, z, ACT.Ln, name, act_2, bias=1.0)
                    else:
                        act.wait_ge(act_2.sem, act_2.now(c, "lz"))
                        do(z, z, ACT.Exp, name, act_2, scale=-1.0)
                elif name.startswith("dbc"):
                    s = int(name[3]) - 1
                    act.wait_ge(pe_2.sem, pe_2.now(c, f"x{s + 1}"))
                    act.wait_ge(dve_2.sem, dve_2.before(c, "bl2") if s == 0 else dve_2.now(c, "bl1"))
                    do(dbc[:, :], pP_2[0:R + 2 * NS, :], ACT.Identity, name, act_2, bias=col(V_BX1 + s, R + 2 * NS))
                else:
                    kind, which, s = name[0], name[1], int(name[2]) - 1
                    v, e, l = Pv[s], Pe[s], Pl[s]
                    if kind == "v":
                        b = {"u": V_BFC, "d": V_BDT1}[which] + s
                        act.wait_ge(pe_2.sem, pe_2.now(c, {"u": ("fc", "bc")[s], "d": f"wdt{s + 1}"}[which]))
                        if which == "u":
                            act.wait_ge(dve_2.sem, dve_2.before(c, f"d{s + 1}"))
                        else:
                            act.wait_ge(dve_2.sem, dve_2.now(c, f"u{s + 1}"))
                        do(v[:, :], pP_2[:, :], ACT.Identity, name, act_2, bias=col(b))
                    elif kind == "a":
                        act.wait_ge(act_2.sem, act_2.now(c, f"v{which}{s + 1}"))
                        do(e[:, :], v[:, :], ACT.Abs, name, act_2)
                    elif kind == "e":
                        act.wait_ge(act_2.sem, act_2.now(c, f"a{which}{s + 1}"))
                        do(e[:, :], e[:, :], ACT.Exp, name, act_2, scale=-1.0)
                    else:
                        act.wait_ge(act_2.sem, act_2.now(c, f"e{which}{s + 1}"))
                        do(l[:, :], e[:, :], ACT.Ln, name, act_2, bias=1.0)

            def later(t):
                return t.rearrange("p (s t) -> p s t", t=SEQ)[:, :, 1:SEQ]

            def states(c, p, with_2, with_1):
                def decay(k):
                    act.wait_ge(dve_s.sem, used(dve_s, c, "s", k))
                    if k == 0:
                        act.wait_ge(dve_2.sem, dve_2.now(c, "d2"))
                    do(later(dA[k % RB][:, :]), later(delta_[k // NS][p][:, :]), ACT.Exp, f"e{k}", act_s,
                       scale=negA[:, k:k + 1])

                def copy_B(k):
                    n = POOL_B.index(k)
                    act.wait_ge(pe_s.sem, pe_s.now(c, f"B{k}"))
                    act.wait_ge(pool_s.sem, pool_s.now(c, f"b{POOL_B[n - 2]}") if n >= 2
                                else pool_s.before(c, f"b{POOL_B[n - 2]}"))
                    do(Bc[n % 2][:, :], pB[k % RB][:, :], ACT.Copy, f"b{k}", act_s)

                decay(0)
                decay(1)
                copy_B(1)
                for k in range(NK):
                    if k + 2 < NK:
                        decay(k + 2)
                        if k + 2 in POOL_B:
                            copy_B(k + 2)
                    woven(k, c, with_2, with_1, ACT_2, ACT_1, lambda n, cc: step_2(n, cc, 1 - p), step_1)

            rounds(act, ACT_2, ACT_1, step_2, step_1, states)

        @block.vector
        def _(dve):
            for s in (dve_1, dve_2, dve_s):
                dve.sem_inc(s.sem, s.per)
            dve.wait_ge(ldc, 96)
            dve.tensor_scalar(msc[:, 0, :], vecs[:, V_CT:V_END], -1.0, 44.0, ALU.mult, ALU.min).then_inc(set_dve, 1)
            dve.tensor_copy(sel[64:128, :], cst[64:128, C_SEL:C_SEL + 32]).then_inc(set_dve, 1)
            dve.wait_ge(set_act, 3)
            dve.tensor_tensor(msc[:, 3, :], vecs[:, V_CT:V_END], msc[:, 1, :], ALU.mult).then_inc(set_dve, 1)
            dve.wait_ge(set_pe, 1)
            mflat = mod[:, :, :, :].rearrange("p l j b -> p (l j b)")
            dve.tensor_copy(mflat, pP_1[:, 0:12 * NSEQ]).then_inc(set_dve, 1)
            dve.wait_ge(set_dve, 4)
            for l in range(2):
                for j in (CA, CB):
                    m = mod[:, l, j, :]
                    last = dve.tensor_scalar(m, m, 1.0, None, ALU.add)
            for l in range(2):
                for n, j in enumerate((GA, GB)):
                    o = slice(n * NSEQ, (n + 1) * NSEQ)
                    dve.tensor_scalar(msc[:, l, o], mod[:, l, j, :], 0.0, 2.0, ALU.is_ge, ALU.mult)
                    last = dve.scalar_tensor_tensor(msc[:, 2 + l, o], mod[:, l, j, :], -1.0, mod[:, l, j, :],
                                                    ALU.mult, ALU.max)
            last.then_inc(set_dve, 1)
            dve.wait_ge(set_dve, 5)
            dve.tensor_scalar(msc[:, 2:4, :], msc[:, 2:4, :], 0.25, None, ALU.max).then_inc(set_dve, 1)
            dve.wait_ge(set_dve, 6)
            for l in range(2):
                for n, j in enumerate((GA, GB)):
                    o = slice(n * NSEQ, (n + 1) * NSEQ)
                    last = dve.scalar_tensor_tensor(mod[:, l, j, :], msc[:, l, o], -1.0, msc[:, 2 + l, o],
                                                    ALU.add, ALU.mult)
            last.then_inc(set_dve, 1)

            def tt(dst, a, b, op, name, S):
                dve.tensor_tensor(dst, a, b, op).then_inc(S.sem, S.step(name))

            def gated(src, q, c, name, S):
                xq = x_f[:, bass.ds(c * CH + q * SEQ, SEQ)]
                dve.scalar_tensor_tensor(xq, src[:, q * SEQ:(q + 1) * SEQ], mod[:, 0, GA, bass.ds(c * SPC + q, 1)],
                                         xq, ALU.mult, ALU.add).then_inc(S.sem, S.step(name))

            def step_1(name, c):
                if name == "xc":
                    dve.wait_ge(pe_1.sem, pe_1.now(c, "mean1"))
                    dve.wait_ge(act_1.sem, act_1.before(c, "xn"))
                    tt(A0[:, :], x_f[:, bass.ds(c * CH, CH)], pP_1[:, :], ALU.subtract, name, dve_1)
                elif name == "hc":
                    dve.wait_ge(pe_1.sem, pe_1.now(c, "mean2"))
                    tt(A0[:, :], H[:, :], pP_1[:, :], ALU.subtract, name, dve_1)
                else:
                    if name == "xg0":
                        dve.wait_ge(act_1.sem, act_1.now(c, f"h{SPC - 1}"))
                    gated(H, int(name[2]), c, name, dve_1)

            def step_2(name, c, p):
                if name == "mz":
                    dve.wait_ge(act_2.sem, act_2.now(c, "pj"))
                    dve.tensor_scalar(z_[p][:, :], PJ[:, :], -44.0, None, ALU.max)\
                        .then_inc(dve_2.sem, dve_2.step(name))
                elif name in ("u1", "u2", "d1", "d2"):
                    s = int(name[1]) - 1
                    dst = U[s] if name[0] == "u" else delta_[s][p]
                    dve.wait_ge(pool_2.sem, pool_2.now(c, "s" + name))
                    if name[0] == "u":
                        dve.wait_ge(pool_2.sem, pool_2.before(c, f"du{s + 1}"))
                        dve.wait_ge(dve_2.sem, dve_2.before(c, "acc"))
                    dve.scalar_tensor_tensor(dst[:, :], Pv[s][:, :], 0.0, Pl[s][:, :], ALU.max, ALU.add)\
                        .then_inc(dve_2.sem, dve_2.step(name))
                elif name in ("tu1", "tu2", "td1", "td2"):
                    s = int(name[2]) - 1
                    dve.wait_ge(act_2.sem, act_2.now(c, f"e{name[1:]}"))
                    dve.wait_ge(pool_2.sem, pool_2.before(c, f"sd{s + 1}") if name[1] == "u"
                                else pool_2.now(c, f"su{s + 1}"))
                    dve.tensor_scalar(Pt[s][:, :], Pe[s][:, :], 1.0, -1.0, ALU.add, ALU.add)\
                        .then_inc(dve_2.sem, dve_2.step(name))
                elif name in ("bh1", "bh2"):
                    s = int(name[2]) - 1
                    dve.wait_ge(act_2.sem, act_2.now(c, f"dbc{s + 1}"))
                    dve.tensor_copy(bcs_[s][p][64:96, :], dbc[R:R + 2 * NS, :]).then_inc(dve_2.sem, dve_2.step(name))
                elif name in ("bl1", "bl2"):
                    s = int(name[2]) - 1
                    dve.wait_ge(dve_2.sem, dve_2.now(c, f"bh{s + 1}"))
                    tt(bcs_[s][p][96:128, :], dbc[R:R + 2 * NS, :], bcs_[s][p][64:96, :].bitcast(F32),
                       ALU.subtract, name, dve_2)
                else:
                    dve.wait_ge(pool_2.sem, pool_2.now(c, "ud1"))
                    dve.scalar_tensor_tensor(acc_[p][:, :], U[1][:, :], col(V_D2), acc_[p][:, :], ALU.mult, ALU.add)\
                        .then_inc(dve_2.sem, dve_2.step(name))

            def states(c, p, with_2, with_1):
                def b_product(k):
                    dve.wait_ge(pe_s.sem, pe_s.now(c, f"B{k}"))
                    dve.wait_ge(dve_s.sem, used(dve_s, c, "s", k))
                    tt(dB[k % RB][:, :], du_[k // NS][p][:, :], pB[k % RB][:, :], ALU.mult, f"b{k}", dve_s)

                def c_product(k):
                    dve.wait_ge(dve_s.sem, dve_s.now(c, f"s{k}"))
                    dve.wait_ge(pe_s.sem, pe_s.now(c, f"C{k}"))
                    dve.wait_ge(pe_s.sem, used(pe_s, c, "y", k))
                    tt(hC[k % RB][:, :], hs[k % RB][:, :], pC[k % 2][:, :], ALU.mult, f"c{k}", dve_s)

                dve.wait_ge(pool_2.sem, pool_2.now(c, "du2"))
                b_product(0)
                for k in range(NK):
                    dve.wait_ge(act_s.sem, act_s.now(c, f"e{k}"))
                    if k in POOL_B:
                        dve.wait_ge(pool_s.sem, pool_s.now(c, f"b{k}"))
                    else:
                        dve.wait_ge(dve_s.sem, dve_s.now(c, f"b{k}"))
                    dve.wait_ge(dve_s.sem, used(dve_s, c, "c", k))
                    dve.tensor_tensor_scan(hs[k % RB][:, :], dA[k % RB][:, :], dB[k % RB][:, :], 0.0, ALU.mult,
                                           ALU.add).then_inc(dve_s.sem, dve_s.step(f"s{k}"))
                    if k + 1 < NK and k + 1 not in POOL_B:
                        b_product(k + 1)
                    if k:
                        c_product(k - 1)
                    woven(k, c, with_2, with_1, DVE_2, DVE_1, lambda n, cc: step_2(n, cc, 1 - p), step_1)
                c_product(NK - 1)
                dve.wait_ge(pe_s.sem, pe_s.now(c, f"y{NK - 1}"))
                dve.wait_ge(dve_s.sem, dve_s.now(c, f"c{NK - 1}"))
                tt(hs[0][:, :], acc_[p][:, :], py[:, :], ALU.add, "y0", dve_s)
                dve.wait_ge(dve_s.sem, dve_s.now(c, "y0"))
                tt(hs[0][:, :], hs[0][:, :], z_[p][:, :], ALU.mult, "y1", dve_s)
                dve.wait_ge(dve_s.sem, dve_s.now(c, "y1"))
                for q in range(SPC):
                    gated(hs[0], q, c, f"x{q}", dve_s)
                dve.wait_ge(dve_s.sem, dve_s.now(c, f"x{SPC - 1}"))

            rounds(dve, DVE_2, DVE_1, step_2, step_1, states)

        @block.gpsimd
        def _(pool):
            for s in (pool_1, pool_2, pool_s):
                pool.sem_inc(s.sem, s.per)
            pool.memset(eps[:, 0:1], 1e-5).then_inc(set_pool, 1)
            pool.memset(eps[:, 1:2], 1e-6).then_inc(set_pool, 1)
            for t in dA:
                pool.memset(t[:, :], 0.0).then_inc(set_pool, 1)
            pool.wait_ge(set_pool, 2 + RB)

            def tt(dst, a, b, op, name, S):
                pool.tensor_tensor(dst, a, b, op).then_inc(S.sem, S.step(name))

            def step_1(name, c):
                pool.wait_ge(act_1.sem, act_1.now(c, {"xh": "rs1", "hn": "rs2"}[name]))
                tt(A0[:, :], A0[:, :], A1[:, :], ALU.mult, name, pool_1)

            def step_2(name, c, p):
                if name == "z":
                    pool.wait_ge(act_2.sem, act_2.now(c, "sz"))
                    tt(z_[p][:, :], PJ[:, :], z_[p][:, :], ALU.mult, name, pool_2)
                elif name == "ud1":
                    pool.wait_ge(dve_2.sem, dve_2.now(c, "u1"))
                    tt(acc_[p][:, :], U[0][:, :], col(V_D1).to_broadcast([128, CH]), ALU.mult, name, pool_2)
                elif name in ("du1", "du2"):
                    s = int(name[2]) - 1
                    pool.wait_ge(dve_2.sem, dve_2.now(c, f"d{s + 1}"))
                    tt(du_[s][p][:, :], delta_[s][p][:, :], U[s][:, :], ALU.mult, name, pool_2)
                else:
                    kind, which, s = name[0], name[1], int(name[2]) - 1
                    if kind == "c":
                        pool.wait_ge(dve_2.sem, dve_2.now(c, f"t{which}{s + 1}"))
                        tt(Pt[s][:, :], Pe[s][:, :], Pt[s][:, :], ALU.subtract, name, pool_2)
                    else:
                        pool.wait_ge(pool_2.sem, pool_2.now(c, f"c{which}{s + 1}"))
                        pool.wait_ge(act_2.sem, act_2.now(c, f"l{which}{s + 1}"))
                        tt(Pl[s][:, :], Pl[s][:, :], Pt[s][:, :], ALU.add, name, pool_2)

            def states(c, p, with_2, with_1):
                def b_product(k):
                    pool.wait_ge(act_s.sem, act_s.now(c, f"b{k}"))
                    pool.wait_ge(dve_s.sem, used(dve_s, c, "s", k))
                    tt(dB[k % RB][:, :], du_[k // NS][p][:, :], Bc[POOL_B.index(k) % 2][:, :], ALU.mult, f"b{k}",
                       pool_s)

                b_product(1)
                for k in range(NK):
                    if k + 2 in POOL_B:
                        b_product(k + 2)
                    woven(k, c, with_2, with_1, POOL_2, POOL_1, lambda n, cc: step_2(n, cc, 1 - p), step_1)

            rounds(pool, POOL_2, POOL_1, step_2, step_1, states)


GSUB = 4
SUB = 512
NG = TOK // (GSUB * SUB)
NT = TOK // 128
GT = GSUB * SUB // 128
NE, NF = 8, 4
QS = SUB // SEQ
F_WG, F_GB = 0, NE
F_PER = 2 * NE
F_GAM, F_BET = 2 * F_PER, 2 * F_PER + 1
F_END = 2 * F_PER + 2
CAPT = NT + 1
DUMMY = NE * CAPT
ROWS = (DUMMY + 1) * 128
RW = D + 1
NJ = 2 * NT + NE
TURN = 4
NR = -(-NJ // TURN)
NJT = (NR + 2) * TURN
AWAY = 1 << 20
E_B1 = NF * 128
E_W2 = E_B1 + NF
E_B2 = E_W2 + NF * D
EW = E_B2 + D
R_TRI, R_ONE, R_J, R_BASE, R_ID, R_P, R_AWAY, R_RANK = (0, 128, 256, 256 + NJT, 264 + NJT, 264 + NJT + GT,
                                                        265 + NJT + GT, 266 + NJT + GT)
R_END = R_RANK + NE
I32 = mybir.dt.int32


def mixture_layer(nc, kept, layer, rconst, fvec, wexp, routed, results, out=None):
    L = f"m{layer}_"
    with ExitStack() as ctx:
        def sb(name, shape, dt=F32):
            return ctx.enter_context(nc.sbuf_tensor(L + name, shape, dt))

        def sem(name):
            return kept.sem(L + name)

        W = sb("W", [128, NE * EW])
        gk = [sb(f"gk{k}", [128, NT]) for k in range(2)]
        table = sb("table", [1, 2, NJT], I32)
        loaded_w = sem("loaded_w")

        def load_weights(sp):
            sp.dma_start(W[:, :], wexp).then_inc(loaded_w, 16)

        route(nc, kept, layer, L, sem, rconst, fvec, routed, gk, table, load_weights)
        experts(nc, kept, layer, L, sem, W, table, loaded_w, routed, results)
        combine(nc, kept, layer, L, sem, gk, results, out)


GATE = (["max0", "shift", "sum", "inv", "prob"] + [f"{n}1" for n in ("max", "is", "rank", "first", "one")]
        + ["mask"] + [f"{n}2" for n in ("max", "is", "rank", "first", "one")] + ["both"]
        + ["den", "den1", "inv2", "g1", "g2", "cum", "ex", "slot", "slot_e", "run", "p1", "s1", "p2", "s2", "ix"])


def route(nc, kept, layer, L, sem, rconst, fvec, routed, gk, table, load_weights):
    two_norms = layer == 0
    x_f, mod, eps, ident, avg = kept.x_f, kept.mod, kept.eps, kept.ident, kept.avg
    with ExitStack() as ctx:
        def sb(name, shape, dt=F32):
            return ctx.enter_context(nc.sbuf_tensor(L + name, shape, dt))

        A, B, H = ([sb(f"{n}{j}", [128, SUB]) for j in range(GSUB)] for n in "ABH")
        pa, pb = ([ctx.enter_context(nc.psum_tensor(f"{L}{n}{j}", [128, SUB], F32)) for j in range(GSUB)]
                  for n in ("pa", "pb"))
        fv, rc = sb("fv", [128, F_END]), sb("rc", [128, R_END])
        xt = [[sb(f"xt{p}{k}", [128, GT, RW]) for k in range(2)] for p in range(2)]
        ix = [[sb(f"ix{p}{k}", [128, GT], I32) for k in range(2)] for p in range(2)]
        lg, P, Q, O1, O2, M = (sb(n, [128, GT, NE]) for n in ("lg", "P", "Q", "O1", "O2", "M"))
        cum, zero = sb("cum", [128, NE, GT]), sb("zero", [128, GT])
        t1 = [sb(f"t1{j}", [128, GT, 1]) for j in range(4)]
        run, idr = sb("run", [128, 1, NE]), sb("idr", [128, GT])
        padrow, padix = sb("padrow", [128, RW]), sb("padix", [128, NE], I32)
        cnt, cmp_, n_e, inc = sb("cnt", [1, NE, 1]), sb("cmp", [1, NE, NT]), sb("n_e", [1, NE]), sb("inc", [1, NE])
        room = sb("room", [1, NE])
        te, tr, ta = (sb(n, [1, NJT]) for n in ("te", "tr", "ta"))
        o = layer * F_PER
        wg, gbias = fv[:, o + F_WG:o + F_WG + NE], fv[:, o + F_GB:o + F_GB + NE]
        PRE, TOT = slice(256, 256 + GT * NE), slice(256, 256 + GT * NE)
        loaded, start = sem("loaded"), sem("start")
        taken = sem("taken")
        sent, padded = [sem(f"sent{p}") for p in range(2)], sem("padded")

        def names(kinds):
            return [f"{k}{p}{j}" for p in range(2) for k in kinds for j in (range(GSUB) if k[-1] == "_" else ("",))]

        first = ("mean1_", "var1_") + (("mean2_", "var2_") if two_norms else ())
        pe_n = Steps(sem("pe_n"), names(first + ("lg_", "tr_", "rank")))
        act_n = Steps(sem("act_n"), names(("sq1_", "ln1_", "rs1_", "h_")
                                          + (("sq2_", "ln2_", "rs2_", "xn_") if two_norms else ())
                                          + ("ta_", "tb_", "exp")))
        dve_n = Steps(sem("dve_n"), names(("xc_", "xh_") + (("xg_", "hc_", "hn_") if two_norms else ())
                                          + ("lc_", "id1", "id2", "id3") + tuple(GATE)))
        pool_n = Steps(sem("pool_n"), ["sent0", "sent1"])
        tab = Steps(sem("tab"), TABLE)
        xn_step = "xn_" if two_norms else "h_"
        block = ctx.enter_context(nc.Block())

        def last(S, g, p, name):
            return S.now(g, f"{name[0]}0{name[1]}") if p else S.before(g, f"{name[0]}1{name[1]}")

        def at(g, p, j, n=SUB, off=0):
            return bass.ds(g * (2 * GSUB * SUB) + p * (GSUB * SUB) + j * SUB + off, n)

        def seq(g, p, j, q):
            return bass.ds(g * (2 * GSUB * QS) + (p * GSUB + j) * QS + q, 1)

        @block.sync
        def _(sp):
            sp.dma_start(fv[:, :], fvec).then_inc(loaded, 16)
            sp.dma_start(rc[:, :], rconst).then_inc(loaded, 16)
            load_weights(sp)

        @block.tensor
        def _(pe):
            pe.sem_inc(pe_n.sem, pe_n.per)
            pe.wait_ge(loaded, 32)
            with pe.Fori(0, NG // 2) as g:
                def mm(dst, lhsT, rhs, name):
                    pe.matmul(dst, lhsT, rhs, start=True, stop=True).then_inc(pe_n.sem, pe_n.step(name))

                for p in range(2):
                    for j in range(GSUB):
                        pe.wait_ge(dve_n.sem, last(dve_n, g, p, ("slot", "")))
                        mm(pa[j][:, :], avg, x_f[:, at(g, p, j)], f"mean1_{p}{j}")
                    for j in range(GSUB):
                        pe.wait_ge(act_n.sem, act_n.now(g, f"sq1_{p}{j}"))
                        pe.wait_ge(act_n.sem, last(act_n, g, p, ("tb_", j)))
                        mm(pb[j][:, :], avg, B[j][:, :], f"var1_{p}{j}")
                    if two_norms:
                        for j in range(GSUB):
                            pe.wait_ge(act_n.sem, act_n.now(g, f"h_{p}{j}"))
                            mm(pa[j][:, :], avg, H[j][:, :], f"mean2_{p}{j}")
                        for j in range(GSUB):
                            pe.wait_ge(act_n.sem, act_n.now(g, f"sq2_{p}{j}"))
                            mm(pb[j][:, :], avg, B[j][:, :], f"var2_{p}{j}")
                    for j in range(GSUB):
                        pe.wait_ge(act_n.sem, act_n.now(g, f"{xn_step}{p}{j}"))
                        for q in range(SUB // 128):
                            m = pe.matmul(pa[j][:, q * NE:(q + 1) * NE], A[j][:, q * 128:(q + 1) * 128], wg,
                                          start=True, stop=True)
                        m.then_inc(pe_n.sem, pe_n.step(f"lg_{p}{j}"))
                    for j in range(GSUB):
                        for q in range(SUB // 128):
                            m = pe.transpose(pb[j][:, q * 128:(q + 1) * 128], A[j][:, q * 128:(q + 1) * 128], ident)
                        m.then_inc(pe_n.sem, pe_n.step(f"tr_{p}{j}"))
                    pe.wait_ge(dve_n.sem, dve_n.now(g, f"both{p}"))
                    flat = M[:, :, :].rearrange("p t e -> p (t e)")
                    pe.matmul(pa[0][:, PRE], rc[:, R_TRI:R_TRI + 128], flat, start=True, stop=True)
                    mm(pa[1][:, TOT], rc[:, R_ONE:R_ONE + 128], flat, f"rank{p}")

        @block.scalar
        def _(act):
            act.sem_inc(act_n.sem, act_n.per)
            act.preload_act_table_set("natural_log_exp_and_others")
            act.wait_ge(loaded, 32)
            with act.Fori(0, NG // 2) as g:
                for p in range(2):
                    def square(n, ready):
                        for j in range(GSUB):
                            act.wait_ge(dve_n.sem, dve_n.now(g, f"{ready}_{p}{j}"))
                            act.activation(B[j][:, :], A[j][:, :], ACT.Square)\
                                .then_inc(act_n.sem, act_n.step(f"sq{n}_{p}{j}"))

                    def rstd(n):
                        for j in range(GSUB):
                            act.wait_ge(pe_n.sem, pe_n.now(g, f"var{n}_{p}{j}"))
                            act.activation(B[j][:, :], pb[j][:, :], ACT.Ln, bias=eps[:, 0:1])\
                                .then_inc(act_n.sem, act_n.step(f"ln{n}_{p}{j}"))
                        for j in range(GSUB):
                            act.wait_ge(act_n.sem, act_n.now(g, f"ln{n}_{p}{j}"))
                            act.activation(B[j][:, :], B[j][:, :], ACT.Exp, scale=-0.5)\
                                .then_inc(act_n.sem, act_n.step(f"rs{n}_{p}{j}"))

                    square(1, "xc")
                    rstd(1)
                    for j in range(GSUB):
                        act.wait_ge(dve_n.sem, dve_n.now(g, f"xh_{p}{j}"))
                        for q in range(QS):
                            dst = (H if two_norms else A)[j][:, q * SEQ:(q + 1) * SEQ]
                            a = act.activation(dst, A[j][:, q * SEQ:(q + 1) * SEQ], ACT.Identity,
                                               scale=mod[:, layer, CB, seq(g, p, j, q)],
                                               bias=mod[:, layer, SB, seq(g, p, j, q)])
                        a.then_inc(act_n.sem, act_n.step(f"h_{p}{j}"))
                    if two_norms:
                        square(2, "hc")
                        rstd(2)
                        for j in range(GSUB):
                            act.wait_ge(dve_n.sem, dve_n.now(g, f"hn_{p}{j}"))
                            act.activation(A[j][:, :], A[j][:, :], ACT.Identity, scale=fv[:, F_GAM:F_GAM + 1],
                                           bias=fv[:, F_BET:F_BET + 1])\
                                .then_inc(act_n.sem, act_n.step(f"xn_{p}{j}"))
                    act.wait_ge(pool_n.sem, pool_n.before(g, f"sent{p}"))
                    for k in range(2):
                        for j in range(GSUB):
                            act.wait_ge(pe_n.sem, pe_n.now(g, f"tr_{p}{j}"))
                            nq = SUB // 128
                            act.activation(xt[p][k][:, j * nq:(j + 1) * nq, 0:D],
                                           pb[j][:, :].rearrange("p (q d) -> p q d", d=D), ACT.Copy)\
                                .then_inc(act_n.sem, act_n.step(f"t{'ab'[k]}_{p}{j}"))
                    act.wait_ge(dve_n.sem, dve_n.now(g, f"shift{p}"))
                    act.activation(P[:, :, :], P[:, :, :], ACT.Exp).then_inc(act_n.sem, act_n.step(f"exp{p}"))

        @block.gpsimd
        def _(pool):
            pool.sem_inc(pool_n.sem, pool_n.per)
            with pool.Fori(0, NG // 2) as g:
                for p in range(2):
                    pool.wait_ge(act_n.sem, act_n.now(g, f"tb_{p}{GSUB - 1}"))
                    pool.wait_ge(dve_n.sem, dve_n.now(g, f"ix{p}"))
                    pool.sem_inc(taken, 1)
                    for k in range(2):
                        for t in range(GT):
                            pool.indirect_dma_start(routed, bass.IndirectOffsetOnAxis(ap=ix[p][k][:, t:t + 1], axis=0),
                                                    xt[p][k][:, t, :], None).then_inc(sent[p], 16)
                    pool.wait_ge(sent[p], (g + 1) * (2 * GT * 16))
                    pool.sem_inc(pool_n.sem, pool_n.step(f"sent{p}"))
            pool.wait_ge(tab.sem, tab.at0("padix"))
            for e in range(NE):
                pool.indirect_dma_start(routed, bass.IndirectOffsetOnAxis(ap=padix[:, e:e + 1], axis=0),
                                        padrow[:, :], None).then_inc(padded, 16)
            pool.dma_start(routed[DUMMY * 128:(DUMMY + 1) * 128, :], padrow[:, :]).then_inc(padded, 16)
            pool.wait_ge(padded, (NE + 1) * 16)

        @block.vector
        def _(dve):
            dve.sem_inc(dve_n.sem, dve_n.per)
            dve.wait_ge(loaded, 32)
            dve.tensor_copy(run[:, 0, :], rc[:, R_BASE:R_BASE + NE]).then_inc(start, 1)
            dve.tensor_copy(idr[:, :], rc[:, R_ID:R_ID + GT]).then_inc(start, 1)
            dve.memset(zero[:, :], 0.0).then_inc(start, 1)
            dve.memset(padrow[:, 0:D], 0.0).then_inc(start, 1)
            dve.tensor_copy(padrow[:, D:RW].bitcast(I32), rc[:, R_AWAY:R_AWAY + 1]).then_inc(start, 1)
            dve.wait_ge(start, 5)
            with dve.Fori(0, NG // 2) as g:
                def step(name, ins):
                    ins.then_inc(dve_n.sem, dve_n.step(name))

                for p in range(2):
                    for j in range(GSUB):
                        dve.wait_ge(pe_n.sem, pe_n.now(g, f"mean1_{p}{j}"))
                        dve.wait_ge(pe_n.sem, last(pe_n, g, p, ("tr_", j)))
                        step(f"xc_{p}{j}", dve.tensor_tensor(A[j][:, :], x_f[:, at(g, p, j)], pa[j][:, :],
                                                             ALU.subtract))
                    for j in range(GSUB):
                        dve.wait_ge(act_n.sem, act_n.now(g, f"rs1_{p}{j}"))
                        step(f"xh_{p}{j}", dve.tensor_tensor(A[j][:, :], A[j][:, :], B[j][:, :], ALU.mult))
                    if two_norms:
                        for j in range(GSUB):
                            dve.wait_ge(act_n.sem, act_n.now(g, f"h_{p}{j}"))
                            for q in range(QS):
                                xq = x_f[:, at(g, p, j, SEQ, q * SEQ)]
                                v = dve.scalar_tensor_tensor(xq, H[j][:, q * SEQ:(q + 1) * SEQ],
                                                             mod[:, layer, GB, seq(g, p, j, q)], xq,
                                                             ALU.mult, ALU.add)
                            step(f"xg_{p}{j}", v)
                        for j in range(GSUB):
                            dve.wait_ge(pe_n.sem, pe_n.now(g, f"mean2_{p}{j}"))
                            step(f"hc_{p}{j}", dve.tensor_tensor(A[j][:, :], H[j][:, :], pa[j][:, :], ALU.subtract))
                        for j in range(GSUB):
                            dve.wait_ge(act_n.sem, act_n.now(g, f"rs2_{p}{j}"))
                            step(f"hn_{p}{j}", dve.tensor_tensor(A[j][:, :], A[j][:, :], B[j][:, :], ALU.mult))
                    for j in range(GSUB):
                        dve.wait_ge(pe_n.sem, pe_n.now(g, f"lg_{p}{j}"))
                        nq = SUB // 128
                        step(f"lc_{p}{j}", dve.tensor_tensor(
                            lg[:, j * nq:(j + 1) * nq, :], pa[j][:, 0:nq * NE].rearrange("p (q e) -> p q e", e=NE),
                            gbias.rearrange("p (q e) -> p q e", q=1).to_broadcast([128, nq, NE]), ALU.add))
                    dve.wait_ge(pool_n.sem, pool_n.before(g, f"sent{p}"))
                    step(f"id1{p}", dve.tensor_copy(xt[p][0][:, :, D].bitcast(I32), idr[:, :]))
                    step(f"id2{p}", dve.tensor_scalar(xt[p][1][:, :, D].bitcast(I32), idr[:, :], float(TOK), None,
                                                      ALU.add))
                    dve.wait_ge(dve_n.sem, dve_n.now(g, f"id2{p}"))
                    step(f"id3{p}", dve.tensor_scalar(idr[:, :], idr[:, :], float(GSUB * SUB), None, ALU.add))

                    def wide(t):
                        return t[:, :, :].to_broadcast([128, GT, NE])

                    def do(name, ins):
                        ins.then_inc(dve_n.sem, dve_n.step(f"{name}{p}"))
                        dve.wait_ge(dve_n.sem, dve_n.now(g, f"{name}{p}"))

                    def tt(name, dst, a, b, op):
                        do(name, dve.tensor_tensor(dst, a, b, op))

                    P_, Q_, S_ = P[:, :, :], Q[:, :, :], lg[:, :, :]
                    dve.wait_ge(dve_n.sem, dve_n.now(g, f"id3{p}"))
                    do("max0", dve.tensor_reduce(t1[0][:, :, 0], S_, AX.X, ALU.max))
                    tt("shift", P_, S_, wide(t1[0]), ALU.subtract)
                    dve.wait_ge(act_n.sem, act_n.now(g, f"exp{p}"))
                    do("sum", dve.tensor_reduce(t1[0][:, :, 0], P_, AX.X, ALU.add))
                    do("inv", dve.reciprocal(t1[0][:, :, :], t1[0][:, :, :]))
                    tt("prob", P_, P_, wide(t1[0]), ALU.mult)
                    rank = rc[:, R_RANK:R_RANK + NE].rearrange("p (q e) -> p q e", q=1).to_broadcast([128, GT, NE])
                    for n, one in ((1, O1), (2, O2)):
                        m = t1[n]
                        do(f"max{n}", dve.tensor_reduce(m[:, :, 0], P_, AX.X, ALU.max))
                        tt(f"is{n}", Q_, P_, wide(m), ALU.is_equal)
                        tt(f"rank{n}", Q_, Q_, rank, ALU.mult)
                        do(f"first{n}", dve.tensor_reduce(t1[3][:, :, 0], Q_, AX.X, ALU.max))
                        tt(f"one{n}", one[:, :, :], Q_, wide(t1[3]), ALU.is_equal)
                        if n == 1:
                            do("mask", dve.scalar_tensor_tensor(P_, O1[:, :, :], -2.0, P_, ALU.mult, ALU.add))
                    tt("both", M[:, :, :], O1[:, :, :], O2[:, :, :], ALU.add)
                    tt("den", t1[0][:, :, :], t1[1][:, :, :], t1[2][:, :, :], ALU.add)
                    do("den1", dve.tensor_scalar(t1[0][:, :, :], t1[0][:, :, :], 1e-9 if layer == 0 else 0.0, None,
                                                 ALU.add))
                    do("inv2", dve.reciprocal(t1[0][:, :, :], t1[0][:, :, :]))
                    for k in range(2):
                        tt(f"g{k + 1}", gk[k][:, bass.ds(g * (2 * GT) + p * GT, GT)], t1[1 + k][:, :, 0],
                           t1[0][:, :, 0], ALU.mult)
                    dve.wait_ge(pe_n.sem, pe_n.now(g, f"rank{p}"))
                    tot = pa[1][:, TOT].rearrange("p (t e) -> p t e", e=NE)
                    for e in range(NE):
                        v = dve.tensor_tensor_scan(cum[:, e, :], tot[:, :, e], zero[:, :], 0.0, ALU.add, ALU.add)
                    do("cum", v)
                    by_tile = cum[:, :, :].rearrange("p e t -> p t e")
                    tt("ex", S_, by_tile, tot, ALU.subtract)
                    tt("slot", S_, S_, pa[0][:, PRE].rearrange("p (t e) -> p t e", e=NE), ALU.add)
                    tt("slot_e", S_, S_, run[:, :, :].to_broadcast([128, GT, NE]), ALU.add)
                    tt("run", run[:, 0, :], run[:, 0, :], cum[:, :, GT - 1], ALU.add)
                    for n, one in ((1, O1), (2, O2)):
                        tt(f"p{n}", Q_, S_, one[:, :, :], ALU.mult)
                        do(f"s{n}", dve.tensor_reduce(t1[n][:, :, 0], Q_, AX.X, ALU.add))
                    dve.tensor_copy(ix[p][0][:, :], t1[1][:, :, 0])
                    do("ix", dve.tensor_copy(ix[p][1][:, :], t1[2][:, :, 0]))

            def do(name, ins):
                ins.then_inc(tab.sem, tab.step(name))
                dve.wait_ge(tab.sem, tab.at0(name))

            J = rc[0:1, R_J:R_J + NJT]
            do("padix", dve.tensor_tensor(padix[:, :], run[:, 0, :],
                                          rc[:, R_P:R_P + 1].to_broadcast([128, NE]), ALU.add))
            do("cnt", dve.tensor_tensor(cnt[:, :, 0], run[0:1, 0, :], rc[0:1, R_BASE:R_BASE + NE], ALU.subtract))
            do("cnt1", dve.tensor_scalar(cnt[:, :, 0], cnt[:, :, 0], 1 / 128, None, ALU.mult))
            do("cmp", dve.tensor_tensor(cmp_[:, :, :], cnt[:, :, :].to_broadcast([1, NE, NT]),
                                        J[:, 0:NT].rearrange("p (e t) -> p e t", e=1).to_broadcast([1, NE, NT]),
                                        ALU.is_gt))
            do("n_e", dve.tensor_reduce(n_e[:, :], cmp_[:, :, :], AX.X, ALU.add))
            do("inc", dve.tensor_tensor_scan(inc[:, :], n_e[:, :], zero[0:1, 0:NE], 0.0, ALU.add, ALU.add))
            do("room", dve.tensor_scalar(room[:, :], n_e[:, :], -1.0, float(CAPT), ALU.mult, ALU.add))
            do("e0", dve.tensor_scalar(te[:, :], J, inc[:, 0:1], None, ALU.is_ge))
            do("r0", dve.tensor_copy(tr[:, :], J))
            for e in range(1, NE):
                do(f"a{e}", dve.tensor_scalar(ta[:, :], J, inc[:, e - 1:e], room[:, e - 1:e], ALU.is_ge, ALU.mult))
                do(f"r{e}", dve.tensor_tensor(tr[:, :], tr[:, :], ta[:, :], ALU.add))
                if e > 1:
                    do(f"e{e}", dve.scalar_tensor_tensor(te[:, :], J, inc[:, e - 1:e], te[:, :], ALU.is_ge, ALU.add))
            do("left", dve.tensor_scalar(ta[:, :], tr[:, :], -1.0, float(DUMMY), ALU.mult, ALU.add))
            do("left1", dve.scalar_tensor_tensor(ta[:, :], J, inc[:, NE - 1:NE], ta[:, :], ALU.is_ge, ALU.mult))
            do("r", dve.tensor_tensor(tr[:, :], tr[:, :], ta[:, :], ALU.add))
            for n, (t, size) in enumerate(((te, EW), (tr, 128))):
                do(f"t{n}", dve.tensor_scalar(table[:, n, :], t[:, :], float(size), None, ALU.mult))


TABLE = (["padix", "cnt", "cnt1", "cmp", "n_e", "inc", "room", "e0", "r0"]
         + [n for e in range(1, NE) for n in (f"a{e}", f"r{e}", f"e{e}") if n != "e1"]
         + ["left", "left1", "r", "t0", "t1"])


def experts(nc, kept, layer, L, sem, W, table, loaded_w, routed, results):
    ident = kept.ident
    gelu, gelu_set = ((ACT.Gelu_apprx_tanh, "gelu_apprx_tanh_and_others") if layer == 0
                      else (ACT.Gelu, "gelu_and_others"))
    with ExitStack() as ctx:
        def ring(name, shape, dt=F32, n=2):
            return [ctx.enter_context(nc.sbuf_tensor(f"{L}{name}{u}", shape, dt)) for u in range(n)]

        xs = ring("xs", [128, RW], n=TURN)
        xT = ring("xT", [D, 128])
        ws = ring("ws", [128, EW], n=TURN)
        hT = ring("hT", [128, NF * 128])
        ys = ring("ys", [128, D])
        idn, ids = ring("idn", [128, 1], I32), ring("ids", [128, 1], I32)
        pT, pu, pd = ([ctx.enter_context(nc.psum_tensor(f"{L}{n}{u}", [128, 512], F32)) for u in range(2)]
                      for n in ("pT", "pu", "pd"))
        transposed, up, down = sem("transposed"), sem("up"), sem("down")
        activated = sem("activated")
        weighted, rows_in, result = sem("weighted"), sem("rows_in"), sem("result")
        kept_ids, moved = sem("kept_ids"), sem("moved")
        taken = sem("taken_x")
        fetched, put = [sem(f"fetched{v}") for v in range(TURN)], [sem(f"put{u}") for u in range(2)]
        block = ctx.enter_context(nc.Block())

        def value(eng, reg, row, j, top):
            eng.reg_load(reg, table[0:1, row, bass.ds(j, 1)] if not isinstance(j, int) else table[0:1, row, j:j + 1])
            return eng.snap(reg, min_val=0, max_val=top)

        @block.sync
        def _(sp):
            with sp.register(L + "place") as reg:
                def fetch(j, v):
                    at = value(sp, reg, 1, j, DUMMY * 128)
                    sp.dma_start(xs[v][:, :], routed[bass.ds(at, 128), :]).then_inc(fetched[v], 16)

                for v in range(TURN):
                    fetch(v, v)
                with sp.Fori(0, NR) as r:
                    for v in range(TURN):
                        j = r * TURN + v
                        sp.wait_ge(transposed, j + 1)
                        sp.wait_ge(kept_ids, j + 1)
                        fetch(j + TURN, v)
            for v in range(TURN):
                sp.wait_ge(fetched[v], (NR + 1) * 16)

        @block.tensor
        def _(pe):
            def transpose(v, j, turn):
                pe.wait_ge(fetched[v], (turn + 1) * 16)
                pe.wait_ge(rows_in, j + 1)
                pe.transpose(pT[v % 2][:, 0:128], xs[v][:, 0:D], ident).then_inc(transposed, 1)

            pe.sem_inc(down, 2)
            pe.sem_inc(up, 2)
            for v in range(2):
                transpose(v, v, 0)
            with pe.Fori(0, NR) as r:
                for pair in range(TURN // 2):
                    for u in range(2):
                        v = 2 * pair + u
                        j = r * TURN + v
                        pe.wait_ge(weighted, j + 1)
                        pe.wait_ge(rows_in, j + 3)
                        pe.wait_ge(activated, j + 1)
                        for f in range(NF):
                            m = pe.matmul(pu[u][:, f * 128:(f + 1) * 128], ws[v][:, f * 128:(f + 1) * 128],
                                          xT[u][:, :], start=True, stop=True)
                        m.then_inc(up, 1)
                    for u in range(2):
                        v = 2 * pair + u
                        j = r * TURN + v
                        transpose((v + 2) % TURN, j + 2, r + (v + 2) // TURN)
                        pe.wait_ge(result, j + 1)
                        pe.wait_ge(activated, j + 3)
                        for f in range(NF):
                            m = pe.matmul(pd[u][:, 0:D], hT[u][:, f * 128:(f + 1) * 128],
                                          ws[v][:, E_W2 + f * D:E_W2 + (f + 1) * D], start=f == 0, stop=f == NF - 1)
                        m.then_inc(down, 1)

        @block.scalar
        def _(act):
            def rows(j, u):
                act.wait_ge(transposed, j + 1)
                act.wait_ge(up, j + 1)
                act.activation(xT[u][:, :], pT[u][:, 0:128], ACT.Copy).then_inc(rows_in, 1)

            act.sem_inc(activated, 2)
            act.sem_inc(rows_in, 2)
            act.preload_act_table_set(gelu_set)
            for u in range(2):
                rows(u, u)
            with act.Fori(0, NR) as r:
                for pair in range(TURN // 2):
                    for u in range(2):
                        v = 2 * pair + u
                        j = r * TURN + v
                        act.wait_ge(down, j + 1)
                        act.wait_ge(up, j + 3)
                        for f in range(NF):
                            a = act.activation(hT[u][:, f * 128:(f + 1) * 128], pu[u][:, f * 128:(f + 1) * 128],
                                               gelu, bias=ws[v][:, E_B1 + f:E_B1 + f + 1])
                        a.then_inc(activated, 1)
                    for u in range(2):
                        rows(r * TURN + (2 * pair + u + 2), u)

        @block.gpsimd
        def _(pool):
            for u in range(2):
                pool.dma_start(ys[u][:, :], ident).then_inc(put[u], 16)
            with pool.Fori(0, NR) as r:
                for v in range(TURN):
                    j, u = r * TURN + v, v % 2
                    pool.wait_ge(result, j + 3)
                    pool.sem_inc(taken, 1)
                    pool.indirect_dma_start(results, bass.IndirectOffsetOnAxis(ap=ids[u][:, 0:1], axis=0),
                                            ys[u][:, :], None, bounds_check=2 * TOK - 1, oob_is_err=False)\
                        .then_inc(put[u], 16)
            for u in range(2):
                pool.wait_ge(put[u], (NR * TURN // 2 + 1) * 16)

        @block.vector
        def _(dve):
            with dve.register(L + "expert") as reg:
                def weights(j, v):
                    w = W[:, bass.ds(value(dve, reg, 0, j, (NE - 1) * EW), EW)]
                    dve.wait_ge(down, j + 1 if isinstance(j, int) else j - 1)
                    dve.tensor_copy(ws[v][:, :], w).then_inc(weighted, 1)

                def places(j, v):
                    dve.tensor_copy(idn[v % 2][:, :], xs[v][:, D:RW].bitcast(I32)).then_inc(kept_ids, 1)

                dve.wait_ge(loaded_w, 16)
                dve.sem_inc(result, 2)
                for u in range(2):
                    weights(u, u)
                    dve.wait_ge(transposed, u + 1)
                    places(u, u)
                with dve.Fori(0, NR) as r:
                    for v in range(TURN):
                        j, u = r * TURN + v, v % 2
                        weights(j + 2, (v + 2) % TURN)
                        dve.wait_ge(put[u], (r * (TURN // 2) + (v // 2 + 1)) * 16)
                        dve.wait_ge(kept_ids, j + 2)
                        dve.tensor_copy(ids[u][:, :], idn[u][:, :]).then_inc(moved, 1)
                        dve.wait_ge(transposed, j + 3)
                        dve.wait_ge(moved, j + 1)
                        places(j + 2, (v + 2) % TURN)
                        dve.wait_ge(down, j + 3)
                        dve.tensor_tensor(ys[u][:, :], pd[u][:, 0:D], ws[v][:, E_B2:EW], ALU.add)\
                            .then_inc(result, 1)


def combine(nc, kept, layer, L, sem, gk, results, out):
    x_f, mod, ident = kept.x_f, kept.mod, kept.ident
    NB, NX = SUB // 128, TOK // SUB // 2
    with ExitStack() as ctx:
        yy = [[ctx.enter_context(nc.sbuf_tensor(f"{L}yy{p}{k}", [128, NB, D], F32)) for k in range(2)]
              for p in range(2)]
        pt = [ctx.enter_context(nc.psum_tensor(f"{L}pt{p}", [128, SUB], F32)) for p in range(2)]
        fetched = [sem(f"back{p}") for p in range(2)]
        pe_c, dve_c = Steps(sem("pe_c"), ["t0", "t1"]), Steps(sem("dve_c"), ["a0", "b0", "x0", "a1", "b1", "x1"])
        stored = sem("stored")
        block = ctx.enter_context(nc.Block())

        @block.sync
        def _(sp):
            with sp.Fori(0, NX) as i:
                for p in range(2):
                    sp.wait_ge(pe_c.sem, pe_c.before(i, f"t{p}"))
                    for k in range(2):
                        sp.dma_start(yy[p][k][:, :, :],
                                     results[bass.ds(i * (2 * SUB) + (k * TOK + p * SUB), SUB), :]
                                     .rearrange("(q t) d -> t q d", t=128)).then_inc(fetched[p], 16)
            if out is not None:
                sp.wait_ge(dve_c.sem, (NX + 1) * dve_c.per)
                sp.dma_start(out, x_f[:, :]).then_inc(stored, 16)
                sp.wait_ge(stored, 16)

        @block.tensor
        def _(pe):
            pe.sem_inc(pe_c.sem, pe_c.per)
            with pe.Fori(0, NX) as i:
                for p in range(2):
                    pe.wait_ge(dve_c.sem, dve_c.now(i, f"b{p}"))
                    pe.wait_ge(dve_c.sem, dve_c.before(i, f"x{p}"))
                    for q in range(NB):
                        m = pe.transpose(pt[p][:, q * 128:(q + 1) * 128], yy[p][0][:, q, :], ident)
                    m.then_inc(pe_c.sem, pe_c.step(f"t{p}"))

        @block.vector
        def _(dve):
            dve.sem_inc(dve_c.sem, dve_c.per)
            with dve.Fori(0, NX) as i:
                for p in range(2):
                    def g(k, q):
                        return gk[k][:, bass.ds(i * (2 * NB) + (p * NB + q), 1)]

                    dve.wait_ge(fetched[p], (i + 1) * 32)
                    for q in range(NB):
                        v = dve.tensor_scalar(yy[p][0][:, q, :], yy[p][0][:, q, :], g(0, q), None, ALU.mult)
                    v.then_inc(dve_c.sem, dve_c.step(f"a{p}"))
                    dve.wait_ge(dve_c.sem, dve_c.now(i, f"a{p}"))
                    for q in range(NB):
                        v = dve.scalar_tensor_tensor(yy[p][0][:, q, :], yy[p][1][:, q, :], g(1, q),
                                                     yy[p][0][:, q, :], ALU.mult, ALU.add)
                    v.then_inc(dve_c.sem, dve_c.step(f"b{p}"))
                    dve.wait_ge(pe_c.sem, pe_c.now(i, f"t{p}"))
                    for q in range(QS):
                        xq = x_f[:, bass.ds(i * (2 * SUB) + (p * SUB + q * SEQ), SEQ)]
                        v = dve.scalar_tensor_tensor(xq, pt[p][:, q * SEQ:(q + 1) * SEQ],
                                                     mod[:, layer, GB, bass.ds(i * (2 * QS) + (p * QS + q), 1)], xq,
                                                     ALU.mult, ALU.add)
                    v.then_inc(dve_c.sem, dve_c.step(f"x{p}"))


NLOC, DH = 4, 8
LF, GF = NLOC * DH, D - NLOC * DH
BLK = 64
HV = DH + 1
VW = NLOC * HV + GF + 1
PW = 2 * GF + D
(A_QK, A_TOK, A_WOG, A_WOL, A_CAUS, A_HEAD) = (0, D, D + PW, 2 * D + PW, 3 * D + PW, 4 * D + PW)
A_ROWS = A_HEAD + GF
A_END = A_ROWS + NLOC
SCALE = DH ** -0.5


def attention_layer(nc, kept, wat):
    L = "a_"
    with ExitStack() as ctx:
        def sb(name, shape, dt=F32):
            return ctx.enter_context(nc.sbuf_tensor(L + name, shape, dt))

        def sem(name):
            return kept.sem(L + name)

        h_f = sb("h_f", [D, TOK])
        wa = sb("wa", [128, A_END])
        loaded, fixed = sem("loaded"), sem("fixed")
        normalise(nc, kept, 1, L, sem, h_f, SA, CA, lambda sp: sp.dma_start(wa[:, :], wat).then_inc(loaded, 16))
        attend(nc, kept, L, sem, h_f, wa, loaded, fixed)


def normalise(nc, kept, layer, L, sem, h_f, shift, scale, load):
    x_f, mod, eps, avg = kept.x_f, kept.mod, kept.eps, kept.avg
    with ExitStack() as pre:
        A = [pre.enter_context(nc.sbuf_tensor(f"{L}A{j}", [128, SUB], F32)) for j in range(GSUB)]
        B = [pre.enter_context(nc.sbuf_tensor(f"{L}B{j}", [128, SUB], F32)) for j in range(GSUB)]
        pa = [pre.enter_context(nc.psum_tensor(f"{L}pa{j}", [128, SUB], F32)) for j in range(GSUB)]
        pb = [pre.enter_context(nc.psum_tensor(f"{L}pb{j}", [128, SUB], F32)) for j in range(GSUB)]
        names = lambda kinds: [f"{k}{j}" for k in kinds for j in range(GSUB)]
        pe_n = Steps(sem("pe_n"), names(("mean_", "var_")))
        act_n = Steps(sem("act_n"), names(("sq_", "ln_", "rs_", "h_")))
        dve_n = Steps(sem("dve_n"), names(("xc_", "xh_")))
        block = pre.enter_context(nc.Block())

        def at(g, j):
            return bass.ds(g * (GSUB * SUB) + j * SUB, SUB)

        @block.sync
        def _(sp):
            load(sp)

        @block.tensor
        def _(pe):
            pe.sem_inc(pe_n.sem, pe_n.per)
            with pe.Fori(0, NG) as g:
                for j in range(GSUB):
                    pe.wait_ge(dve_n.sem, dve_n.before(g, f"xc_{j}"))
                    pe.matmul(pa[j][:, :], avg, x_f[:, at(g, j)], start=True, stop=True)\
                        .then_inc(pe_n.sem, pe_n.step(f"mean_{j}"))
                for j in range(GSUB):
                    pe.wait_ge(act_n.sem, act_n.now(g, f"sq_{j}"))
                    pe.matmul(pb[j][:, :], avg, B[j][:, :], start=True, stop=True)\
                        .then_inc(pe_n.sem, pe_n.step(f"var_{j}"))

        @block.scalar
        def _(act):
            act.sem_inc(act_n.sem, act_n.per)
            act.preload_act_table_set("natural_log_exp_and_others")
            with act.Fori(0, NG) as g:
                for j in range(GSUB):
                    act.wait_ge(dve_n.sem, dve_n.now(g, f"xc_{j}"))
                    act.activation(B[j][:, :], A[j][:, :], ACT.Square).then_inc(act_n.sem, act_n.step(f"sq_{j}"))
                for j in range(GSUB):
                    act.wait_ge(pe_n.sem, pe_n.now(g, f"var_{j}"))
                    act.activation(B[j][:, :], pb[j][:, :], ACT.Ln, bias=eps[:, 0:1])\
                        .then_inc(act_n.sem, act_n.step(f"ln_{j}"))
                for j in range(GSUB):
                    act.wait_ge(act_n.sem, act_n.now(g, f"ln_{j}"))
                    act.activation(B[j][:, :], B[j][:, :], ACT.Exp, scale=-0.5)\
                        .then_inc(act_n.sem, act_n.step(f"rs_{j}"))
                for j in range(GSUB):
                    act.wait_ge(dve_n.sem, dve_n.now(g, f"xh_{j}"))
                    for q in range(QS):
                        s = g * (GSUB * QS) + j * QS + q
                        a = act.activation(h_f[:, bass.ds(g * (GSUB * SUB) + j * SUB + q * SEQ, SEQ)],
                                           A[j][:, q * SEQ:(q + 1) * SEQ], ACT.Identity,
                                           scale=mod[:, layer, scale, bass.ds(s, 1)],
                                           bias=mod[:, layer, shift, bass.ds(s, 1)])
                    a.then_inc(act_n.sem, act_n.step(f"h_{j}"))

        @block.vector
        def _(dve):
            dve.sem_inc(dve_n.sem, dve_n.per)
            with dve.Fori(0, NG) as g:
                for j in range(GSUB):
                    dve.wait_ge(pe_n.sem, pe_n.now(g, f"mean_{j}"))
                    dve.wait_ge(act_n.sem, act_n.before(g, f"h_{j}"))
                    dve.tensor_tensor(A[j][:, :], x_f[:, at(g, j)], pa[j][:, :], ALU.subtract)\
                        .then_inc(dve_n.sem, dve_n.step(f"xc_{j}"))
                for j in range(GSUB):
                    dve.wait_ge(act_n.sem, act_n.now(g, f"rs_{j}"))
                    dve.tensor_tensor(A[j][:, :], A[j][:, :], B[j][:, :], ALU.mult)\
                        .then_inc(dve_n.sem, dve_n.step(f"xh_{j}"))


def attend(nc, kept, L, sem, h_f, wa, loaded, fixed):
    x_f, mod, ident = kept.x_f, kept.mod, kept.ident
    NP = NSEQ // 2
    BF = mybir.dt.bfloat16
    wqk = wa[:, A_QK:A_QK + 2 * LF]
    wtok = wa[:, A_TOK:A_TOK + PW]
    wog, wol = wa[0:GF, A_WOG:A_WOG + D], wa[0:LF + 1, A_WOL:A_WOL + D]
    caus, same = wa[:, A_CAUS:A_CAUS + 128], wa[0:GF, A_HEAD:A_HEAD + GF]
    with ExitStack() as ctx:
        def sb(name, shape, dt=F32):
            return ctx.enter_context(nc.sbuf_tensor(L + name, shape, dt))

        def two(name, shape):
            return [sb(f"{name}{p}", shape) for p in range(2)]

        idb, mask0, mask1 = sb("idb", [128, 128], BF), sb("mask0", [128, 4, 128], BF), sb("mask1", [128, 2, 256], BF)
        hs = two("hs", [128, SEQ])
        qk = two("qk", [LF, SEQ])
        kd = two("kd", [LF, NLOC, SEQ])
        tk = two("tk", [128, 2, 2 * GF])
        va = two("va", [128, 2, VW])
        qe, qm = two("qe", [128, 2, 12, DH]), two("qm", [128, 2, 12])
        kk, km = two("kk", [128, 2, GF]), two("km", [128, 2, GF])
        mx = two("mx", [128, 2, NLOC])
        P0, P1 = two("P0", [128, NLOC, 128]), two("P1", [128, NLOC, 256])
        pt = two("pt", [128, 3, NLOC, 128])
        kr, cn = two("kr", [GF, 3, 1]), two("cn", [GF, 3, GF])
        qT, og = two("qT", [GF, SEQ]), two("og", [GF, SEQ])
        rs, ol, olT = two("rs", [128, 2, NLOC, 1]), two("ol", [128, 2, NLOC, DH]), two("olT", [LF + 1, SEQ])
        S0 = [ctx.enter_context(nc.psum_tensor(f"{L}S0{p}", [128, 512], F32)) for p in range(2)]
        S1 = [ctx.enter_context(nc.psum_tensor(f"{L}S1{p}", [128, 2, 512], F32)) for p in range(2)]
        X = [ctx.enter_context(nc.psum_tensor(f"{L}X{p}", [128, 512], F32)) for p in range(2)]
        CW = GF + 1
        both = lambda kinds: [f"{k}{p}" for k in kinds for p in range(2)]
        pe_s = Steps(sem("pe_s"), both(("proj", "S", "ctx", "qT", "PT", "og", "pv", "olT", "wo")))
        act_s = Steps(sem("act_s"), [f"{k}{p}" for p in range(2) for k in ("tk", "qk", "vl", "vg")]
                      + both(("kex", "qex", "sexp", "pt", "og")))
        dve_s = Steps(sem("dve_s"), both(("kd", "kmn")) + [f"{k}{p}" for p in range(2) for k in ("qmx", "qsh")]
                      + both(("kk", "smx", "smn", "qsm", "qrc", "qn", "kr", "krc", "cn", "qT", "pt", "rrc", "ol", "olT",
                              "x")))

        pool_s = Steps(sem("pool_s"), both(("hs",)))
        made, MADE = sem("made"), 6
        block = ctx.enter_context(nc.Block())

        @block.tensor
        def _(pe):
            pe.wait_ge(made, MADE)
            pe.sem_inc(pe_s.sem, pe_s.per)
            pe.wait_ge(loaded, 16)
            pe.wait_ge(fixed, 3)
            with pe.Fori(0, NP) as i:
                for p in range(2):
                    pe.wait_ge(pool_s.sem, pool_s.now(i, f"hs{p}"))
                    pe.wait_ge(dve_s.sem, dve_s.before(i, f"x{p}"))
                    pe.matmul(S0[p][0:2 * LF, 0:SEQ], wqk, hs[p][:, :], start=True, stop=True)
                    for t in range(2):
                        mm = pe.matmul(S1[p][:, t, 0:PW], hs[p][:, t * 128:(t + 1) * 128], wtok, start=True, stop=True)
                    mm.then_inc(pe_s.sem, pe_s.step(f"proj{p}"))
                for p in range(2):
                    pe.wait_ge(act_s.sem, act_s.now(i, f"vg{p}"))
                    pe.wait_ge(dve_s.sem, dve_s.now(i, f"kd{p}"))
                    pe.matmul(S0[p][:, :], idb[:, :], mask0[:, :, :].rearrange("p a b -> p (a b)"), start=True,
                              stop=False)
                    for b in range(2):
                        pe.matmul(S1[p][:, b, :], idb[:, :], mask1[:, :, :].rearrange("p a b -> p (a b)"),
                                  start=True, stop=False)
                    pe.matmul(S0[p][:, :], qk[p][:, 0:128], kd[p][:, :, 0:128], start=False, stop=True)
                    for b in range(2):
                        mm = pe.matmul(S1[p][:, b, :], qk[p][:, 128:256],
                                       kd[p][:, 2 * b:2 * b + 2, :].rearrange("p a b -> p (a b)"),
                                       start=False, stop=True)
                    mm.then_inc(pe_s.sem, pe_s.step(f"S{p}"))
                for p in range(2):
                    pe.wait_ge(dve_s.sem, dve_s.now(i, f"kk{p}"))
                    pe.wait_ge(act_s.sem, act_s.before(i, f"og{p}"))
                    g = slice(NLOC * HV, VW)
                    pe.matmul(X[p][0:GF, 0:CW], kk[p][0:BLK, 0, :], va[p][0:BLK, 0, g], start=True, stop=True)
                    pe.matmul(X[p][0:GF, CW:2 * CW], kk[p][:, 0, :], va[p][:, 0, g], start=True, stop=True)
                    pe.matmul(X[p][0:GF, 2 * CW:3 * CW], kk[p][:, 0, :], va[p][:, 0, g], start=True, stop=False)
                    pe.matmul(X[p][0:GF, 2 * CW:3 * CW], kk[p][0:BLK, 1, :], va[p][0:BLK, 1, g], start=False,
                              stop=True).then_inc(pe_s.sem, pe_s.step(f"ctx{p}"))
                for p in range(2):
                    pe.wait_ge(dve_s.sem, dve_s.now(i, f"cn{p}"))
                    for t in range(2):
                        mm = pe.transpose(X[p][0:GF, t * 128:(t + 1) * 128],
                                          qe[p][:, t, :, :].rearrange("p h x -> p (h x)"), ident)
                    mm.then_inc(pe_s.sem, pe_s.step(f"qT{p}"))
                for p in range(2):
                    pe.wait_ge(act_s.sem, act_s.now(i, f"sexp{p}"))
                    for h in range(NLOC):
                        o = slice(h * 128, (h + 1) * 128)
                        pe.transpose(S0[p][:, o], P0[p][:, h, :], ident)
                        pe.transpose(S1[p][:, 0, o], P1[p][:, h, 0:128], ident)
                        mm = pe.transpose(S1[p][:, 1, o], P1[p][:, h, 128:256], ident)
                    mm.then_inc(pe_s.sem, pe_s.step(f"PT{p}"))
                for p in range(2):
                    pe.wait_ge(dve_s.sem, dve_s.now(i, f"qT{p}"))
                    for b in range(1, SEQ // BLK):
                        mm = pe.matmul(X[p][0:GF, b * BLK:(b + 1) * BLK], cn[p][:, b - 1, :],
                                       qT[p][:, b * BLK:(b + 1) * BLK], start=True, stop=True)
                    mm.then_inc(pe_s.sem, pe_s.step(f"og{p}"))
                for p in range(2):
                    pe.wait_ge(act_s.sem, act_s.now(i, f"pt{p}"))
                    pe.wait_ge(dve_s.sem, dve_s.now(i, f"pt{p}"))
                    for h in range(NLOC):
                        v = slice(h * HV, (h + 1) * HV)
                        pe.matmul(S0[p][:, h * HV:(h + 1) * HV], pt[p][:, 0, h, :], va[p][:, 0, v],
                                  start=True, stop=True)
                        o = slice((NLOC + h) * HV, (NLOC + h + 1) * HV)
                        pe.matmul(S0[p][:, o], pt[p][:, 1, h, :], va[p][:, 0, v], start=True, stop=False)
                        mm = pe.matmul(S0[p][:, o], pt[p][:, 2, h, :], va[p][:, 1, v], start=False, stop=True)
                    mm.then_inc(pe_s.sem, pe_s.step(f"pv{p}"))
                for p in range(2):
                    pe.wait_ge(dve_s.sem, dve_s.now(i, f"ol{p}"))
                    for t in range(2):
                        mm = pe.transpose(S0[p][0:LF, t * 128:(t + 1) * 128],
                                          ol[p][:, t, :, :].rearrange("p h x -> p (h x)"), ident)
                    mm.then_inc(pe_s.sem, pe_s.step(f"olT{p}"))
                for p in range(2):
                    pe.wait_ge(dve_s.sem, dve_s.now(i, f"olT{p}"))
                    pe.wait_ge(act_s.sem, act_s.now(i, f"og{p}"))
                    o = S0[p][:, SEQ:2 * SEQ]
                    pe.matmul(o, wog, og[p][:, :], start=True, stop=False)
                    pe.matmul(o, wol, olT[p][:, :], start=False, stop=True).then_inc(pe_s.sem, pe_s.step(f"wo{p}"))

        @block.scalar
        def _(act):
            act.sem_inc(act_s.sem, act_s.per)
            act.preload_act_table_set("natural_log_exp_and_others")
            act.wait_ge(made, MADE)
            with act.Fori(0, NP) as i:
                for p in range(2):
                    act.wait_ge(pe_s.sem, pe_s.now(i, f"proj{p}"))
                    act.wait_ge(dve_s.sem, dve_s.before(i, f"kk{p}"))
                    act.wait_ge(pe_s.sem, pe_s.before(i, f"pv{p}"))
                    act.activation(tk[p][:, :, :], S1[p][:, :, 0:2 * GF], ACT.Copy)\
                        .then_inc(act_s.sem, act_s.step(f"tk{p}"))
                    act.wait_ge(dve_s.sem, dve_s.now(i, f"kd{p}"))
                    act.activation(qk[p][:, :], S0[p][0:LF, 0:SEQ], ACT.Copy)\
                        .then_inc(act_s.sem, act_s.step(f"qk{p}"))
                    vl = va[p][:, :, 0:NLOC * HV].rearrange("p t (h x) -> p t h x", x=HV)[:, :, :, 0:DH]
                    act.activation(vl, S1[p][:, :, 2 * GF:2 * GF + LF].rearrange("p t (h x) -> p t h x", x=DH),
                                   ACT.Copy).then_inc(act_s.sem, act_s.step(f"vl{p}"))
                    act.activation(va[p][:, :, NLOC * HV:VW - 1], S1[p][:, :, 2 * GF + LF:PW], ACT.Copy)\
                        .then_inc(act_s.sem, act_s.step(f"vg{p}"))
                for p in range(2):
                    act.wait_ge(dve_s.sem, dve_s.now(i, f"kmn{p}"))
                    act.activation(km[p][:, :, :], km[p][:, :, :], ACT.Exp).then_inc(act_s.sem, act_s.step(f"kex{p}"))
                for p in range(2):
                    act.wait_ge(dve_s.sem, dve_s.now(i, f"qsh{p}"))
                    act.activation(qe[p][:, :, :, :], qe[p][:, :, :, :], ACT.Exp)\
                        .then_inc(act_s.sem, act_s.step(f"qex{p}"))
                for p in range(2):
                    act.wait_ge(dve_s.sem, dve_s.now(i, f"smn{p}"))
                    for h in range(NLOC):
                        act.activation(P0[p][:, h, :], S0[p][:, h * 128:(h + 1) * 128], ACT.Exp, scale=SCALE,
                                       bias=mx[p][:, 0, h:h + 1])
                    for h in range(NLOC):
                        a = act.activation(P1[p][:, h, :], S1[p][:, h // 2, (h % 2) * 256:(h % 2 + 1) * 256], ACT.Exp,
                                           scale=SCALE, bias=mx[p][:, 1, h:h + 1])
                    a.then_inc(act_s.sem, act_s.step(f"sexp{p}"))
                for p in range(2):
                    act.wait_ge(pe_s.sem, pe_s.now(i, f"PT{p}"))
                    for b in range(2):
                        a = act.activation(pt[p][:, b, :, :].rearrange("p h q -> p (h q)"),
                                           S0[p][:, :] if b == 0 else S1[p][:, 0, :], ACT.Copy)
                    a.then_inc(act_s.sem, act_s.step(f"pt{p}"))
                for p in range(2):
                    act.wait_ge(pe_s.sem, pe_s.now(i, f"og{p}"))
                    act.wait_ge(pe_s.sem, pe_s.before(i, f"wo{p}"))
                    act.activation(og[p][:, BLK:SEQ], X[p][0:GF, BLK:SEQ], ACT.Copy)\
                        .then_inc(act_s.sem, act_s.step(f"og{p}"))

        @block.gpsimd
        def _(pool):
            n = 0
            for p in range(2):
                for t, v in ((va[p][:, :, :], 1.0), (og[p][:, 0:BLK], 0.0), (olT[p][LF:LF + 1, :], 1.0)):
                    pool.memset(t, v).then_inc(made, 1)
                    n += 1
                    pool.wait_ge(made, n)
            pool.sem_inc(pool_s.sem, pool_s.per)
            with pool.Fori(0, NP) as i:
                for p in range(2):
                    pool.wait_ge(pe_s.sem, pe_s.before(i, f"proj{p}"))
                    pool.tensor_copy(hs[p][:, :], h_f[:, bass.ds((i * 2 + p) * SEQ, SEQ)])\
                        .then_inc(pool_s.sem, pool_s.step(f"hs{p}"))

        @block.vector
        def _(dve):
            dve.sem_inc(dve_s.sem, dve_s.per)
            dve.wait_ge(loaded, 16)
            dve.wait_ge(made, MADE)
            dve.tensor_copy(idb[:, :], ident).then_inc(fixed, 1)
            dve.tensor_copy(mask0[:, :, :],
                            caus.rearrange("p (a b) -> p a b", a=1).to_broadcast([128, NLOC, 128]))\
                .then_inc(fixed, 1)
            dve.memset(mask1[:, :, 0:128], 0.0)
            dve.tensor_copy(mask1[:, :, 128:256],
                            caus.rearrange("p (a b) -> p a b", a=1).to_broadcast([128, 2, 128])).then_inc(fixed, 1)
            with dve.Fori(0, NP) as i:
                def tok(p, at, n):
                    return tk[p][:, :, at:at + n]

                def heads(t):
                    return t.rearrange("p t (h x) -> p t h x", x=DH)

                def wide(t, n):
                    return t.rearrange("p t (h x) -> p t h x", x=1).to_broadcast([128, 2, 12, n])

                def done(name, ins):
                    ins.then_inc(dve_s.sem, dve_s.step(name))

                def after(name):
                    dve.wait_ge(dve_s.sem, dve_s.now(i, name))

                for p in range(2):
                    dve.wait_ge(pe_s.sem, pe_s.now(i, f"proj{p}"))
                    done(f"kd{p}", dve.tensor_tensor(
                        kd[p][:, :, :],
                        S0[p][LF:2 * LF, 0:SEQ].rearrange("p (a t) -> p a t", a=1).to_broadcast([LF, NLOC, SEQ]),
                        wa[LF:2 * LF, A_ROWS:A_ROWS + NLOC].rearrange("p (a t) -> p a t", t=1)
                        .to_broadcast([LF, NLOC, SEQ]), ALU.mult))
                for p in range(2):
                    dve.wait_ge(act_s.sem, act_s.now(i, f"tk{p}"))
                    done(f"kmn{p}", dve.tensor_scalar(km[p][:, :, :], tok(p, GF, GF), 0.0, None, ALU.min))
                for p in range(2):
                    done(f"qmx{p}", dve.tensor_reduce(qm[p][:, :, :], heads(tok(p, 0, GF)), AX.X, ALU.max))
                    after(f"qmx{p}")
                    done(f"qsh{p}", dve.tensor_tensor(qe[p][:, :, :, :], heads(tok(p, 0, GF)),
                                                      wide(qm[p][:, :, :], DH), ALU.subtract))
                for p in range(2):
                    dve.wait_ge(act_s.sem, act_s.now(i, f"kex{p}"))
                    done(f"kk{p}", dve.scalar_tensor_tensor(kk[p][:, :, :], tok(p, GF, GF), 0.0, km[p][:, :, :],
                                                            ALU.max, ALU.add))
                for p in range(2):
                    dve.wait_ge(pe_s.sem, pe_s.now(i, f"S{p}"))
                    dve.tensor_reduce(mx[p][:, 0, :], S0[p][:, :].rearrange("p (h k) -> p h k", h=NLOC), AX.X,
                                      ALU.max)
                    done(f"smx{p}", dve.tensor_reduce(
                        mx[p][:, 1, :], S1[p][:, :, :].rearrange("p b (h k) -> p (b h) k", h=2), AX.X, ALU.max))
                for p in range(2):
                    after(f"smx{p}")
                    done(f"smn{p}", dve.tensor_scalar(mx[p][:, :, :], mx[p][:, :, :], -SCALE, None, ALU.mult))
                for p in range(2):
                    dve.wait_ge(act_s.sem, act_s.now(i, f"qex{p}"))
                    done(f"qsm{p}", dve.tensor_reduce(qm[p][:, :, :], qe[p][:, :, :, :], AX.X, ALU.add))
                for p in range(2):
                    after(f"qsm{p}")
                    done(f"qrc{p}", dve.reciprocal(qm[p][:, :, :], qm[p][:, :, :]))
                for p in range(2):
                    after(f"qrc{p}")
                    done(f"qn{p}", dve.tensor_tensor(qe[p][:, :, :, :], qe[p][:, :, :, :], wide(qm[p][:, :, :], DH),
                                                     ALU.mult))
                for p in range(2):
                    dve.wait_ge(pe_s.sem, pe_s.now(i, f"ctx{p}"))
                    c = X[p][0:GF, 0:3 * CW].rearrange("p (b e) -> p b e", e=CW)
                    done(f"kr{p}", dve.tensor_scalar(kr[p][:, :, :], c[:, :, GF:CW], 1e-6, None, ALU.add))
                for p in range(2):
                    after(f"kr{p}")
                    done(f"krc{p}", dve.reciprocal(kr[p][:, :, :], kr[p][:, :, :]))
                for p in range(2):
                    after(f"krc{p}")
                    for b in range(3):
                        v = dve.scalar_tensor_tensor(cn[p][:, b, :], X[p][0:GF, b * CW:b * CW + GF],
                                                     kr[p][:, b, :], same, ALU.mult, ALU.mult)
                    done(f"cn{p}", v)
                for p in range(2):
                    dve.wait_ge(pe_s.sem, pe_s.now(i, f"qT{p}"))
                    done(f"qT{p}", dve.tensor_copy(qT[p][:, :], X[p][0:GF, 0:SEQ]))
                for p in range(2):
                    dve.wait_ge(pe_s.sem, pe_s.now(i, f"PT{p}"))
                    done(f"pt{p}", dve.tensor_copy(pt[p][:, 2, :, :].rearrange("p h q -> p (h q)"), S1[p][:, 1, :]))
                for p in range(2):
                    dve.wait_ge(pe_s.sem, pe_s.now(i, f"pv{p}"))
                    o = S0[p][:, 0:2 * NLOC * HV].rearrange("p (t h x) -> p t h x", t=2, x=HV)
                    done(f"rrc{p}", dve.reciprocal(rs[p][:, :, :, :], o[:, :, :, DH:HV]))
                for p in range(2):
                    o = S0[p][:, 0:2 * NLOC * HV].rearrange("p (t h x) -> p t h x", t=2, x=HV)
                    after(f"rrc{p}")
                    done(f"ol{p}", dve.tensor_tensor(ol[p][:, :, :, :], o[:, :, :, 0:DH],
                                                     rs[p][:, :, :, :].to_broadcast([128, 2, NLOC, DH]), ALU.mult))
                for p in range(2):
                    dve.wait_ge(pe_s.sem, pe_s.now(i, f"olT{p}"))
                    done(f"olT{p}", dve.tensor_copy(olT[p][0:LF, :], S0[p][0:LF, 0:SEQ]))
                for p in range(2):
                    dve.wait_ge(pe_s.sem, pe_s.now(i, f"wo{p}"))
                    xq = x_f[:, bass.ds((i * 2 + p) * SEQ, SEQ)]
                    done(f"x{p}", dve.scalar_tensor_tensor(xq, S0[p][:, SEQ:2 * SEQ],
                                                           mod[:, 1, GA, bass.ds(i * 2 + p, 1)], xq,
                                                           ALU.mult, ALU.add))


def pack(i):
    f = {k: np.asarray(v) for k, v in i.items()}
    xT = np.ascontiguousarray(f["L0_attn_inputs"].reshape(TOK, D).T)
    eye = np.eye(128, dtype=np.float32)
    sel = np.zeros((128, 32), np.float32)
    sel[64:96], sel[96:128] = np.eye(32), np.eye(32)
    consts = np.concatenate([eye, np.full((128, 128), 1 / 128, np.float32), sel], axis=1)

    def pad(v):
        return np.concatenate([v, np.zeros(128 - len(v), np.float32)]) if len(v) < 128 else v

    a = "L0_attn_"
    cols = [f[a + n] for n in ("gamma", "beta", "b_proj", "b_fc", "b_bc", "b_dt1", "b_dt2", "D1", "D2")]
    cols += [pad(f[a + "b_x1"]), pad(f[a + "b_x2"])]
    vec = np.concatenate([np.stack(cols, 1), f[a + "A_log1"], f[a + "A_log2"], f["L0_c"].T, f["L1_c"].T], axis=1)
    wpk = np.concatenate([f[a + n] for n in ("W_proj", "W_fc", "W_bc", "W_x1", "W_x2")], axis=1)
    wdt = np.concatenate([f[a + "W_dt1"], f[a + "W_dt2"]], axis=1)
    wmod = np.stack([f["L0_wmod"], f["L1_wmod"]], 1)
    m0 = {"wg": f["L0_ffn_Wg"].T, "gb": np.zeros((128, NE), np.float32), "b1": f["L0_ffn_b1"], "w1": f["L0_ffn_W1"],
          "w2": f["L0_ffn_W2"], "b2": f["L0_ffn_b2"]}
    m1 = {"wg": f["L1_ffn_gate_w"], "gb": np.tile(f["L1_ffn_gate_b"], (128, 1)), "b1": f["L1_ffn_b1"],
          "w1": f["L1_ffn_w1"], "w2": f["L1_ffn_w2"], "b2": f["L1_ffn_b2"]}
    fcols = []
    for m in (m0, m1):
        fcols += [m["wg"], m["gb"]]
    fcols += [f["L0_ffn_gamma"][:, None], f["L0_ffn_beta"][:, None]]
    p = np.arange(128)[:, None]
    rconst = np.concatenate([p < p.T, np.ones((128, 128)), np.tile(np.arange(NJT), (128, 1)),
                             np.tile(np.arange(NE) * CAPT * 128, (128, 1)), p + 128 * np.arange(GT)[None], p,
                             np.full((128, 1), AWAY), np.tile(np.arange(NE, 0, -1), (128, 1))], axis=1)
    packed = {"xT": xT, "consts": consts, "vec": vec, "wpk": wpk, "wdt": wdt, "wmod": wmod,
              "rconst": rconst.astype(np.float32), "fvec": np.concatenate(fcols, axis=1)}
    for l, m in enumerate((m0, m1)):
        packed[f"wexp{l}"] = np.concatenate(
            [m["w1"].transpose(1, 0, 2), m["b1"].reshape(NE, NF, 128).transpose(2, 0, 1),
             m["w2"].reshape(NE, NF, 128, D).transpose(2, 0, 1, 3).reshape(128, NE, NF * D),
             np.broadcast_to(m["b2"][None], (128, NE, D))], axis=2).reshape(128, NE * EW)
    wq, wk, wv, wo = (f["L1_attn_" + n] for n in ("Wq", "Wk", "Wv", "Wo"))
    wat = np.zeros((128, A_END), np.float32)
    wat[:, A_QK:A_QK + LF], wat[:, A_QK + LF:A_QK + 2 * LF] = wq[:, :LF], wk[:, :LF]
    wat[LF:2 * LF, A_ROWS:A_ROWS + NLOC] = np.kron(np.eye(NLOC), np.ones((DH, 1)))
    wat[:, A_TOK:A_TOK + PW] = np.concatenate([wq[:, LF:], wk[:, LF:], wv], axis=1)
    wat[0:GF, A_WOG:A_WOG + D] = wo[LF:]
    wat[0:LF, A_WOL:A_WOL + D] = wo[:LF]
    wat[LF, A_WOL:A_WOL + D] = f["L1_attn_bo"]
    wat[:, A_CAUS:A_CAUS + 128] = np.where(np.tril(np.ones((128, 128), bool)), 0, -3e38)
    wat[0:GF, A_HEAD:A_HEAD + GF] = np.kron(np.eye(12), np.ones((DH, DH)))
    packed["wat"] = wat
    return {k: np.ascontiguousarray(v, dtype=np.float32) for k, v in packed.items()}


_OUT = (D, TOK)


def kernel(**inputs):
    import concourse.bacc as bacc
    from concourse.bass_utils import run_bass_kernel_spmd

    nc = bacc.Bacc("TRN2", target_bir_lowering=False, num_devices=1)
    packed = pack(inputs)
    args = [nc.dram_tensor(k, v.shape, mybir.dt.from_np(v.dtype), kind="ExternalInput").ap()
            for k, v in packed.items()]
    out = nc.dram_tensor("out_0_dram", _OUT, F32, kind="ExternalOutput").ap()
    build(nc, *args, out)
    r = run_bass_kernel_spmd(nc, [packed], core_ids=[0])
    return np.ascontiguousarray(r.results[0]["out_0_dram"].T).reshape(NSEQ, SEQ, D)
```

```python
from contextlib import ExitStack

import numpy as np

import concourse.bass as bass
from concourse import mybir

F32 = mybir.dt.float32
F32R = mybir.dt.float32r
ALU = mybir.AluOpType
ACT = mybir.ActivationFunctionType
AX = mybir.AxisListType

D = 128
NSEQ, SEQ = 32, 256
TOK = NSEQ * SEQ
R, NS = 64, 16
CH = 512
NCH = TOK // CH
SPC = CH // SEQ
HB = 512
SA, CA, GA, SB, CB, GB = range(6)

C_ID, C_AVG, C_SEL = 0, 128, 256
C_END = 288
(V_GAM, V_BET, V_BPROJ, V_BFC, V_BBC, V_BDT1, V_BDT2, V_D1, V_D2, V_BX1, V_BX2) = range(11)
V_ALOG = 11
V_CT = V_ALOG + 2 * NS
V_END = V_CT + 2 * NSEQ
W_PROJ, W_FC, W_BC, W_X1, W_X2 = 0, 128, 256, 384, 480
W_END = 576


class Steps:

    def __init__(self, sem, names, rounds=1):
        self.sem, self.names, self.per, self.at = sem, list(names), len(names), 0
        self.rounds = rounds
        self.index = {n: i + 1 for i, n in enumerate(self.names)}
        assert len(self.index) == self.per, "two steps of one name"

    def step(self, name):
        assert self.names[self.at % self.per] == name, (self.names[self.at % self.per], name)
        self.at += 1
        return 1

    def now(self, c, name):
        return (c + self.rounds) * self.per + self.index[name]

    def two_before(self, c, name):
        return c * self.per + self.index[name]

    def before(self, c, name):
        return c * self.per + self.index[name]

    def at0(self, name):
        return self.index[name]


PE_1 = {"mean1": 6, "var1": 13, "mean2": 18, "var2": 21}
PE_2 = {"proj": 0, "fc": 2, "bc": 4, "x1": 9, "wdt1": 11, "x2": 15, "wdt2": 16}
ACT_1 = {"sq1": 9, "ln1": 15, "rs1": 15, "h0": 17, "h1": 17, "sq2": 22, "ln2": 24, "rs2": 24, "xn": 27}
ACT_2 = {"pj": 2, "vu1": 4, "au1": 4, "eu1": 5, "lu1": 5, "vu2": 6, "au2": 6, "eu2": 7, "lu2": 7, "ez": 8, "lz": 10,
         "sz": 10, "dbc1": 11, "bh1": 11, "vd1": 13, "ad1": 13, "ed1": 14, "ld1": 14, "dbc2": 17, "bh2": 17,
         "vd2": 19, "ad2": 19, "ed2": 20, "ld2": 20}
DVE_1 = {"xc": 8, "xg0": 20, "xg1": 20, "hc": 21}
DVE_2 = {"mz": 3, "tu1": 6, "tu2": 8, "u1": 10, "bl1": 12, "u2": 13, "td1": 15, "d1": 17, "bl2": 18, "td2": 21,
         "d2": 24}
POOL_1 = {"xh": 16, "hn": 24}
POOL_2 = {"cu1": 7, "su1": 7, "cu2": 9, "su2": 9, "ud1": 11, "z": 11, "ud2": 13, "acc": 13, "cd1": 15, "sd1": 15,
          "du1": 18, "cd2": 21, "sd2": 21, "du2": 25}
READER = {"mean1": "xc", "var1": "ln1", "mean2": "hc", "var2": "ln2", "proj": "pj", "fc": "vu1", "bc": "vu2",
          "x1": "bh1", "wdt1": "vd1", "x2": "bh2", "wdt2": "vd2"}
NK = 2 * NS
RB = 3
POOL_B = [k for k in range(NK) if k % 2 == 1]


class Kept:

    def __init__(self, nc, ctx):
        def sb(name, shape, dt=F32):
            return ctx.enter_context(nc.sbuf_tensor(name, shape, dt))

        self.sem = lambda name: ctx.enter_context(nc.semaphore(name))
        self.x_f = sb("x_f", [D, TOK])
        self.cst = sb("cst", [128, C_END])
        self.mod = sb("mod", [128, 2, 6, NSEQ])
        self.eps = sb("eps", [128, 2])
        self.ident, self.avg = self.cst[:, C_ID:C_ID + 128], self.cst[:, C_AVG:C_AVG + 128]


def build(nc, xT, consts, vec, wpk, wdt, wmod, rconst, fvec, wexp0, wexp1, wat, out):
    with ExitStack() as ctx:
        kept = Kept(nc, ctx)
        ssm_layer(nc, kept, xT, consts, vec, wpk, wdt, wmod)
        routed = nc.dram_tensor("routed", (ROWS, RW), F32, kind="Internal").ap()
        results = nc.dram_tensor("results", (2 * TOK, D), F32, kind="Internal").ap()
        mixture_layer(nc, kept, 0, rconst, fvec, wexp0, routed, results)
        attention_layer(nc, kept, wat)
        mixture_layer(nc, kept, 1, rconst, fvec, wexp1, routed, results, out)


def ssm_layer(nc, kept, xT, consts, vec, wpk, wdt, wmod):
    with ExitStack() as ctx:
        def sb(name, shape, dt=F32):
            return ctx.enter_context(nc.sbuf_tensor(name, shape, dt))

        def ps(name, shape):
            return ctx.enter_context(nc.psum_tensor(name, shape, F32))

        sem, x_f, cst, mod, eps, ident, avg = (kept.sem, kept.x_f, kept.cst, kept.mod, kept.eps, kept.ident,
                                               kept.avg)
        vecs = sb("vecs", [128, V_END])
        w = sb("w", [128, W_END])
        wd = sb("wd", [R, 2 * D])
        sel = sb("sel", [128, 32], F32R)
        msc = sb("msc", [128, 4, 2 * NSEQ])
        negA = sb("negA", [128, 2 * NS])

        def col(v, p=128):
            return vecs[0:p, v:v + 1]

        def two(name, shape=(128, CH), dt=F32):
            return [sb(f"{name}{i}", list(shape), dt) for i in range(2)]

        z_, acc_ = two("z"), two("acc")
        delta_ = [two("delta1"), two("delta2")]
        du_ = [two("du1"), two("du2")]
        bcs_ = [two("bcs1", (128, CH), F32R), two("bcs2", (128, CH), F32R)]
        def ring(name, n=RB):
            return [sb(f"{name}{i}", [128, CH]) for i in range(n)]

        dA, dB, hs, hC, Bc = ring("dA"), ring("dB"), ring("hs"), ring("hC"), ring("Bc", 2)
        A0, A1, H = sb("A0", [128, CH]), sb("A1", [128, CH]), sb("H", [128, CH])
        XN, PJ = sb("XN", [128, CH]), sb("PJ", [128, CH])
        Pv = two("Pv")
        Pe = two("Pe")
        Pl = two("Pl")
        Pt = two("Pt")
        wm = [sb(f"wm{l}", [128, 6 * D]) for l in range(2)]
        Q = sb("Q", [128, CH])
        U = [sb("U1", [128, CH]), sb("U2", [128, CH])]
        dbc = sb("dbc", [R + 2 * NS, CH])

        py, pB, pC = ps("py", [128, CH]), [ps(f"pB{i}", [128, CH]) for i in range(RB)], \
            [ps(f"pC{i}", [128, CH]) for i in range(2)]
        pP_1, pP_2 = ps("pP_1", [128, CH]), ps("pP_2", [128, CH])

        ld0, ldc, ldx = sem("ld0"), sem("ldc"), sem("ldx")
        set_pe, set_act, set_dve, set_pool = sem("set_pe"), sem("set_act"), sem("set_dve"), sem("set_pool")
        pe_1, act_1, dve_1, pool_1 = (Steps(sem(n), t) for n, t in
                                      (("pe_1", PE_1), ("act_1", ACT_1), ("dve_1", DVE_1), ("pool_1", POOL_1)))
        pe_2, act_2, dve_2, pool_2 = (Steps(sem(n), t) for n, t in
                                      (("pe_2", PE_2), ("act_2", ACT_2), ("dve_2", DVE_2), ("pool_2", POOL_2)))
        pe_names = ["B0", "C0", "B1", "B2"]
        for k in range(NK):
            pe_names += ([f"B{k + 3}"] if k + 3 < NK else []) + ([f"C{k + 1}"] if k + 1 < NK else [])
            pe_names += [f"y{k - 1}"] if k else []
        pe_s = Steps(sem("pe_s"), pe_names + [f"y{NK - 1}"])
        act_names = ["e0", "e1", "b1"]
        for k in range(NK - 2):
            act_names += [f"e{k + 2}"] + ([f"b{k + 2}"] if k + 2 in POOL_B else [])
        act_s = Steps(sem("act_s"), act_names)
        dve_names = ["b0"]
        for k in range(NK):
            dve_names += [f"s{k}"] + ([f"b{k + 1}"] if k + 1 < NK and k + 1 not in POOL_B else [])
            dve_names += [f"c{k - 1}"] if k else []
        dve_names += [f"c{NK - 1}"]
        dve_names += ["y0", "y1"] + [f"x{q}" for q in range(SPC)]
        dve_s = Steps(sem("dve_s"), dve_names)
        pool_s = Steps(sem("pool_s"), [f"b{k}" for k in POOL_B])

        block = ctx.enter_context(nc.Block())

        def used(S, c, name, k, n=RB):
            if k >= n:
                return S.now(c, f"{name}{k - n}")
            return S.before(c, f"{name}{max(j for j in range(NK) if j % n == k % n)}")

        def woven(k, c, with_2, with_1, steps_2, steps_1, step_2, step_1):
            for name, at in steps_2.items():
                if with_2 and at == k:
                    step_2(name, c + 1)
            for name, at in steps_1.items():
                if with_1 and at == k:
                    step_1(name, c + 2)

        def rounds(eng, steps_2, steps_1, step_2, step_1, states, at_loop=lambda c: None):
            for name in steps_1:
                step_1(name, 0)
            for name in steps_2:
                step_2(name, 0, 0)
            for name in steps_1:
                step_1(name, 1)
            with eng.Fori(0, NCH // 2 - 1) as i:
                at_loop(i * 2)
                for p in range(2):
                    states(i * 2 + p, p, True, True)
            states(NCH - 2, 0, True, False)
            states(NCH - 1, 1, False, False)

        @block.sync
        def _(sp):
            sp.dma_start(cst[:, :], consts).then_inc(ldc, 16)
            sp.dma_start(vecs[:, :], vec).then_inc(ldc, 16)
            for l in range(2):
                sp.dma_start(wm[l][:, :], wmod[:, l, :]).then_inc(ldc, 16)
            sp.dma_start(x_f[:, 0:CH], xT[:, 0:CH]).then_inc(ld0, 16)
            sp.dma_start(w[:, :], wpk).then_inc(ldc, 16)
            sp.dma_start(wd[:, :], wdt).then_inc(ldc, 16)
            sp.dma_start(x_f[:, CH:TOK], xT[:, CH:TOK]).then_inc(ldx, 16)

        @block.tensor
        def _(pe):
            for s in (pe_1, pe_2, pe_s):
                pe.sem_inc(s.sem, s.per)
            pe.wait_ge(ldc, 96)
            pe.wait_ge(set_dve, 3)
            for l in range(2):
                for j in range(6):
                    at = (l * 6 + j) * NSEQ
                    mm = pe.matmul(pP_1[:, at:at + NSEQ], wm[l][:, j * D:(j + 1) * D],
                                   msc[:, 3, l * NSEQ:(l + 1) * NSEQ], start=True, stop=True)
            mm.then_inc(set_pe, 1)

            def full(dst, lhsT, rhs, name, m=128, start=True, stop=True, S=None):
                for q in range(CH // HB):
                    mm = pe.matmul(dst[0:m, q * HB:(q + 1) * HB], lhsT, rhs(q), start=start, stop=stop)
                mm.then_inc(S.sem, S.step(name))

            def half(t):
                return lambda q: t[:, q * HB:(q + 1) * HB]

            reader = [(act_1, 0, None), (act_2, 0, None)]

            def free_pP(n):
                S, c, name = reader[n - 1]
                if name:
                    pe.wait_ge(S.sem, S.now(c, name))

            def step_1(name, c):
                free_pP(1)
                if name == "mean1":
                    if isinstance(c, int) and c == 0:
                        pe.wait_ge(ld0, 16)
                        pe.wait_ge(set_dve, 4)
                    else:
                        pe.wait_ge(ldx, 16)
                    full(pP_1, avg, lambda q: x_f[:, bass.ds(c * CH + q * HB, HB)], name, S=pe_1)
                elif name == "mean2":
                    pe.wait_ge(act_1.sem, act_1.now(c, f"h{SPC - 1}"))
                    full(pP_1, avg, half(H), name, S=pe_1)
                else:
                    pe.wait_ge(act_1.sem, act_1.now(c, f"sq{name[3]}"))
                    full(pP_1, avg, half(A1), name, S=pe_1)
                reader[0] = (dve_1 if name[0] == "m" else act_1, c, READER[name])

            def step_2(name, c, p=0):
                free_pP(2)
                if name == "proj":
                    pe.wait_ge(act_1.sem, act_1.now(c, "xn"))
                    full(pP_2, w[:, W_PROJ:W_PROJ + D], half(XN), name, S=pe_2)
                elif name in ("fc", "bc"):
                    at = {"fc": W_FC, "bc": W_BC}[name]
                    pe.wait_ge(act_2.sem, act_2.now(c, "pj"))
                    full(pP_2, w[:, at:at + D], half(PJ), name, S=pe_2)
                elif name[0] == "x":
                    s = int(name[1]) - 1
                    at = (W_X1, W_X2)[s]
                    pe.wait_ge(dve_2.sem, dve_2.now(c, f"u{s + 1}"))
                    full(pP_2, w[:, at:at + R + 2 * NS], half(U[s]), name, m=R + 2 * NS, S=pe_2)
                else:
                    s = int(name[3]) - 1
                    pe.wait_ge(act_2.sem, act_2.now(c, f"dbc{s + 1}"))
                    full(pP_2, wd[:, s * D:(s + 1) * D], lambda q: dbc[0:R, q * HB:(q + 1) * HB], name, S=pe_2)
                reader[1] = (act_2, c, READER[name])

            def spread(dst, k, is_c, p, name):
                row = (k % NS) + (NS if is_c else 0)
                rows = bcs_[k // NS][p]
                full(dst, sel[64:128, row:row + 1].to_broadcast([64, 128]),
                     lambda q: rows[64:128, q * HB:(q + 1) * HB], name, S=pe_s)

            def spread_B(k, c, p):
                of = k - RB if k >= RB else max(j for j in range(NK) if j % RB == k % RB)
                S = act_s if of in POOL_B else dve_s
                pe.wait_ge(S.sem, used(S, c, "b", k))
                spread(pB[k % RB], k, False, p, f"B{k}")

            def spread_C(k, c, p):
                pe.wait_ge(dve_s.sem, used(dve_s, c, "c", k, 2))
                spread(pC[k % 2], k, True, p, f"C{k}")

            def add_y(k, c):
                pe.wait_ge(dve_s.sem, dve_s.now(c, f"c{k}"))
                if k == 0:
                    pe.wait_ge(dve_s.sem, dve_s.before(c, "y0"))
                full(py, ident, half(hC[k % RB]), f"y{k}", start=k == 0, stop=k == NK - 1, S=pe_s)

            def states(c, p, with_2, with_1):
                pe.wait_ge(dve_2.sem, dve_2.now(c, "bl2"))
                spread_B(0, c, p)
                spread_C(0, c, p)
                spread_B(1, c, p)
                spread_B(2, c, p)
                for k in range(NK):
                    if k + 3 < NK:
                        spread_B(k + 3, c, p)
                    if k + 1 < NK:
                        spread_C(k + 1, c, p)
                    if k:
                        add_y(k - 1, c)
                    woven(k, c, with_2, with_1, PE_2, PE_1, step_2, step_1)
                add_y(NK - 1, c)

            def at_loop(c):
                free_pP(1)
                free_pP(2)
                reader[0] = (act_1, c + 1, READER["var2"])
                reader[1] = (act_2, c, READER["wdt2"])

            rounds(pe, PE_2, PE_1, step_2, step_1, states, at_loop)

        @block.scalar
        def _(act):
            for s in (act_1, act_2, act_s):
                act.sem_inc(s.sem, s.per)
            act.preload_act_table_set("natural_log_exp_and_others")
            act.wait_ge(set_dve, 1)
            act.activation(msc[:, 1, :], msc[:, 0, :], ACT.Exp).then_inc(set_act, 1)
            act.wait_ge(set_act, 1)
            act.activation(msc[:, 2, :], msc[:, 1, :], ACT.Ln, bias=1.0).then_inc(set_act, 1)
            act.wait_ge(set_act, 2)
            act.activation(msc[:, 1, :], msc[:, 2, :], ACT.Exp, scale=-1.0).then_inc(set_act, 1)
            act.activation(negA[:, :], vecs[:, V_ALOG:V_ALOG + 2 * NS], ACT.Exp).then_inc(set_act, 1)
            act.wait_ge(set_act, 4)
            act.mul(negA[:, :], negA[:, :], -1.0).then_inc(set_act, 1)

            act.wait_ge(set_dve, 7)
            act.wait_ge(set_pool, 2 + RB)

            def do(dst, src, f, name, S, **kw):
                act.activation(dst, src, f, **kw).then_inc(S.sem, S.step(name))

            def step_1(name, c):
                if name == "sq1":
                    act.wait_ge(dve_1.sem, dve_1.now(c, "xc"))
                    act.wait_ge(pool_1.sem, pool_1.before(c, "hn"))
                    do(A1[:, :], A0[:, :], ACT.Square, name, act_1)
                elif name == "sq2":
                    act.wait_ge(dve_1.sem, dve_1.now(c, "hc"))
                    do(A1[:, :], A0[:, :], ACT.Square, name, act_1)
                elif name in ("ln1", "ln2"):
                    act.wait_ge(pe_1.sem, pe_1.now(c, f"var{name[2]}"))
                    do(A1[:, :], pP_1[:, :], ACT.Ln, name, act_1, bias=eps[:, int(name[2]) - 1:int(name[2])])
                elif name in ("rs1", "rs2"):
                    act.wait_ge(act_1.sem, act_1.now(c, f"ln{name[2]}"))
                    do(A1[:, :], A1[:, :], ACT.Exp, name, act_1, scale=-0.5)
                elif name == "xn":
                    act.wait_ge(pool_1.sem, pool_1.now(c, "hn"))
                    act.wait_ge(pe_2.sem, pe_2.before(c, "proj"))
                    do(XN[:, :], A0[:, :], ACT.Identity, name, act_1, scale=col(V_GAM), bias=col(V_BET))
                else:
                    q = int(name[1])
                    act.wait_ge(pool_1.sem, pool_1.now(c, "xh"))
                    act.wait_ge(dve_1.sem, dve_1.before(c, "hc"))
                    b = c * SPC + q
                    do(H[:, q * SEQ:(q + 1) * SEQ], A0[:, q * SEQ:(q + 1) * SEQ], ACT.Identity, name, act_1,
                       scale=mod[:, 0, CA, bass.ds(b, 1)], bias=mod[:, 0, SA, bass.ds(b, 1)])

            def step_2(name, c, p):
                if name == "pj":
                    act.wait_ge(pe_2.sem, pe_2.now(c, "proj"))
                    act.wait_ge(pe_2.sem, pe_2.before(c, "bc"))
                    act.wait_ge(pool_2.sem, pool_2.before(c, "z"))
                    do(PJ[:, :], pP_2[:, :], ACT.Identity, name, act_2, bias=col(V_BPROJ))
                elif name in ("ez", "lz", "sz"):
                    z = z_[p][:, :]
                    if name == "ez":
                        act.wait_ge(dve_2.sem, dve_2.now(c, "mz"))
                        do(z, z, ACT.Exp, name, act_2, scale=-1.0)
                    elif name == "lz":
                        act.wait_ge(act_2.sem, act_2.now(c, "ez"))
                        do(z, z, ACT.Ln, name, act_2, bias=1.0)
                    else:
                        act.wait_ge(act_2.sem, act_2.now(c, "lz"))
                        do(z, z, ACT.Exp, name, act_2, scale=-1.0)
                elif name.startswith("dbc"):
                    s = int(name[3]) - 1
                    act.wait_ge(pe_2.sem, pe_2.now(c, f"x{s + 1}"))
                    act.wait_ge(dve_2.sem, dve_2.before(c, "bl2") if s == 0 else dve_2.now(c, "bl1"))
                    do(dbc[:, :], pP_2[0:R + 2 * NS, :], ACT.Identity, name, act_2, bias=col(V_BX1 + s, R + 2 * NS))
                elif name in ("bh1", "bh2"):
                    s = int(name[2]) - 1
                    do(bcs_[s][p][64:96, :], pP_2[R:R + 2 * NS, :], ACT.Identity, name, act_2,
                       bias=vecs[R:R + 2 * NS, V_BX1 + s:V_BX1 + s + 1])
                else:
                    kind, which, s = name[0], name[1], int(name[2]) - 1
                    v, e, l = Pv[s], Pe[s], Pl[s]
                    if kind == "v":
                        b = {"u": V_BFC, "d": V_BDT1}[which] + s
                        act.wait_ge(pe_2.sem, pe_2.now(c, {"u": ("fc", "bc")[s], "d": f"wdt{s + 1}"}[which]))
                        if which == "u":
                            act.wait_ge(dve_2.sem, dve_2.before(c, f"d{s + 1}"))
                        else:
                            act.wait_ge(dve_2.sem, dve_2.now(c, f"u{s + 1}"))
                        do(v[:, :], pP_2[:, :], ACT.Identity, name, act_2, bias=col(b))
                    elif kind == "a":
                        act.wait_ge(act_2.sem, act_2.now(c, f"v{which}{s + 1}"))
                        do(e[:, :], v[:, :], ACT.Abs, name, act_2)
                    elif kind == "e":
                        act.wait_ge(act_2.sem, act_2.now(c, f"a{which}{s + 1}"))
                        do(e[:, :], e[:, :], ACT.Exp, name, act_2, scale=-1.0)
                    else:
                        act.wait_ge(act_2.sem, act_2.now(c, f"e{which}{s + 1}"))
                        do(l[:, :], e[:, :], ACT.Ln, name, act_2, bias=1.0)

            def later(t):
                return t.rearrange("p (s t) -> p s t", t=SEQ)[:, :, 1:SEQ]

            def states(c, p, with_2, with_1):
                def decay(k):
                    act.wait_ge(dve_s.sem, used(dve_s, c, "s", k))
                    if k == 0:
                        act.wait_ge(dve_2.sem, dve_2.now(c, "d2"))
                    do(later(dA[k % RB][:, :]), later(delta_[k // NS][p][:, :]), ACT.Exp, f"e{k}", act_s,
                       scale=negA[:, k:k + 1])

                def copy_B(k):
                    n = POOL_B.index(k)
                    act.wait_ge(pe_s.sem, pe_s.now(c, f"B{k}"))
                    act.wait_ge(pool_s.sem, pool_s.now(c, f"b{POOL_B[n - 2]}") if n >= 2
                                else pool_s.before(c, f"b{POOL_B[n - 2]}"))
                    do(Bc[n % 2][:, :], pB[k % RB][:, :], ACT.Copy, f"b{k}", act_s)

                decay(0)
                decay(1)
                copy_B(1)
                for k in range(NK):
                    if k + 2 < NK:
                        decay(k + 2)
                        if k + 2 in POOL_B:
                            copy_B(k + 2)
                    woven(k, c, with_2, with_1, ACT_2, ACT_1, lambda n, cc: step_2(n, cc, 1 - p), step_1)

            rounds(act, ACT_2, ACT_1, step_2, step_1, states)

        @block.vector
        def _(dve):
            for s in (dve_1, dve_2, dve_s):
                dve.sem_inc(s.sem, s.per)
            dve.wait_ge(ldc, 96)
            dve.tensor_scalar(msc[:, 0, :], vecs[:, V_CT:V_END], -1.0, 44.0, ALU.mult, ALU.min).then_inc(set_dve, 1)
            dve.tensor_copy(sel[64:128, :], cst[64:128, C_SEL:C_SEL + 32]).then_inc(set_dve, 1)
            dve.wait_ge(set_act, 3)
            dve.tensor_tensor(msc[:, 3, :], vecs[:, V_CT:V_END], msc[:, 1, :], ALU.mult).then_inc(set_dve, 1)
            dve.wait_ge(set_pe, 1)
            mflat = mod[:, :, :, :].rearrange("p l j b -> p (l j b)")
            dve.tensor_copy(mflat, pP_1[:, 0:12 * NSEQ]).then_inc(set_dve, 1)
            dve.wait_ge(set_dve, 4)
            for l in range(2):
                for j in (CA, CB):
                    m = mod[:, l, j, :]
                    last = dve.tensor_scalar(m, m, 1.0, None, ALU.add)
            for l in range(2):
                for n, j in enumerate((GA, GB)):
                    o = slice(n * NSEQ, (n + 1) * NSEQ)
                    dve.tensor_scalar(msc[:, l, o], mod[:, l, j, :], 0.0, 2.0, ALU.is_ge, ALU.mult)
                    last = dve.scalar_tensor_tensor(msc[:, 2 + l, o], mod[:, l, j, :], -1.0, mod[:, l, j, :],
                                                    ALU.mult, ALU.max)
            last.then_inc(set_dve, 1)
            dve.wait_ge(set_dve, 5)
            dve.tensor_scalar(msc[:, 2:4, :], msc[:, 2:4, :], 0.25, None, ALU.max).then_inc(set_dve, 1)
            dve.wait_ge(set_dve, 6)
            for l in range(2):
                for n, j in enumerate((GA, GB)):
                    o = slice(n * NSEQ, (n + 1) * NSEQ)
                    last = dve.scalar_tensor_tensor(mod[:, l, j, :], msc[:, l, o], -1.0, msc[:, 2 + l, o],
                                                    ALU.add, ALU.mult)
            last.then_inc(set_dve, 1)

            def tt(dst, a, b, op, name, S):
                dve.tensor_tensor(dst, a, b, op).then_inc(S.sem, S.step(name))

            def gated(src, q, c, name, S):
                xq = x_f[:, bass.ds(c * CH + q * SEQ, SEQ)]
                dve.scalar_tensor_tensor(xq, src[:, q * SEQ:(q + 1) * SEQ], mod[:, 0, GA, bass.ds(c * SPC + q, 1)],
                                         xq, ALU.mult, ALU.add).then_inc(S.sem, S.step(name))

            def step_1(name, c):
                if name == "xc":
                    dve.wait_ge(pe_1.sem, pe_1.now(c, "mean1"))
                    dve.wait_ge(act_1.sem, act_1.before(c, "xn"))
                    tt(A0[:, :], x_f[:, bass.ds(c * CH, CH)], pP_1[:, :], ALU.subtract, name, dve_1)
                elif name == "hc":
                    dve.wait_ge(pe_1.sem, pe_1.now(c, "mean2"))
                    tt(A0[:, :], H[:, :], pP_1[:, :], ALU.subtract, name, dve_1)
                else:
                    if name == "xg0":
                        dve.wait_ge(act_1.sem, act_1.now(c, f"h{SPC - 1}"))
                    gated(H, int(name[2]), c, name, dve_1)

            def step_2(name, c, p):
                if name == "mz":
                    dve.wait_ge(act_2.sem, act_2.now(c, "pj"))
                    dve.tensor_scalar(z_[p][:, :], PJ[:, :], -44.0, None, ALU.max)\
                        .then_inc(dve_2.sem, dve_2.step(name))
                elif name in ("u1", "u2", "d1", "d2"):
                    s = int(name[1]) - 1
                    dst = U[s] if name[0] == "u" else delta_[s][p]
                    dve.wait_ge(pool_2.sem, pool_2.now(c, "s" + name))
                    if name[0] == "u":
                        dve.wait_ge(pool_2.sem, pool_2.before(c, f"du{s + 1}"))
                        dve.wait_ge(pool_2.sem, pool_2.before(c, f"ud{s + 1}"))
                    dve.scalar_tensor_tensor(dst[:, :], Pv[s][:, :], 0.0, Pl[s][:, :], ALU.max, ALU.add)\
                        .then_inc(dve_2.sem, dve_2.step(name))
                elif name in ("tu1", "tu2", "td1", "td2"):
                    s = int(name[2]) - 1
                    dve.wait_ge(act_2.sem, act_2.now(c, f"e{name[1:]}"))
                    dve.wait_ge(pool_2.sem, pool_2.before(c, f"sd{s + 1}") if name[1] == "u"
                                else pool_2.now(c, f"su{s + 1}"))
                    dve.tensor_scalar(Pt[s][:, :], Pe[s][:, :], 1.0, -1.0, ALU.add, ALU.add)\
                        .then_inc(dve_2.sem, dve_2.step(name))
                elif name in ("bl1", "bl2"):
                    s = int(name[2]) - 1
                    dve.wait_ge(act_2.sem, act_2.now(c, f"bh{s + 1}"))
                    tt(bcs_[s][p][96:128, :], dbc[R:R + 2 * NS, :], bcs_[s][p][64:96, :].bitcast(F32),
                       ALU.subtract, name, dve_2)

            def states(c, p, with_2, with_1):
                def b_product(k):
                    dve.wait_ge(pe_s.sem, pe_s.now(c, f"B{k}"))
                    dve.wait_ge(dve_s.sem, used(dve_s, c, "s", k))
                    tt(dB[k % RB][:, :], du_[k // NS][p][:, :], pB[k % RB][:, :], ALU.mult, f"b{k}", dve_s)

                def c_product(k):
                    dve.wait_ge(dve_s.sem, dve_s.now(c, f"s{k}"))
                    dve.wait_ge(pe_s.sem, pe_s.now(c, f"C{k}"))
                    dve.wait_ge(pe_s.sem, used(pe_s, c, "y", k))
                    tt(hC[k % RB][:, :], hs[k % RB][:, :], pC[k % 2][:, :], ALU.mult, f"c{k}", dve_s)

                dve.wait_ge(pool_2.sem, pool_2.now(c, "du2"))
                b_product(0)
                for k in range(NK):
                    dve.wait_ge(act_s.sem, act_s.now(c, f"e{k}"))
                    if k in POOL_B:
                        dve.wait_ge(pool_s.sem, pool_s.now(c, f"b{k}"))
                    else:
                        dve.wait_ge(dve_s.sem, dve_s.now(c, f"b{k}"))
                    dve.wait_ge(dve_s.sem, used(dve_s, c, "c", k))
                    dve.tensor_tensor_scan(hs[k % RB][:, :], dA[k % RB][:, :], dB[k % RB][:, :], 0.0, ALU.mult,
                                           ALU.add).then_inc(dve_s.sem, dve_s.step(f"s{k}"))
                    if k + 1 < NK and k + 1 not in POOL_B:
                        b_product(k + 1)
                    if k:
                        c_product(k - 1)
                    woven(k, c, with_2, with_1, DVE_2, DVE_1, lambda n, cc: step_2(n, cc, 1 - p), step_1)
                c_product(NK - 1)
                dve.wait_ge(pe_s.sem, pe_s.now(c, f"y{NK - 1}"))
                dve.wait_ge(dve_s.sem, dve_s.now(c, f"c{NK - 1}"))
                tt(hs[0][:, :], acc_[p][:, :], py[:, :], ALU.add, "y0", dve_s)
                dve.wait_ge(dve_s.sem, dve_s.now(c, "y0"))
                tt(hs[0][:, :], hs[0][:, :], z_[p][:, :], ALU.mult, "y1", dve_s)
                dve.wait_ge(dve_s.sem, dve_s.now(c, "y1"))
                for q in range(SPC):
                    gated(hs[0], q, c, f"x{q}", dve_s)
                dve.wait_ge(dve_s.sem, dve_s.now(c, f"x{SPC - 1}"))

            rounds(dve, DVE_2, DVE_1, step_2, step_1, states)

        @block.gpsimd
        def _(pool):
            for s in (pool_1, pool_2, pool_s):
                pool.sem_inc(s.sem, s.per)
            pool.memset(eps[:, 0:1], 1e-5).then_inc(set_pool, 1)
            pool.memset(eps[:, 1:2], 1e-6).then_inc(set_pool, 1)
            for t in dA:
                pool.memset(t[:, :], 0.0).then_inc(set_pool, 1)
            pool.wait_ge(set_pool, 2 + RB)

            def tt(dst, a, b, op, name, S):
                pool.tensor_tensor(dst, a, b, op).then_inc(S.sem, S.step(name))

            def step_1(name, c):
                pool.wait_ge(act_1.sem, act_1.now(c, {"xh": "rs1", "hn": "rs2"}[name]))
                tt(A0[:, :], A0[:, :], A1[:, :], ALU.mult, name, pool_1)

            def step_2(name, c, p):
                if name == "z":
                    pool.wait_ge(act_2.sem, act_2.now(c, "sz"))
                    tt(z_[p][:, :], PJ[:, :], z_[p][:, :], ALU.mult, name, pool_2)
                elif name == "ud1":
                    pool.wait_ge(dve_2.sem, dve_2.now(c, "u1"))
                    tt(acc_[p][:, :], U[0][:, :], col(V_D1).to_broadcast([128, CH]), ALU.mult, name, pool_2)
                elif name == "ud2":
                    pool.wait_ge(dve_2.sem, dve_2.now(c, "u2"))
                    pool.wait_ge(pool_2.sem, pool_2.before(c, "acc"))
                    tt(Q[:, :], U[1][:, :], col(V_D2).to_broadcast([128, CH]), ALU.mult, name, pool_2)
                elif name == "acc":
                    pool.wait_ge(pool_2.sem, pool_2.now(c, "ud2"))
                    tt(acc_[p][:, :], acc_[p][:, :], Q[:, :], ALU.add, name, pool_2)
                elif name in ("du1", "du2"):
                    s = int(name[2]) - 1
                    pool.wait_ge(dve_2.sem, dve_2.now(c, f"d{s + 1}"))
                    tt(du_[s][p][:, :], delta_[s][p][:, :], U[s][:, :], ALU.mult, name, pool_2)
                else:
                    kind, which, s = name[0], name[1], int(name[2]) - 1
                    if kind == "c":
                        pool.wait_ge(dve_2.sem, dve_2.now(c, f"t{which}{s + 1}"))
                        tt(Pt[s][:, :], Pe[s][:, :], Pt[s][:, :], ALU.subtract, name, pool_2)
                    else:
                        pool.wait_ge(pool_2.sem, pool_2.now(c, f"c{which}{s + 1}"))
                        pool.wait_ge(act_2.sem, act_2.now(c, f"l{which}{s + 1}"))
                        tt(Pl[s][:, :], Pl[s][:, :], Pt[s][:, :], ALU.add, name, pool_2)

            def states(c, p, with_2, with_1):
                def b_product(k):
                    pool.wait_ge(act_s.sem, act_s.now(c, f"b{k}"))
                    pool.wait_ge(dve_s.sem, used(dve_s, c, "s", k))
                    tt(dB[k % RB][:, :], du_[k // NS][p][:, :], Bc[POOL_B.index(k) % 2][:, :], ALU.mult, f"b{k}",
                       pool_s)

                b_product(1)
                for k in range(NK):
                    if k + 2 in POOL_B:
                        b_product(k + 2)
                    woven(k, c, with_2, with_1, POOL_2, POOL_1, lambda n, cc: step_2(n, cc, 1 - p), step_1)

            rounds(pool, POOL_2, POOL_1, step_2, step_1, states)


GSUB = 4
SUB = 512
NG = TOK // (GSUB * SUB)
NT = TOK // 128
GT = GSUB * SUB // 128
NE, NF = 8, 4
QS = SUB // SEQ
F_WG, F_GB = 0, NE
F_PER = 2 * NE
F_GAM, F_BET = 2 * F_PER, 2 * F_PER + 1
F_END = 2 * F_PER + 2
CAPT = NT + 1
DUMMY = NE * CAPT
ROWS = (DUMMY + 1) * 128
RW = D + 1
NJ = 2 * NT + NE
TURN = 4
NR = -(-NJ // TURN)
NJT = (NR + 2) * TURN
AWAY = 1 << 20
E_B1 = NF * 128
E_W2 = E_B1 + NF
E_B2 = E_W2 + NF * D
EW = E_B2 + D
R_TRI, R_ONE, R_J, R_BASE, R_ID, R_P, R_AWAY, R_RANK = (0, 128, 256, 256 + NJT, 264 + NJT, 264 + NJT + GT,
                                                        265 + NJT + GT, 266 + NJT + GT)
R_END = R_RANK + NE
I32 = mybir.dt.int32


def mixture_layer(nc, kept, layer, rconst, fvec, wexp, routed, results, out=None):
    L = f"m{layer}_"
    with ExitStack() as ctx:
        def sb(name, shape, dt=F32):
            return ctx.enter_context(nc.sbuf_tensor(L + name, shape, dt))

        def sem(name):
            return kept.sem(L + name)

        W = sb("W", [128, NE * EW])
        gk = [sb(f"gk{k}", [128, NT]) for k in range(2)]
        table = sb("table", [1, 2, NJT], I32)
        loaded_w = sem("loaded_w")

        def load_weights(sp):
            sp.dma_start(W[:, :], wexp).then_inc(loaded_w, 16)

        route(nc, kept, layer, L, sem, rconst, fvec, routed, gk, table, load_weights)
        experts(nc, kept, layer, L, sem, W, table, loaded_w, routed, results)
        combine(nc, kept, layer, L, sem, gk, results, out)


GATE = (["max0", "shift"] + [f"{n}0" for n in ("is", "rank", "first", "one")] + ["mask", "max1"]
        + [f"{n}1" for n in ("is", "rank", "first", "one")] + ["both", "d1", "sum", "den", "den1", "inv", "g2"]
        + ["cum", "ex", "slot", "slot_e", "run", "p1", "p2", "s1", "s2", "ix"])


def route(nc, kept, layer, L, sem, rconst, fvec, routed, gk, table, load_weights):
    two_norms = layer == 0
    x_f, mod, eps, ident, avg = kept.x_f, kept.mod, kept.eps, kept.ident, kept.avg
    with ExitStack() as ctx:
        def sb(name, shape, dt=F32):
            return ctx.enter_context(nc.sbuf_tensor(L + name, shape, dt))

        A, B, H = ([sb(f"{n}{j}", [128, SUB]) for j in range(GSUB)] for n in "ABH")
        pa, pb = ([ctx.enter_context(nc.psum_tensor(f"{L}{n}{j}", [128, SUB], F32)) for j in range(GSUB)]
                  for n in ("pa", "pb"))
        fv, rc = sb("fv", [128, F_END]), sb("rc", [128, R_END])
        xt = [[sb(f"xt{p}{k}", [128, GT, RW]) for k in range(2)] for p in range(2)]
        ix = [[sb(f"ix{p}{k}", [128, GT], I32) for k in range(2)] for p in range(2)]
        lg, P, Q, O1, O2, M = (sb(n, [128, GT, NE]) for n in ("lg", "P", "Q", "O1", "O2", "M"))
        cum, zero = sb("cum", [128, NE, GT]), sb("zero", [128, GT])
        t1 = [sb(f"t1{j}", [128, GT, 1]) for j in range(4)]
        run, idr = sb("run", [128, 1, NE]), sb("idr", [128, GT])
        padrow, padix = sb("padrow", [128, RW]), sb("padix", [128, NE], I32)
        cnt, cmp_, n_e, inc = sb("cnt", [1, NE, 1]), sb("cmp", [1, NE, NT]), sb("n_e", [1, NE]), sb("inc", [1, NE])
        room = sb("room", [1, NE])
        te, tr, ta = (sb(n, [1, NJT]) for n in ("te", "tr", "ta"))
        o = layer * F_PER
        wg, gbias = fv[:, o + F_WG:o + F_WG + NE], fv[:, o + F_GB:o + F_GB + NE]
        PRE, TOT = slice(256, 256 + GT * NE), slice(256, 256 + GT * NE)
        loaded, start = sem("loaded"), sem("start")
        taken, dummy = sem("taken"), sem("dummy")
        sent, padded = [sem(f"sent{p}") for p in range(2)], sem("padded")

        def names(kinds):
            return [f"{k}{p}{j}" for p in range(2) for k in kinds for j in (range(GSUB) if k[-1] == "_" else ("",))]

        first = ("mean1_", "var1_") + (("mean2_", "var2_") if two_norms else ())
        pe_n = Steps(sem("pe_n"), names(first + ("lg_", "tr_", "rank")))
        act_n = Steps(sem("act_n"), names(("sq1_", "ln1_", "rs1_", "h_")
                                          + (("sq2_", "ln2_", "rs2_", "xn_") if two_norms else ())
                                          + ("ta_", "tb_", "exp1", "exp2")))
        dve_n = Steps(sem("dve_n"), names(("xc_", "xh_") + (("xg_", "hc_", "hn_") if two_norms else ())
                                          + ("lc_", "id1", "id2", "id3") + tuple(GATE)))
        pool_n = Steps(sem("pool_n"), ["sent0", "sent1"])
        tab = Steps(sem("tab"), TABLE)
        xn_step = "xn_" if two_norms else "h_"
        block = ctx.enter_context(nc.Block())

        def last(S, g, p, name):
            return S.now(g, f"{name[0]}0{name[1]}") if p else S.before(g, f"{name[0]}1{name[1]}")

        def at(g, p, j, n=SUB, off=0):
            return bass.ds(g * (2 * GSUB * SUB) + p * (GSUB * SUB) + j * SUB + off, n)

        def seq(g, p, j, q):
            return bass.ds(g * (2 * GSUB * QS) + (p * GSUB + j) * QS + q, 1)

        @block.sync
        def _(sp):
            sp.dma_start(fv[:, :], fvec).then_inc(loaded, 16)
            sp.dma_start(rc[:, :], rconst).then_inc(loaded, 16)
            load_weights(sp)
            sp.wait_ge(start, 5)
            sp.dma_start(routed[DUMMY * 128:(DUMMY + 1) * 128, :], padrow[:, :]).then_inc(dummy, 16)
            sp.wait_ge(dummy, 16)

        @block.tensor
        def _(pe):
            pe.sem_inc(pe_n.sem, pe_n.per)
            pe.wait_ge(loaded, 32)
            with pe.Fori(0, NG // 2) as g:
                def mm(dst, lhsT, rhs, name):
                    pe.matmul(dst, lhsT, rhs, start=True, stop=True).then_inc(pe_n.sem, pe_n.step(name))

                for p in range(2):
                    for j in range(GSUB):
                        pe.wait_ge(dve_n.sem, last(dve_n, g, p, ("slot", "")))
                        mm(pa[j][:, :], avg, x_f[:, at(g, p, j)], f"mean1_{p}{j}")
                    for j in range(GSUB):
                        pe.wait_ge(act_n.sem, act_n.now(g, f"sq1_{p}{j}"))
                        pe.wait_ge(act_n.sem, last(act_n, g, p, ("tb_", j)))
                        mm(pb[j][:, :], avg, B[j][:, :], f"var1_{p}{j}")
                    if two_norms:
                        for j in range(GSUB):
                            pe.wait_ge(act_n.sem, act_n.now(g, f"h_{p}{j}"))
                            mm(pa[j][:, :], avg, H[j][:, :], f"mean2_{p}{j}")
                        for j in range(GSUB):
                            pe.wait_ge(act_n.sem, act_n.now(g, f"sq2_{p}{j}"))
                            mm(pb[j][:, :], avg, B[j][:, :], f"var2_{p}{j}")
                    for j in range(GSUB):
                        pe.wait_ge(act_n.sem, act_n.now(g, f"{xn_step}{p}{j}"))
                        for q in range(SUB // 128):
                            m = pe.matmul(pa[j][:, q * NE:(q + 1) * NE], A[j][:, q * 128:(q + 1) * 128], wg,
                                          start=True, stop=True)
                        m.then_inc(pe_n.sem, pe_n.step(f"lg_{p}{j}"))
                    for j in range(GSUB):
                        for q in range(SUB // 128):
                            m = pe.transpose(pb[j][:, q * 128:(q + 1) * 128], A[j][:, q * 128:(q + 1) * 128], ident)
                        m.then_inc(pe_n.sem, pe_n.step(f"tr_{p}{j}"))
                    pe.wait_ge(dve_n.sem, dve_n.now(g, f"both{p}"))
                    flat = M[:, :, :].rearrange("p t e -> p (t e)")
                    pe.matmul(pa[0][:, PRE], rc[:, R_TRI:R_TRI + 128], flat, start=True, stop=True)
                    mm(pa[1][:, TOT], rc[:, R_ONE:R_ONE + 128], flat, f"rank{p}")

        @block.scalar
        def _(act):
            act.sem_inc(act_n.sem, act_n.per)
            act.preload_act_table_set("natural_log_exp_and_others")
            act.wait_ge(loaded, 32)
            with act.Fori(0, NG // 2) as g:
                for p in range(2):
                    def square(n, ready):
                        for j in range(GSUB):
                            act.wait_ge(dve_n.sem, dve_n.now(g, f"{ready}_{p}{j}"))
                            act.activation(B[j][:, :], A[j][:, :], ACT.Square)\
                                .then_inc(act_n.sem, act_n.step(f"sq{n}_{p}{j}"))

                    def rstd(n):
                        for j in range(GSUB):
                            act.wait_ge(pe_n.sem, pe_n.now(g, f"var{n}_{p}{j}"))
                            act.activation(B[j][:, :], pb[j][:, :], ACT.Ln, bias=eps[:, 0:1])\
                                .then_inc(act_n.sem, act_n.step(f"ln{n}_{p}{j}"))
                        for j in range(GSUB):
                            act.wait_ge(act_n.sem, act_n.now(g, f"ln{n}_{p}{j}"))
                            act.activation(B[j][:, :], B[j][:, :], ACT.Exp, scale=-0.5)\
                                .then_inc(act_n.sem, act_n.step(f"rs{n}_{p}{j}"))

                    square(1, "xc")
                    rstd(1)
                    for j in range(GSUB):
                        act.wait_ge(dve_n.sem, dve_n.now(g, f"xh_{p}{j}"))
                        for q in range(QS):
                            dst = (H if two_norms else A)[j][:, q * SEQ:(q + 1) * SEQ]
                            a = act.activation(dst, A[j][:, q * SEQ:(q + 1) * SEQ], ACT.Identity,
                                               scale=mod[:, layer, CB, seq(g, p, j, q)],
                                               bias=mod[:, layer, SB, seq(g, p, j, q)])
                        a.then_inc(act_n.sem, act_n.step(f"h_{p}{j}"))
                    if two_norms:
                        square(2, "hc")
                        rstd(2)
                        for j in range(GSUB):
                            act.wait_ge(dve_n.sem, dve_n.now(g, f"hn_{p}{j}"))
                            act.activation(A[j][:, :], A[j][:, :], ACT.Identity, scale=fv[:, F_GAM:F_GAM + 1],
                                           bias=fv[:, F_BET:F_BET + 1])\
                                .then_inc(act_n.sem, act_n.step(f"xn_{p}{j}"))
                    act.wait_ge(pool_n.sem, pool_n.before(g, f"sent{p}"))
                    for k in range(2):
                        for j in range(GSUB):
                            act.wait_ge(pe_n.sem, pe_n.now(g, f"tr_{p}{j}"))
                            nq = SUB // 128
                            act.activation(xt[p][k][:, j * nq:(j + 1) * nq, 0:D],
                                           pb[j][:, :].rearrange("p (q d) -> p q d", d=D), ACT.Copy)\
                                .then_inc(act_n.sem, act_n.step(f"t{'ab'[k]}_{p}{j}"))
                    act.wait_ge(dve_n.sem, dve_n.now(g, f"shift{p}"))
                    act.activation(P[:, :, :], P[:, :, :], ACT.Exp).then_inc(act_n.sem, act_n.step(f"exp1{p}"))
                    act.wait_ge(dve_n.sem, dve_n.now(g, f"d1{p}"))
                    act.activation(t1[2][:, :, :], t1[2][:, :, :], ACT.Exp).then_inc(act_n.sem, act_n.step(f"exp2{p}"))

        @block.gpsimd
        def _(pool):
            pool.sem_inc(pool_n.sem, pool_n.per)
            with pool.Fori(0, NG // 2) as g:
                for p in range(2):
                    pool.wait_ge(act_n.sem, act_n.now(g, f"tb_{p}{GSUB - 1}"))
                    pool.wait_ge(dve_n.sem, dve_n.now(g, f"ix{p}"))
                    pool.sem_inc(taken, 1)
                    for k in range(2):
                        for t in range(GT):
                            pool.indirect_dma_start(routed, bass.IndirectOffsetOnAxis(ap=ix[p][k][:, t:t + 1], axis=0),
                                                    xt[p][k][:, t, :], None).then_inc(sent[p], 16)
                for p in range(2):
                    pool.wait_ge(sent[p], (g + 1) * (2 * GT * 16))
                    pool.sem_inc(pool_n.sem, pool_n.step(f"sent{p}"))
            pool.wait_ge(tab.sem, tab.at0("padix"))
            for e in range(NE):
                pool.indirect_dma_start(routed, bass.IndirectOffsetOnAxis(ap=padix[:, e:e + 1], axis=0),
                                        padrow[:, :], None).then_inc(padded, 16)
            pool.wait_ge(padded, NE * 16)

        @block.vector
        def _(dve):
            dve.sem_inc(dve_n.sem, dve_n.per)
            dve.wait_ge(loaded, 32)
            dve.tensor_copy(run[:, 0, :], rc[:, R_BASE:R_BASE + NE]).then_inc(start, 1)
            dve.tensor_copy(idr[:, :], rc[:, R_ID:R_ID + GT]).then_inc(start, 1)
            dve.memset(zero[:, :], 0.0).then_inc(start, 1)
            dve.memset(padrow[:, 0:D], 0.0).then_inc(start, 1)
            dve.tensor_copy(padrow[:, D:RW].bitcast(I32), rc[:, R_AWAY:R_AWAY + 1]).then_inc(start, 1)
            dve.wait_ge(start, 5)
            with dve.Fori(0, NG // 2) as g:
                def step(name, ins):
                    ins.then_inc(dve_n.sem, dve_n.step(name))

                for p in range(2):
                    for j in range(GSUB):
                        dve.wait_ge(pe_n.sem, pe_n.now(g, f"mean1_{p}{j}"))
                        dve.wait_ge(pe_n.sem, last(pe_n, g, p, ("tr_", j)))
                        step(f"xc_{p}{j}", dve.tensor_tensor(A[j][:, :], x_f[:, at(g, p, j)], pa[j][:, :],
                                                             ALU.subtract))
                    for j in range(GSUB):
                        dve.wait_ge(act_n.sem, act_n.now(g, f"rs1_{p}{j}"))
                        step(f"xh_{p}{j}", dve.tensor_tensor(A[j][:, :], A[j][:, :], B[j][:, :], ALU.mult))
                    if two_norms:
                        for j in range(GSUB):
                            dve.wait_ge(act_n.sem, act_n.now(g, f"h_{p}{j}"))
                            for q in range(QS):
                                xq = x_f[:, at(g, p, j, SEQ, q * SEQ)]
                                v = dve.scalar_tensor_tensor(xq, H[j][:, q * SEQ:(q + 1) * SEQ],
                                                             mod[:, layer, GB, seq(g, p, j, q)], xq,
                                                             ALU.mult, ALU.add)
                            step(f"xg_{p}{j}", v)
                        for j in range(GSUB):
                            dve.wait_ge(pe_n.sem, pe_n.now(g, f"mean2_{p}{j}"))
                            step(f"hc_{p}{j}", dve.tensor_tensor(A[j][:, :], H[j][:, :], pa[j][:, :], ALU.subtract))
                        for j in range(GSUB):
                            dve.wait_ge(act_n.sem, act_n.now(g, f"rs2_{p}{j}"))
                            step(f"hn_{p}{j}", dve.tensor_tensor(A[j][:, :], A[j][:, :], B[j][:, :], ALU.mult))
                    for j in range(GSUB):
                        dve.wait_ge(pe_n.sem, pe_n.now(g, f"lg_{p}{j}"))
                        nq = SUB // 128
                        step(f"lc_{p}{j}", dve.tensor_tensor(
                            lg[:, j * nq:(j + 1) * nq, :], pa[j][:, 0:nq * NE].rearrange("p (q e) -> p q e", e=NE),
                            gbias.rearrange("p (q e) -> p q e", q=1).to_broadcast([128, nq, NE]), ALU.add))
                    dve.wait_ge(pool_n.sem, pool_n.before(g, f"sent{p}"))
                    step(f"id1{p}", dve.tensor_copy(xt[p][0][:, :, D].bitcast(I32), idr[:, :]))
                    step(f"id2{p}", dve.tensor_scalar(xt[p][1][:, :, D].bitcast(I32), idr[:, :], float(TOK), None,
                                                      ALU.add))
                    dve.wait_ge(dve_n.sem, dve_n.now(g, f"id2{p}"))
                    step(f"id3{p}", dve.tensor_scalar(idr[:, :], idr[:, :], float(GSUB * SUB), None, ALU.add))

                    def wide(t):
                        return t[:, :, :].to_broadcast([128, GT, NE])

                    def do(name, ins):
                        ins.then_inc(dve_n.sem, dve_n.step(f"{name}{p}"))
                        dve.wait_ge(dve_n.sem, dve_n.now(g, f"{name}{p}"))

                    def tt(name, dst, a, b, op):
                        do(name, dve.tensor_tensor(dst, a, b, op))

                    P_, Q_, S_ = P[:, :, :], Q[:, :, :], lg[:, :, :]
                    dve.wait_ge(dve_n.sem, dve_n.now(g, f"id3{p}"))
                    do("max0", dve.tensor_reduce(t1[0][:, :, 0], S_, AX.X, ALU.max))
                    tt("shift", P_, S_, wide(t1[0]), ALU.subtract)
                    rank = rc[:, R_RANK:R_RANK + NE].rearrange("p (q e) -> p q e", q=1).to_broadcast([128, GT, NE])
                    for n, one in ((0, O1), (1, O2)):
                        m = t1[n]
                        tt(f"is{n}", Q_, S_, wide(m), ALU.is_equal)
                        tt(f"rank{n}", Q_, Q_, rank, ALU.mult)
                        do(f"first{n}", dve.tensor_reduce(t1[3][:, :, 0], Q_, AX.X, ALU.max))
                        tt(f"one{n}", one[:, :, :], Q_, wide(t1[3]), ALU.is_equal)
                        if n == 0:
                            do("mask", dve.scalar_tensor_tensor(S_, O1[:, :, :], -1e38, S_, ALU.mult, ALU.add))
                            do("max1", dve.tensor_reduce(t1[1][:, :, 0], S_, AX.X, ALU.max))
                    tt("both", M[:, :, :], O1[:, :, :], O2[:, :, :], ALU.add)
                    tt("d1", t1[2][:, :, :], t1[1][:, :, :], t1[0][:, :, :], ALU.subtract)
                    dve.wait_ge(act_n.sem, act_n.now(g, f"exp2{p}"))
                    do("sum", dve.tensor_reduce(t1[0][:, :, 0], P_, AX.X, ALU.add))
                    do("den", dve.tensor_scalar(t1[0][:, :, :], t1[0][:, :, :], 1e-9 if layer == 0 else 0.0, 1.0,
                                                ALU.mult, ALU.add))
                    tt("den1", t1[0][:, :, :], t1[0][:, :, :], t1[2][:, :, :], ALU.add)
                    g1 = gk[0][:, bass.ds(g * (2 * GT) + p * GT, GT)]
                    do("inv", dve.reciprocal(g1, t1[0][:, :, 0]))
                    tt("g2", gk[1][:, bass.ds(g * (2 * GT) + p * GT, GT)], t1[2][:, :, 0],
                       gk[0][:, bass.ds(g * (2 * GT) + p * GT, GT)], ALU.mult)
                    dve.wait_ge(pe_n.sem, pe_n.now(g, f"rank{p}"))
                    tot = pa[1][:, TOT].rearrange("p (t e) -> p t e", e=NE)
                    for e in range(NE):
                        v = dve.tensor_tensor_scan(cum[:, e, :], tot[:, :, e], zero[:, :], 0.0, ALU.add, ALU.add)
                    do("cum", v)
                    by_tile = cum[:, :, :].rearrange("p e t -> p t e")
                    tt("ex", S_, by_tile, tot, ALU.subtract)
                    tt("slot", S_, S_, pa[0][:, PRE].rearrange("p (t e) -> p t e", e=NE), ALU.add)
                    tt("slot_e", S_, S_, run[:, :, :].to_broadcast([128, GT, NE]), ALU.add)
                    tt("run", run[:, 0, :], run[:, 0, :], cum[:, :, GT - 1], ALU.add)
                    step(f"p1{p}", dve.tensor_tensor(Q_, S_, O1[:, :, :], ALU.mult))
                    tt("p2", P_, S_, O2[:, :, :], ALU.mult)
                    step(f"s1{p}", dve.tensor_reduce(t1[1][:, :, 0], Q_, AX.X, ALU.add))
                    do("s2", dve.tensor_reduce(t1[2][:, :, 0], P_, AX.X, ALU.add))
                    dve.tensor_copy(ix[p][0][:, :], t1[1][:, :, 0])
                    do("ix", dve.tensor_copy(ix[p][1][:, :], t1[2][:, :, 0]))

            def do(name, ins):
                ins.then_inc(tab.sem, tab.step(name))
                dve.wait_ge(tab.sem, tab.at0(name))

            J = rc[0:1, R_J:R_J + NJT]
            do("padix", dve.tensor_tensor(padix[:, :], run[:, 0, :],
                                          rc[:, R_P:R_P + 1].to_broadcast([128, NE]), ALU.add))
            do("cnt", dve.tensor_tensor(cnt[:, :, 0], run[0:1, 0, :], rc[0:1, R_BASE:R_BASE + NE], ALU.subtract))
            do("cnt1", dve.tensor_scalar(cnt[:, :, 0], cnt[:, :, 0], 1 / 128, None, ALU.mult))
            do("cmp", dve.tensor_tensor(cmp_[:, :, :], cnt[:, :, :].to_broadcast([1, NE, NT]),
                                        J[:, 0:NT].rearrange("p (e t) -> p e t", e=1).to_broadcast([1, NE, NT]),
                                        ALU.is_gt))
            do("n_e", dve.tensor_reduce(n_e[:, :], cmp_[:, :, :], AX.X, ALU.add))
            do("inc", dve.tensor_tensor_scan(inc[:, :], n_e[:, :], zero[0:1, 0:NE], 0.0, ALU.add, ALU.add))
            do("room", dve.tensor_scalar(room[:, :], n_e[:, :], -1.0, float(CAPT), ALU.mult, ALU.add))
            do("e0", dve.tensor_scalar(te[:, :], J, inc[:, 0:1], None, ALU.is_ge))
            do("r0", dve.tensor_copy(tr[:, :], J))
            for e in range(1, NE):
                do(f"a{e}", dve.tensor_scalar(ta[:, :], J, inc[:, e - 1:e], room[:, e - 1:e], ALU.is_ge, ALU.mult))
                do(f"r{e}", dve.tensor_tensor(tr[:, :], tr[:, :], ta[:, :], ALU.add))
                if e > 1:
                    do(f"e{e}", dve.scalar_tensor_tensor(te[:, :], J, inc[:, e - 1:e], te[:, :], ALU.is_ge, ALU.add))
            do("left", dve.tensor_scalar(ta[:, :], tr[:, :], -1.0, float(DUMMY), ALU.mult, ALU.add))
            do("left1", dve.scalar_tensor_tensor(ta[:, :], J, inc[:, NE - 1:NE], ta[:, :], ALU.is_ge, ALU.mult))
            do("r", dve.tensor_tensor(tr[:, :], tr[:, :], ta[:, :], ALU.add))
            for n, (t, size) in enumerate(((te, EW), (tr, 128))):
                do(f"t{n}", dve.tensor_scalar(table[:, n, :], t[:, :], float(size), None, ALU.mult))


TABLE = (["padix", "cnt", "cnt1", "cmp", "n_e", "inc", "room", "e0", "r0"]
         + [n for e in range(1, NE) for n in (f"a{e}", f"r{e}", f"e{e}") if n != "e1"]
         + ["left", "left1", "r", "t0", "t1"])


def experts(nc, kept, layer, L, sem, W, table, loaded_w, routed, results):
    ident = kept.ident
    gelu, gelu_set = ((ACT.Gelu_apprx_tanh, "gelu_apprx_tanh_and_others") if layer == 0
                      else (ACT.Gelu, "gelu_and_others"))
    with ExitStack() as ctx:
        def ring(name, shape, dt=F32, n=2):
            return [ctx.enter_context(nc.sbuf_tensor(f"{L}{name}{u}", shape, dt)) for u in range(n)]

        xs = ring("xs", [128, RW], n=TURN)
        xT = ring("xT", [D, 128])
        ws = ring("ws", [128, EW], n=TURN)
        hT = ring("hT", [128, NF * 128])
        ys = ring("ys", [128, D])
        idn, ids = ring("idn", [128, 1], I32), ring("ids", [128, 1], I32)
        pT, pu, pd = ([ctx.enter_context(nc.psum_tensor(f"{L}{n}{u}", [128, 512], F32)) for u in range(2)]
                      for n in ("pT", "pu", "pd"))
        transposed, up, down = sem("transposed"), sem("up"), sem("down")
        activated = sem("activated")
        weighted, rows_in, result = sem("weighted"), sem("rows_in"), sem("result")
        kept_ids, moved = sem("kept_ids"), sem("moved")
        taken = sem("taken_x")
        fetched, put = [sem(f"fetched{v}") for v in range(TURN)], [sem(f"put{u}") for u in range(2)]
        block = ctx.enter_context(nc.Block())

        def value(eng, reg, row, j, top):
            eng.reg_load(reg, table[0:1, row, bass.ds(j, 1)] if not isinstance(j, int) else table[0:1, row, j:j + 1])
            return eng.snap(reg, min_val=0, max_val=top)

        @block.sync
        def _(sp):
            with sp.register(L + "place") as reg:
                def fetch(j, v):
                    at = value(sp, reg, 1, j, DUMMY * 128)
                    sp.dma_start(xs[v][:, :], routed[bass.ds(at, 128), :]).then_inc(fetched[v], 16)

                for v in range(TURN):
                    fetch(v, v)
                with sp.Fori(0, NR) as r:
                    for v in range(TURN):
                        j = r * TURN + v
                        sp.wait_ge(transposed, j + 1)
                        sp.wait_ge(kept_ids, j + 1)
                        fetch(j + TURN, v)
            for v in range(TURN):
                sp.wait_ge(fetched[v], (NR + 1) * 16)

        @block.tensor
        def _(pe):
            def transpose(v, j, turn):
                pe.wait_ge(fetched[v], (turn + 1) * 16)
                pe.wait_ge(rows_in, j + 1)
                pe.transpose(pT[v % 2][:, 0:128], xs[v][:, 0:D], ident).then_inc(transposed, 1)

            pe.sem_inc(down, 2)
            pe.sem_inc(up, 2)
            for v in range(2):
                transpose(v, v, 0)
            with pe.Fori(0, NR) as r:
                for pair in range(TURN // 2):
                    for u in range(2):
                        v = 2 * pair + u
                        j = r * TURN + v
                        pe.wait_ge(weighted, j + 1)
                        pe.wait_ge(rows_in, j + 3)
                        pe.wait_ge(activated, j + 1)
                        for f in range(NF):
                            m = pe.matmul(pu[u][:, f * 128:(f + 1) * 128], ws[v][:, f * 128:(f + 1) * 128],
                                          xT[u][:, :], start=True, stop=True)
                        m.then_inc(up, 1)
                    for u in range(2):
                        v = 2 * pair + u
                        j = r * TURN + v
                        transpose((v + 2) % TURN, j + 2, r + (v + 2) // TURN)
                        pe.wait_ge(result, j + 1)
                        pe.wait_ge(activated, j + 3)
                        for f in range(NF):
                            m = pe.matmul(pd[u][:, 0:D], hT[u][:, f * 128:(f + 1) * 128],
                                          ws[v][:, E_W2 + f * D:E_W2 + (f + 1) * D], start=f == 0, stop=f == NF - 1)
                        m.then_inc(down, 1)

        @block.scalar
        def _(act):
            def rows(j, u):
                act.wait_ge(transposed, j + 1)
                act.wait_ge(up, j + 1)
                act.activation(xT[u][:, :], pT[u][:, 0:128], ACT.Copy).then_inc(rows_in, 1)

            act.sem_inc(activated, 2)
            act.sem_inc(rows_in, 2)
            act.preload_act_table_set(gelu_set)
            for u in range(2):
                rows(u, u)
            with act.Fori(0, NR) as r:
                for pair in range(TURN // 2):
                    for u in range(2):
                        v = 2 * pair + u
                        j = r * TURN + v
                        act.wait_ge(down, j + 1)
                        act.wait_ge(up, j + 3)
                        for f in range(NF):
                            a = act.activation(hT[u][:, f * 128:(f + 1) * 128], pu[u][:, f * 128:(f + 1) * 128],
                                               gelu, bias=ws[v][:, E_B1 + f:E_B1 + f + 1])
                        a.then_inc(activated, 1)
                    for u in range(2):
                        rows(r * TURN + (2 * pair + u + 2), u)

        @block.gpsimd
        def _(pool):
            for u in range(2):
                pool.dma_start(ys[u][:, :], ident).then_inc(put[u], 16)
            with pool.Fori(0, NR) as r:
                for v in range(TURN):
                    j, u = r * TURN + v, v % 2
                    pool.wait_ge(result, j + 3)
                    pool.sem_inc(taken, 1)
                    pool.indirect_dma_start(results, bass.IndirectOffsetOnAxis(ap=ids[u][:, 0:1], axis=0),
                                            ys[u][:, :], None, bounds_check=2 * TOK - 1, oob_is_err=False)\
                        .then_inc(put[u], 16)
            for u in range(2):
                pool.wait_ge(put[u], (NR * TURN // 2 + 1) * 16)

        @block.vector
        def _(dve):
            with dve.register(L + "expert") as reg:
                def weights(j, v):
                    w = W[:, bass.ds(value(dve, reg, 0, j, (NE - 1) * EW), EW)]
                    dve.wait_ge(down, j + 1 if isinstance(j, int) else j - 1)
                    dve.tensor_copy(ws[v][:, :], w).then_inc(weighted, 1)

                def places(j, v):
                    dve.tensor_copy(idn[v % 2][:, :], xs[v][:, D:RW].bitcast(I32)).then_inc(kept_ids, 1)

                dve.wait_ge(loaded_w, 16)
                dve.sem_inc(result, 2)
                for u in range(2):
                    weights(u, u)
                    dve.wait_ge(transposed, u + 1)
                    places(u, u)
                with dve.Fori(0, NR) as r:
                    for v in range(TURN):
                        j, u = r * TURN + v, v % 2
                        weights(j + 2, (v + 2) % TURN)
                        dve.wait_ge(put[u], (r * (TURN // 2) + (v // 2 + 1)) * 16)
                        dve.wait_ge(kept_ids, j + 2)
                        dve.tensor_copy(ids[u][:, :], idn[u][:, :]).then_inc(moved, 1)
                        dve.wait_ge(transposed, j + 3)
                        dve.wait_ge(moved, j + 1)
                        places(j + 2, (v + 2) % TURN)
                        dve.wait_ge(down, j + 3)
                        dve.tensor_tensor(ys[u][:, :], pd[u][:, 0:D], ws[v][:, E_B2:EW], ALU.add)\
                            .then_inc(result, 1)


def combine(nc, kept, layer, L, sem, gk, results, out):
    x_f, mod, ident = kept.x_f, kept.mod, kept.ident
    NB, NX = SUB // 128, TOK // SUB // 4
    with ExitStack() as ctx:
        yy = [[ctx.enter_context(nc.sbuf_tensor(f"{L}yy{p}{k}", [128, NB, D], F32)) for k in range(2)]
              for p in range(4)]
        pt = [ctx.enter_context(nc.psum_tensor(f"{L}pt{p}", [128, SUB], F32)) for p in range(4)]
        fetched = [[sem(f"back{p}{k}") for k in range(2)] for p in range(4)]
        pe_c, act_c = Steps(sem("pe_c"), [f"t{p}" for p in range(4)]), Steps(sem("act_c"), [f"a{p}" for p in range(4)])
        dve_c = Steps(sem("dve_c"), ["b0"] + [n for p in range(1, 4) for n in (f"b{p}", f"x{p - 1}")] + ["x3"])
        stored = sem("stored")
        block = ctx.enter_context(nc.Block())

        @block.sync
        def _(sp):
            with sp.Fori(0, NX) as i:
                for p in range(4):
                    sp.wait_ge(pe_c.sem, pe_c.before(i, f"t{p}"))
                    for k in range(2):
                        sp.dma_start(yy[p][k][:, :, :],
                                     results[bass.ds(i * (4 * SUB) + (k * TOK + p * SUB), SUB), :]
                                     .rearrange("(q t) d -> t q d", t=128)).then_inc(fetched[p][k], 16)
            if out is not None:
                sp.wait_ge(dve_c.sem, (NX + 1) * dve_c.per)
                sp.dma_start(out, x_f[:, :]).then_inc(stored, 16)
                sp.wait_ge(stored, 16)

        @block.tensor
        def _(pe):
            pe.sem_inc(pe_c.sem, pe_c.per)
            with pe.Fori(0, NX) as i:
                for p in range(4):
                    pe.wait_ge(dve_c.sem, dve_c.now(i, f"b{p}"))
                    pe.wait_ge(dve_c.sem, dve_c.before(i, f"x{p}"))
                    for q in range(NB):
                        m = pe.transpose(pt[p][:, q * 128:(q + 1) * 128], yy[p][0][:, q, :], ident)
                    m.then_inc(pe_c.sem, pe_c.step(f"t{p}"))

        @block.scalar
        def _(act):
            act.sem_inc(act_c.sem, act_c.per)
            with act.Fori(0, NX) as i:
                for p in range(4):
                    act.wait_ge(fetched[p][0], (i + 1) * 16)
                    for q in range(NB):
                        a = act.activation(yy[p][0][:, q, :], yy[p][0][:, q, :], ACT.Identity,
                                           scale=gk[0][:, bass.ds(i * (4 * NB) + (p * NB + q), 1)])
                    a.then_inc(act_c.sem, act_c.step(f"a{p}"))

        @block.vector
        def _(dve):
            dve.sem_inc(dve_c.sem, dve_c.per)
            with dve.Fori(0, NX) as i:
                def second(p):
                    dve.wait_ge(fetched[p][1], (i + 1) * 16)
                    dve.wait_ge(act_c.sem, act_c.now(i, f"a{p}"))
                    for q in range(NB):
                        v = dve.scalar_tensor_tensor(yy[p][0][:, q, :], yy[p][1][:, q, :],
                                                     gk[1][:, bass.ds(i * (4 * NB) + (p * NB + q), 1)],
                                                     yy[p][0][:, q, :], ALU.mult, ALU.add)
                    v.then_inc(dve_c.sem, dve_c.step(f"b{p}"))

                def add(p):
                    dve.wait_ge(pe_c.sem, pe_c.now(i, f"t{p}"))
                    for q in range(QS):
                        xq = x_f[:, bass.ds(i * (4 * SUB) + (p * SUB + q * SEQ), SEQ)]
                        v = dve.scalar_tensor_tensor(xq, pt[p][:, q * SEQ:(q + 1) * SEQ],
                                                     mod[:, layer, GB, bass.ds(i * (4 * QS) + (p * QS + q), 1)], xq,
                                                     ALU.mult, ALU.add)
                    v.then_inc(dve_c.sem, dve_c.step(f"x{p}"))

                for p in range(4):
                    second(p)
                    if p:
                        add(p - 1)
                add(3)



NLOC, DH = 4, 8
LF, GF = NLOC * DH, D - NLOC * DH
BLK = 64
HV = DH + 1
VW = NLOC * HV + GF + 1
PW = 2 * GF + D
(A_QK, A_TOK, A_WOG, A_WOL, A_CAUS, A_HEAD) = (0, 2 * D, 2 * D + PW, 3 * D + PW, 4 * D + PW, 5 * D + PW)
A_ROWS = A_HEAD + GF
A_END = A_ROWS + NLOC
SCALE = DH ** -0.5


def attention_layer(nc, kept, wat):
    L = "a_"
    with ExitStack() as ctx:
        def sb(name, shape, dt=F32):
            return ctx.enter_context(nc.sbuf_tensor(L + name, shape, dt))

        def sem(name):
            return kept.sem(L + name)

        h_f = sb("h_f", [D, TOK])
        wa = sb("wa", [128, A_END])
        loaded, fixed = sem("loaded"), sem("fixed")
        normalise(nc, kept, 1, L, sem, h_f, SA, CA, lambda sp: sp.dma_start(wa[:, :], wat).then_inc(loaded, 16))
        attend(nc, kept, L, sem, h_f, wa, loaded, fixed)


def normalise(nc, kept, layer, L, sem, h_f, shift, scale, load):
    x_f, mod, eps, avg = kept.x_f, kept.mod, kept.eps, kept.avg
    with ExitStack() as pre:
        A = [pre.enter_context(nc.sbuf_tensor(f"{L}A{j}", [128, SUB], F32)) for j in range(GSUB)]
        B = [pre.enter_context(nc.sbuf_tensor(f"{L}B{j}", [128, SUB], F32)) for j in range(GSUB)]
        pa = [pre.enter_context(nc.psum_tensor(f"{L}pa{j}", [128, SUB], F32)) for j in range(GSUB)]
        pb = [pre.enter_context(nc.psum_tensor(f"{L}pb{j}", [128, SUB], F32)) for j in range(GSUB)]
        names = lambda kinds: [f"{k}{j}" for k in kinds for j in range(GSUB)]
        pe_n = Steps(sem("pe_n"), names(("mean_", "var_")))
        act_n = Steps(sem("act_n"), names(("sq_", "ln_", "rs_", "h_")))
        dve_n = Steps(sem("dve_n"), names(("xc_", "xh_")))
        block = pre.enter_context(nc.Block())

        def at(g, j):
            return bass.ds(g * (GSUB * SUB) + j * SUB, SUB)

        @block.sync
        def _(sp):
            load(sp)

        @block.tensor
        def _(pe):
            pe.sem_inc(pe_n.sem, pe_n.per)
            with pe.Fori(0, NG) as g:
                for j in range(GSUB):
                    pe.wait_ge(dve_n.sem, dve_n.before(g, f"xc_{j}"))
                    pe.matmul(pa[j][:, :], avg, x_f[:, at(g, j)], start=True, stop=True)\
                        .then_inc(pe_n.sem, pe_n.step(f"mean_{j}"))
                for j in range(GSUB):
                    pe.wait_ge(act_n.sem, act_n.now(g, f"sq_{j}"))
                    pe.matmul(pb[j][:, :], avg, B[j][:, :], start=True, stop=True)\
                        .then_inc(pe_n.sem, pe_n.step(f"var_{j}"))

        @block.scalar
        def _(act):
            act.sem_inc(act_n.sem, act_n.per)
            act.preload_act_table_set("natural_log_exp_and_others")
            with act.Fori(0, NG) as g:
                for j in range(GSUB):
                    act.wait_ge(dve_n.sem, dve_n.now(g, f"xc_{j}"))
                    act.activation(B[j][:, :], A[j][:, :], ACT.Square).then_inc(act_n.sem, act_n.step(f"sq_{j}"))
                for j in range(GSUB):
                    act.wait_ge(pe_n.sem, pe_n.now(g, f"var_{j}"))
                    act.activation(B[j][:, :], pb[j][:, :], ACT.Ln, bias=eps[:, 0:1])\
                        .then_inc(act_n.sem, act_n.step(f"ln_{j}"))
                for j in range(GSUB):
                    act.wait_ge(act_n.sem, act_n.now(g, f"ln_{j}"))
                    act.activation(B[j][:, :], B[j][:, :], ACT.Exp, scale=-0.5)\
                        .then_inc(act_n.sem, act_n.step(f"rs_{j}"))
                for j in range(GSUB):
                    act.wait_ge(dve_n.sem, dve_n.now(g, f"xh_{j}"))
                    for q in range(QS):
                        s = g * (GSUB * QS) + j * QS + q
                        a = act.activation(h_f[:, bass.ds(g * (GSUB * SUB) + j * SUB + q * SEQ, SEQ)],
                                           A[j][:, q * SEQ:(q + 1) * SEQ], ACT.Identity,
                                           scale=mod[:, layer, scale, bass.ds(s, 1)],
                                           bias=mod[:, layer, shift, bass.ds(s, 1)])
                    a.then_inc(act_n.sem, act_n.step(f"h_{j}"))

        @block.vector
        def _(dve):
            dve.sem_inc(dve_n.sem, dve_n.per)
            with dve.Fori(0, NG) as g:
                for j in range(GSUB):
                    dve.wait_ge(pe_n.sem, pe_n.now(g, f"mean_{j}"))
                    dve.wait_ge(act_n.sem, act_n.before(g, f"h_{j}"))
                    dve.tensor_tensor(A[j][:, :], x_f[:, at(g, j)], pa[j][:, :], ALU.subtract)\
                        .then_inc(dve_n.sem, dve_n.step(f"xc_{j}"))
                for j in range(GSUB):
                    dve.wait_ge(act_n.sem, act_n.now(g, f"rs_{j}"))
                    dve.tensor_tensor(A[j][:, :], A[j][:, :], B[j][:, :], ALU.mult)\
                        .then_inc(dve_n.sem, dve_n.step(f"xh_{j}"))


def attend(nc, kept, L, sem, h_f, wa, loaded, fixed):
    x_f, mod, ident = kept.x_f, kept.mod, kept.ident
    BF = mybir.dt.bfloat16
    wq4, wk4 = wa[:, A_QK:A_QK + D], wa[:, A_QK + D:A_QK + 2 * D]
    wtok = wa[:, A_TOK:A_TOK + PW]
    wog, wol = wa[0:GF, A_WOG:A_WOG + D], wa[0:LF + 1, A_WOL:A_WOL + D]
    caus, same = wa[:, A_CAUS:A_CAUS + 128], wa[0:GF, A_HEAD:A_HEAD + GF]
    with ExitStack() as ctx:
        def sb(name, shape, dt=F32):
            return ctx.enter_context(nc.sbuf_tensor(L + name, shape, dt))

        def two(name, shape, dt=F32):
            return [sb(f"{name}{p}", shape, dt) for p in range(2)]

        idb, mask0, mask1 = sb("idb", [128, 128], BF), sb("mask0", [128, 4, 128], BF), sb("mask1", [128, 2, 256], BF)
        hs = two("hs", [128, SEQ])
        kq = two("kq", [128, 2, SEQ], F32R)
        k4, q4 = [t[:, 0, :] for t in kq], [t[:, 1, :] for t in kq]
        kd = two("kd", [128, NLOC, SEQ], F32R)
        tk = two("tk", [128, 2, 2 * GF])
        va = two("va", [128, 2, VW])
        qe, qm = two("qe", [128, 2, 12, DH]), two("qm", [128, 2, 12])
        kk, km = two("kk", [128, 2, GF]), two("km", [128, 2, GF])
        mx = two("mx", [128, 2, NLOC])
        P0, P1 = two("P0", [128, NLOC, 128]), two("P1", [128, NLOC, 256])
        pt = two("pt", [128, 3, NLOC, 128])
        kr, cn = two("kr", [GF, 3, 1]), two("cn", [GF, 3, GF])
        qT, og = two("qT", [GF, SEQ]), two("og", [GF, SEQ])
        rs, ol, olT = two("rs", [128, 2, NLOC, 1]), two("ol", [128, 2, NLOC, DH]), two("olT", [LF + 1, SEQ])
        S0 = [ctx.enter_context(nc.psum_tensor(f"{L}S0{p}", [128, 512], F32)) for p in range(2)]
        S1 = [ctx.enter_context(nc.psum_tensor(f"{L}S1{p}", [128, 2, 512], F32)) for p in range(2)]
        X = [ctx.enter_context(nc.psum_tensor(f"{L}X{p}", [128, 512], F32)) for p in range(2)]
        CW = GF + 1
        def steps(name, names):
            return Steps(sem(name), names, rounds=2)

        pe_f, pe_b = steps("pe_f", ("S0", "S", "ctx", "qT")), steps("pe_b", ("PT", "og", "pv", "olT", "wo"))
        pe_l = steps("pe_l", ("rows", "local"))
        act_f = steps("act_f", ("tk", "vl", "vg", "u", "kex", "qex", "sexp", "qT"))
        act_b = steps("act_b", ("pt", "og", "olT"))
        dve_f = steps("dve_f", ("kmn", "qmx", "qsh", "kl", "ql", "kd", "kk", "smx", "smn", "qsm", "qrc", "qn", "kr",
                                "krc", "cn"))
        dve_b = steps("dve_b", ("pt", "rrc", "ol", "x"))
        pool_f = steps("pool_f", ("hs",))
        made, MADE = sem("made"), 6
        block = ctx.enter_context(nc.Block())

        def sequences(eng, body):
            body(None, 1, 0, 1)
            with eng.Fori(0, NSEQ // 2 - 1) as i:
                for p in range(2):
                    body(i * 2 + p, p, i * 2 + (p + 1), i * 2 + (p + 2))
            body(NSEQ - 2, 0, NSEQ - 1, None)
            body(NSEQ - 1, 1, None, None)

        @block.tensor
        def _(pe):
            for S in (pe_l, pe_f, pe_b):
                pe.sem_inc(S.sem, 2 * S.per)
            pe.wait_ge(made, MADE)
            pe.wait_ge(loaded, 16)
            pe.wait_ge(fixed, 3)

            def rows(m, p):
                pe.wait_ge(pool_f.sem, pool_f.now(m, "hs"))
                for t in range(2):
                    mm = pe.matmul(S1[p][:, t, 0:PW], hs[p][:, t * 128:(t + 1) * 128], wtok, start=True, stop=True)
                mm.then_inc(pe_l.sem, pe_l.step("rows"))

            def local(m, p):
                for q, wl in enumerate((wk4, wq4)):
                    mm = pe.matmul(S0[p][:, q * SEQ:(q + 1) * SEQ], wl, hs[p][:, :], start=True, stop=True)
                mm.then_inc(pe_l.sem, pe_l.step("local"))

            rows(0, 0)
            local(0, 0)

            def body(s, p, n, m):
                o = 1 - p
                if s is not None:
                    pe.wait_ge(act_f.sem, act_f.now(s, "sexp"))
                    for h in range(NLOC):
                        c = slice(h * 128, (h + 1) * 128)
                        pe.transpose(S0[p][:, c], P0[p][:, h, :], ident)
                        pe.transpose(S1[p][:, 0, c], P1[p][:, h, 0:128], ident)
                        mm = pe.transpose(S1[p][:, 1, c], P1[p][:, h, 128:256], ident)
                    mm.then_inc(pe_b.sem, pe_b.step("PT"))
                    pe.wait_ge(act_f.sem, act_f.now(s, "qT"))
                    for b in range(1, SEQ // BLK):
                        mm = pe.matmul(X[p][0:GF, b * BLK:(b + 1) * BLK], cn[p][:, b - 1, :],
                                       qT[p][:, b * BLK:(b + 1) * BLK], start=True, stop=True)
                    mm.then_inc(pe_b.sem, pe_b.step("og"))
                if n is not None:
                    pe.wait_ge(act_f.sem, act_f.now(n, "vg"))
                    pe.wait_ge(dve_f.sem, dve_f.now(n, "ql"))
                    pe.matmul(S0[o][:, :], idb[:, :], mask0[:, :, :].rearrange("p a b -> p (a b)"), start=True,
                              stop=False)
                    for b in range(2):
                        pe.matmul(S1[o][:, b, :], idb[:, :], mask1[:, :, :].rearrange("p a b -> p (a b)"),
                                  start=True, stop=False)
                    pe.wait_ge(dve_f.sem, dve_f.now(n, "kd"))
                    pe.matmul(S0[o][:, :], q4[o][:, 0:128], kd[o][:, :, 0:128], start=False, stop=True)\
                        .then_inc(pe_f.sem, pe_f.step("S0"))
                    for b in range(2):
                        mm = pe.matmul(S1[o][:, b, :], q4[o][:, 128:256],
                                       kd[o][:, 2 * b:2 * b + 2, :].rearrange("p a b -> p (a b)"),
                                       start=False, stop=True)
                    mm.then_inc(pe_f.sem, pe_f.step("S"))
                if s is not None:
                    pe.wait_ge(act_b.sem, act_b.now(s, "pt"))
                    pe.wait_ge(dve_b.sem, dve_b.now(s, "pt"))
                    for h in range(NLOC):
                        v = slice(h * HV, (h + 1) * HV)
                        pe.matmul(S0[p][:, h * HV:(h + 1) * HV], pt[p][:, 0, h, :], va[p][:, 0, v], start=True,
                                  stop=True)
                        c = slice((NLOC + h) * HV, (NLOC + h + 1) * HV)
                        pe.matmul(S0[p][:, c], pt[p][:, 1, h, :], va[p][:, 0, v], start=True, stop=False)
                        mm = pe.matmul(S0[p][:, c], pt[p][:, 2, h, :], va[p][:, 1, v], start=False, stop=True)
                    mm.then_inc(pe_b.sem, pe_b.step("pv"))
                if n is not None:
                    pe.wait_ge(dve_f.sem, dve_f.now(n, "kk"))
                    pe.wait_ge(dve_b.sem, dve_b.two_before(n, "x"))
                    g = slice(NLOC * HV, VW)
                    pe.matmul(X[o][0:GF, 0:CW], kk[o][0:BLK, 0, :], va[o][0:BLK, 0, g], start=True, stop=True)
                    pe.matmul(X[o][0:GF, CW:2 * CW], kk[o][:, 0, :], va[o][:, 0, g], start=True, stop=True)
                    pe.matmul(X[o][0:GF, 2 * CW:3 * CW], kk[o][:, 0, :], va[o][:, 0, g], start=True, stop=False)
                    pe.matmul(X[o][0:GF, 2 * CW:3 * CW], kk[o][0:BLK, 1, :], va[o][0:BLK, 1, g], start=False,
                              stop=True).then_inc(pe_f.sem, pe_f.step("ctx"))
                if m is not None:
                    rows(m, p)
                if s is not None:
                    pe.wait_ge(dve_b.sem, dve_b.now(s, "ol"))
                    for t in range(2):
                        mm = pe.transpose(S0[p][0:LF, t * 128:(t + 1) * 128],
                                          ol[p][:, t, :, :].rearrange("p h x -> p (h x)"), ident)
                    mm.then_inc(pe_b.sem, pe_b.step("olT"))
                if n is not None:
                    pe.wait_ge(dve_f.sem, dve_f.now(n, "cn"))
                    for t in range(2):
                        mm = pe.transpose(X[o][0:GF, t * 128:(t + 1) * 128],
                                          qe[o][:, t, :, :].rearrange("p h x -> p (h x)"), ident)
                    mm.then_inc(pe_f.sem, pe_f.step("qT"))
                if s is not None:
                    pe.wait_ge(act_b.sem, act_b.now(s, "olT"))
                    y = X[p][:, SEQ:2 * SEQ]
                    pe.matmul(y, wog, og[p][:, :], start=True, stop=False)
                    pe.matmul(y, wol, olT[p][:, :], start=False, stop=True).then_inc(pe_b.sem, pe_b.step("wo"))
                if m is not None:
                    local(m, p)

            sequences(pe, body)

        @block.scalar
        def _(act):
            for S in (act_f, act_b):
                act.sem_inc(S.sem, 2 * S.per)
            act.preload_act_table_set("natural_log_exp_and_others")
            act.wait_ge(made, MADE)

            def body(s, p, n, m):
                o = 1 - p
                if n is not None:
                    act.wait_ge(pe_l.sem, pe_l.now(n, "rows"))
                    act.wait_ge(dve_f.sem, dve_f.two_before(n, "kk"))
                    act.wait_ge(pe_b.sem, pe_b.two_before(n, "pv"))
                    act.activation(tk[o][:, :, :], S1[o][:, :, 0:2 * GF], ACT.Copy)\
                        .then_inc(act_f.sem, act_f.step("tk"))
                    vl = va[o][:, :, 0:NLOC * HV].rearrange("p t (h x) -> p t h x", x=HV)[:, :, :, 0:DH]
                    act.activation(vl, S1[o][:, :, 2 * GF:2 * GF + LF].rearrange("p t (h x) -> p t h x", x=DH),
                                   ACT.Copy).then_inc(act_f.sem, act_f.step("vl"))
                    act.activation(va[o][:, :, NLOC * HV:VW - 1], S1[o][:, :, 2 * GF + LF:PW], ACT.Copy)\
                        .then_inc(act_f.sem, act_f.step("vg"))
                    act.wait_ge(pe_l.sem, pe_l.now(n, "local"))
                    act.activation(kq[o][:, :, :].rearrange("p a t -> p (a t)"), S0[o][:, :], ACT.Copy)\
                        .then_inc(act_f.sem, act_f.step("u"))
                if s is not None:
                    act.wait_ge(pe_b.sem, pe_b.now(s, "PT"))
                    for b in range(2):
                        a = act.activation(pt[p][:, b, :, :].rearrange("p h q -> p (h q)"),
                                           S0[p][:, :] if b == 0 else S1[p][:, 0, :], ACT.Copy)
                    a.then_inc(act_b.sem, act_b.step("pt"))
                    act.wait_ge(pe_b.sem, pe_b.now(s, "og"))
                    act.wait_ge(pe_b.sem, pe_b.two_before(s, "wo"))
                    act.activation(og[p][:, BLK:SEQ], X[p][0:GF, BLK:SEQ], ACT.Copy)\
                        .then_inc(act_b.sem, act_b.step("og"))
                if n is not None:
                    act.wait_ge(dve_f.sem, dve_f.now(n, "kmn"))
                    act.activation(km[o][:, :, :], km[o][:, :, :], ACT.Exp).then_inc(act_f.sem, act_f.step("kex"))
                    act.wait_ge(dve_f.sem, dve_f.now(n, "qsh"))
                    act.activation(qe[o][:, :, :, :], qe[o][:, :, :, :], ACT.Exp)\
                        .then_inc(act_f.sem, act_f.step("qex"))
                    act.wait_ge(dve_f.sem, dve_f.now(n, "smn"))
                    for h in range(NLOC):
                        act.activation(P0[o][:, h, :], S0[o][:, h * 128:(h + 1) * 128], ACT.Exp, scale=SCALE,
                                       bias=mx[o][:, 0, h:h + 1])
                    for h in range(NLOC):
                        a = act.activation(P1[o][:, h, :], S1[o][:, h // 2, (h % 2) * 256:(h % 2 + 1) * 256], ACT.Exp,
                                           scale=SCALE, bias=mx[o][:, 1, h:h + 1])
                    a.then_inc(act_f.sem, act_f.step("sexp"))
                if s is not None:
                    act.wait_ge(pe_b.sem, pe_b.now(s, "olT"))
                    act.activation(olT[p][0:LF, :], S0[p][0:LF, 0:SEQ], ACT.Copy)\
                        .then_inc(act_b.sem, act_b.step("olT"))
                if n is not None:
                    act.wait_ge(pe_f.sem, pe_f.now(n, "qT"))
                    act.activation(qT[o][:, :], X[o][0:GF, 0:SEQ], ACT.Copy).then_inc(act_f.sem, act_f.step("qT"))

            sequences(act, body)

        @block.gpsimd
        def _(pool):
            n = 0
            for p in range(2):
                for t, v in ((va[p][:, :, :], 1.0), (og[p][:, 0:BLK], 0.0), (olT[p][LF:LF + 1, :], 1.0)):
                    pool.memset(t, v).then_inc(made, 1)
                    n += 1
                    pool.wait_ge(made, n)
            pool.sem_inc(pool_f.sem, 2 * pool_f.per)
            with pool.Fori(0, NSEQ // 2) as i:
                for p in range(2):
                    pool.wait_ge(pe_l.sem, pe_l.two_before(i * 2 + p, "local"))
                    pool.tensor_copy(hs[p][:, :], h_f[:, bass.ds((i * 2 + p) * SEQ, SEQ)])\
                        .then_inc(pool_f.sem, pool_f.step("hs"))

        @block.vector
        def _(dve):
            for S in (dve_f, dve_b):
                dve.sem_inc(S.sem, 2 * S.per)
            dve.wait_ge(loaded, 16)
            dve.wait_ge(made, MADE)
            dve.tensor_copy(idb[:, :], ident).then_inc(fixed, 1)
            dve.tensor_copy(mask0[:, :, :],
                            caus.rearrange("p (a b) -> p a b", a=1).to_broadcast([128, NLOC, 128]))\
                .then_inc(fixed, 1)
            dve.memset(mask1[:, :, 0:128], 0.0)
            dve.tensor_copy(mask1[:, :, 128:256],
                            caus.rearrange("p (a b) -> p a b", a=1).to_broadcast([128, 2, 128])).then_inc(fixed, 1)

            def heads(t):
                return t.rearrange("p t (h x) -> p t h x", x=DH)

            def wide(t):
                return t.rearrange("p t (h x) -> p t h x", x=1).to_broadcast([128, 2, 12, DH])

            def body(s, p, n, m):
                o = 1 - p

                def front(name, ins):
                    ins.then_inc(dve_f.sem, dve_f.step(name))

                def after(name):
                    dve.wait_ge(dve_f.sem, dve_f.now(n, name))

                def back(name, ins):
                    ins.then_inc(dve_b.sem, dve_b.step(name))

                if n is not None:
                    gq, gk_ = tk[o][:, :, 0:GF], tk[o][:, :, GF:2 * GF]
                    dve.wait_ge(act_f.sem, act_f.now(n, "tk"))
                    front("kmn", dve.tensor_scalar(km[o][:, :, :], gk_, 0.0, None, ALU.min))
                    front("qmx", dve.tensor_reduce(qm[o][:, :, :], heads(gq), AX.X, ALU.max))
                    after("qmx")
                    front("qsh", dve.tensor_tensor(qe[o][:, :, :, :], heads(gq), wide(qm[o][:, :, :]), ALU.subtract))
                    dve.wait_ge(act_f.sem, act_f.now(n, "u"))
                    k_, q_ = S0[o][:, 0:SEQ], S0[o][:, SEQ:2 * SEQ]
                    for g in (slice(32, 64), slice(64, 96)):
                        v = dve.tensor_tensor(k4[o][g, :], k_[g, :], k4[o][g, :].bitcast(F32), ALU.subtract)
                    front("kl", v)
                    front("ql", dve.tensor_tensor(q4[o][64:128, :], q_[64:128, :], q4[o][64:128, :].bitcast(F32),
                                                  ALU.subtract))
                    after("kl")
                    front("kd", dve.tensor_tensor(
                        kd[o][:, :, :],
                        k4[o][:, :].bitcast(F32).rearrange("p (a t) -> p a t", a=1).to_broadcast([128, NLOC, SEQ]),
                        wa[:, A_ROWS:A_ROWS + NLOC].rearrange("p (a t) -> p a t", t=1)
                        .to_broadcast([128, NLOC, SEQ]), ALU.mult))
                if s is not None:
                    dve.wait_ge(pe_b.sem, pe_b.now(s, "PT"))
                    back("pt", dve.tensor_copy(pt[p][:, 2, :, :].rearrange("p h q -> p (h q)"), S1[p][:, 1, :]))
                if n is not None:
                    dve.wait_ge(act_f.sem, act_f.now(n, "kex"))
                    front("kk", dve.scalar_tensor_tensor(kk[o][:, :, :], gk_, 0.0, km[o][:, :, :], ALU.max, ALU.add))
                    dve.wait_ge(pe_f.sem, pe_f.now(n, "S0"))
                    dve.tensor_reduce(mx[o][:, 0, :], S0[o][:, :].rearrange("p (h k) -> p h k", h=NLOC), AX.X, ALU.max)
                    dve.wait_ge(pe_f.sem, pe_f.now(n, "S"))
                    front("smx", dve.tensor_reduce(
                        mx[o][:, 1, :], S1[o][:, :, :].rearrange("p b (h k) -> p (b h) k", h=2), AX.X, ALU.max))
                    after("smx")
                    front("smn", dve.tensor_scalar(mx[o][:, :, :], mx[o][:, :, :], -SCALE, None, ALU.mult))
                    dve.wait_ge(act_f.sem, act_f.now(n, "qex"))
                    front("qsm", dve.tensor_reduce(qm[o][:, :, :], qe[o][:, :, :, :], AX.X, ALU.add))
                    after("qsm")
                    front("qrc", dve.reciprocal(qm[o][:, :, :], qm[o][:, :, :]))
                if s is not None:
                    dve.wait_ge(pe_b.sem, pe_b.now(s, "pv"))
                    y = S0[p][:, 0:2 * NLOC * HV].rearrange("p (t h x) -> p t h x", t=2, x=HV)
                    back("rrc", dve.reciprocal(rs[p][:, :, :, :], y[:, :, :, DH:HV]))
                    dve.wait_ge(dve_b.sem, dve_b.now(s, "rrc"))
                    back("ol", dve.tensor_tensor(ol[p][:, :, :, :], y[:, :, :, 0:DH],
                                                 rs[p][:, :, :, :].to_broadcast([128, 2, NLOC, DH]), ALU.mult))
                if n is not None:
                    after("qrc")
                    front("qn", dve.tensor_tensor(qe[o][:, :, :, :], qe[o][:, :, :, :], wide(qm[o][:, :, :]),
                                                  ALU.mult))
                    dve.wait_ge(pe_f.sem, pe_f.now(n, "ctx"))
                    c = X[o][0:GF, 0:3 * CW].rearrange("p (b e) -> p b e", e=CW)
                    front("kr", dve.tensor_scalar(kr[o][:, :, :], c[:, :, GF:CW], 1e-6, None, ALU.add))
                    after("kr")
                    front("krc", dve.reciprocal(kr[o][:, :, :], kr[o][:, :, :]))
                    after("krc")
                    for b in range(3):
                        v = dve.scalar_tensor_tensor(cn[o][:, b, :], X[o][0:GF, b * CW:b * CW + GF],
                                                     kr[o][:, b, :], same, ALU.mult, ALU.mult)
                    front("cn", v)
                if s is not None:
                    dve.wait_ge(pe_b.sem, pe_b.now(s, "wo"))
                    xq = x_f[:, bass.ds(s * SEQ, SEQ)]
                    back("x", dve.scalar_tensor_tensor(xq, X[p][:, SEQ:2 * SEQ], mod[:, 1, GA, bass.ds(s, 1)], xq,
                                                       ALU.mult, ALU.add))

            sequences(dve, body)


def pack(i):
    f = {k: np.asarray(v) for k, v in i.items()}
    xT = np.ascontiguousarray(f["L0_attn_inputs"].reshape(TOK, D).T)
    eye = np.eye(128, dtype=np.float32)
    sel = np.zeros((128, 32), np.float32)
    sel[64:96], sel[96:128] = np.eye(32), np.eye(32)
    consts = np.concatenate([eye, np.full((128, 128), 1 / 128, np.float32), sel], axis=1)

    def pad(v):
        return np.concatenate([v, np.zeros(128 - len(v), np.float32)]) if len(v) < 128 else v

    a = "L0_attn_"
    cols = [f[a + n] for n in ("gamma", "beta", "b_proj", "b_fc", "b_bc", "b_dt1", "b_dt2", "D1", "D2")]
    cols += [pad(f[a + "b_x1"]), pad(f[a + "b_x2"])]
    vec = np.concatenate([np.stack(cols, 1), f[a + "A_log1"], f[a + "A_log2"], f["L0_c"].T, f["L1_c"].T], axis=1)
    wpk = np.concatenate([f[a + n] for n in ("W_proj", "W_fc", "W_bc", "W_x1", "W_x2")], axis=1)
    wdt = np.concatenate([f[a + "W_dt1"], f[a + "W_dt2"]], axis=1)
    wmod = np.stack([f["L0_wmod"], f["L1_wmod"]], 1)
    m0 = {"wg": f["L0_ffn_Wg"].T, "gb": np.zeros((128, NE), np.float32), "b1": f["L0_ffn_b1"], "w1": f["L0_ffn_W1"],
          "w2": f["L0_ffn_W2"], "b2": f["L0_ffn_b2"]}
    m1 = {"wg": f["L1_ffn_gate_w"], "gb": np.tile(f["L1_ffn_gate_b"], (128, 1)), "b1": f["L1_ffn_b1"],
          "w1": f["L1_ffn_w1"], "w2": f["L1_ffn_w2"], "b2": f["L1_ffn_b2"]}
    fcols = []
    for m in (m0, m1):
        fcols += [m["wg"], m["gb"]]
    fcols += [f["L0_ffn_gamma"][:, None], f["L0_ffn_beta"][:, None]]
    p = np.arange(128)[:, None]
    rconst = np.concatenate([p < p.T, np.ones((128, 128)), np.tile(np.arange(NJT), (128, 1)),
                             np.tile(np.arange(NE) * CAPT * 128, (128, 1)), p + 128 * np.arange(GT)[None], p,
                             np.full((128, 1), AWAY), np.tile(np.arange(NE, 0, -1), (128, 1))], axis=1)
    packed = {"xT": xT, "consts": consts, "vec": vec, "wpk": wpk, "wdt": wdt, "wmod": wmod,
              "rconst": rconst.astype(np.float32), "fvec": np.concatenate(fcols, axis=1)}
    for l, m in enumerate((m0, m1)):
        packed[f"wexp{l}"] = np.concatenate(
            [m["w1"].transpose(1, 0, 2), m["b1"].reshape(NE, NF, 128).transpose(2, 0, 1),
             m["w2"].reshape(NE, NF, 128, D).transpose(2, 0, 1, 3).reshape(128, NE, NF * D),
             np.broadcast_to(m["b2"][None], (128, NE, D))], axis=2).reshape(128, NE * EW)
    wq, wk, wv, wo = (f["L1_attn_" + n] for n in ("Wq", "Wk", "Wv", "Wo"))
    wat = np.zeros((128, A_END), np.float32)
    wat[:, A_QK:A_QK + 2 * D] = np.concatenate([np.tile(wq[:, :LF], 4), np.tile(wk[:, :LF], 4)], axis=1)
    wat[:, A_ROWS:A_ROWS + NLOC] = np.tile(np.kron(np.eye(NLOC), np.ones((DH, 1))), (4, 1))
    wat[:, A_TOK:A_TOK + PW] = np.concatenate([wq[:, LF:], wk[:, LF:], wv], axis=1)
    wat[0:GF, A_WOG:A_WOG + D] = wo[LF:]
    wat[0:LF, A_WOL:A_WOL + D] = wo[:LF]
    wat[LF, A_WOL:A_WOL + D] = f["L1_attn_bo"]
    wat[:, A_CAUS:A_CAUS + 128] = np.where(np.tril(np.ones((128, 128), bool)), 0, -3e38)
    wat[0:GF, A_HEAD:A_HEAD + GF] = np.kron(np.eye(12), np.ones((DH, DH)))
    packed["wat"] = wat
    return {k: np.ascontiguousarray(v, dtype=np.float32) for k, v in packed.items()}


_OUT = (D, TOK)


def kernel(**inputs):
    import concourse.bacc as bacc
    from concourse.bass_utils import run_bass_kernel_spmd

    nc = bacc.Bacc("TRN2", target_bir_lowering=False, num_devices=1)
    packed = pack(inputs)
    args = [nc.dram_tensor(k, v.shape, mybir.dt.from_np(v.dtype), kind="ExternalInput").ap()
            for k, v in packed.items()]
    out = nc.dram_tensor("out_0_dram", _OUT, F32, kind="ExternalOutput").ap()
    build(nc, *args, out)
    r = run_bass_kernel_spmd(nc, [packed], core_ids=[0])
    return np.ascontiguousarray(r.results[0]["out_0_dram"].T).reshape(NSEQ, SEQ, D)
```
